# Optimizing a Trainium2 kernel written in Bass

```python
import numpy as np
import jax
import jax.numpy as jnp

def _softmax(x, axis=-1):
    return jax.nn.softmax(x, axis=axis)

def _gelu(x):
    return jax.nn.gelu(x, approximate=True)

def _silu(x):
    return jax.nn.silu(x)

def _sigmoid(x):
    return jax.nn.sigmoid(x)

def _layernorm(x, axis=-1, eps=1e-05):
    m = jnp.mean(x, axis=axis, keepdims=True)
    v = jnp.var(x, axis=axis, keepdims=True)
    return (x - m) / jnp.sqrt(v + eps)

def _scatter_add(tgt, idx, src, axis=0):
    return tgt.at[idx].add(src)

def _segment_sum(src, seg, n):
    return jax.ops.segment_sum(src, seg, n)
kernel_name = 'mk_decoder_preln_d2_seqx_r8_d3990c'

def setup_inputs(seed: int=0):
    np.random.seed(seed)
    _w = jnp.asarray

    def _rec_inputs():
        import jax
        import jax.numpy as jnp
        _rk = jax.random.key(seed)
        x = 7.22e-05 + 1 * jax.random.normal(jax.random.fold_in(_rk, 1), (8, 256, 128), jnp.float32)
        _lenS = 256 - jax.random.randint(jax.random.fold_in(_rk, 7), (8,), 0, max(1, 256 // 4) + 1, jnp.int32)
        _lenS2 = 512 - jax.random.randint(jax.random.fold_in(_rk, 8), (8,), 0, max(1, 512 // 4) + 1, jnp.int32)
        _ctx_1024P = jax.random.normal(jax.random.fold_in(_rk, 11), (8, 16, 128), jnp.float32)
        _ctx_1024c = jax.random.dirichlet(jax.random.fold_in(_rk, 511), 0.3 * jnp.ones((16,), jnp.float32), (8, 512))
        _ctx_1024t = jnp.einsum('bsk,bkd->bsd', _ctx_1024c, _ctx_1024P)
        _ctx_1024t = _ctx_1024t * jax.lax.rsqrt(jnp.mean(jnp.square(_ctx_1024t)) + 1e-12) * 0.953939
        ctx_1024 = 4.13588e-05 + 0.999923 * (_ctx_1024t + 0.3 * jax.random.normal(jax.random.fold_in(_rk, 611), (8, 512, 128), jnp.float32))
        _validS = jnp.arange(256)[None, :] < _lenS[:, None]
        _validS2 = jnp.arange(512)[None, :] < _lenS2[:, None]
        _causal = jnp.tril(jnp.ones((256, 256), dtype=bool))
        mask_SxS2_bk1 = jnp.broadcast_to(_validS2[0:1, :], (256, 512))
        return (x, ctx_1024, mask_SxS2_bk1)
    x, ctx_1024, mask_SxS2_bk1 = _rec_inputs()

    def _L0_attn_setup():
        import jax, jax.numpy as jnp
        import numpy as np
        EPS = 1e-06
        NUM_HEADS = 16

        def _phi(x):
            return jax.nn.elu(x) + 1.0
        key = jax.random.key(seed)
        ks = jax.random.split(key, 5)
        B, S, D = (2, 256, 128)
        scale = 1.0 / np.sqrt(D)
        return {'x': jax.random.normal(ks[0], (B, S, D), dtype=jnp.float32), 'Wq': jax.random.normal(ks[1], (D, D), dtype=jnp.float32) * scale, 'bq': jnp.zeros((D,), dtype=jnp.float32), 'Wk': jax.random.normal(ks[2], (D, D), dtype=jnp.float32) * scale, 'bk': jnp.zeros((D,), dtype=jnp.float32), 'Wv': jax.random.normal(ks[3], (D, D), dtype=jnp.float32) * scale, 'bv': jnp.zeros((D,), dtype=jnp.float32), 'Wo': jax.random.normal(ks[4], (D, D), dtype=jnp.float32) * scale, 'bo': jnp.zeros((D,), dtype=jnp.float32)}
    _L0_attn_all = _L0_attn_setup()
    _L0_attn_in = {k: v for k, v in _L0_attn_all.items() if k in ('Wq', 'bq', 'Wk', 'bk', 'Wv', 'bv', 'Wo', 'bo')}
    del _L0_attn_all

    def _L0_xattn_setup():
        import math
        import jax, jax.numpy as jnp
        import numpy as np
        EMBED_DIM = 128
        NUM_HEADS = 16
        HEAD_DIM = EMBED_DIM // NUM_HEADS
        B, S = (4, 256)

        def _split_heads(x):
            b, s, _ = x.shape
            return x.reshape(b, s, NUM_HEADS, HEAD_DIM).transpose(0, 2, 1, 3)
        key = jax.random.key(seed)
        ks = jax.random.split(key, 12)
        sc = 1.0 / math.sqrt(EMBED_DIM)
        inp = {'query': jax.random.normal(ks[0], (B, S, EMBED_DIM), jnp.float32), 'key': jax.random.normal(ks[1], (B, S, EMBED_DIM), jnp.float32), 'value': jax.random.normal(ks[2], (B, S, EMBED_DIM), jnp.float32), 'attn_mask': jnp.triu(jnp.ones((S, S), jnp.bool_), k=1), 'q_w': jax.random.normal(ks[3], (EMBED_DIM, EMBED_DIM), jnp.float32) * sc, 'q_b': jax.random.normal(ks[4], (EMBED_DIM,), jnp.float32) * sc, 'k_w': jax.random.normal(ks[5], (EMBED_DIM, EMBED_DIM), jnp.float32) * sc, 'k_b': jax.random.normal(ks[6], (EMBED_DIM,), jnp.float32) * sc, 'v_w': jax.random.normal(ks[7], (EMBED_DIM, EMBED_DIM), jnp.float32) * sc, 'v_b': jax.random.normal(ks[8], (EMBED_DIM,), jnp.float32) * sc, 'o_w': jax.random.normal(ks[9], (EMBED_DIM, EMBED_DIM), jnp.float32) * sc, 'o_b': jax.random.normal(ks[10], (EMBED_DIM,), jnp.float32) * sc}
        return inp
    _L0_xattn_all = _L0_xattn_setup()
    _L0_xattn_in = {k: v for k, v in _L0_xattn_all.items() if k in ('q_w', 'q_b', 'k_w', 'k_b', 'v_w', 'v_b', 'o_w', 'o_b')}
    del _L0_xattn_all

    def _L0_ffn_setup():
        import jax, jax.numpy as jnp
        import numpy as np
        IN_DIM = 128
        OUT_DIM = 128
        NUM_EXPERTS = 8
        TOP_K = 2
        key = jax.random.key(seed)
        ks = jax.random.split(key, 5)
        s = 1.0 / np.sqrt(IN_DIM)
        x = jax.random.normal(ks[0], (4, 256, IN_DIM), dtype=jnp.float32)
        Wg = jax.random.uniform(ks[1], (IN_DIM, NUM_EXPERTS), jnp.float32, -s, s)
        bg = jnp.zeros((NUM_EXPERTS,), jnp.float32)
        We = jax.random.uniform(ks[2], (NUM_EXPERTS, OUT_DIM, IN_DIM), jnp.float32, -s, s)
        be = jax.random.uniform(ks[3], (NUM_EXPERTS, OUT_DIM), jnp.float32, -s, s)
        return {'x': x, 'Wg': Wg, 'bg': bg, 'We': We, 'be': be}
    _L0_ffn_all = _L0_ffn_setup()
    _L0_ffn_in = {k: v for k, v in _L0_ffn_all.items() if k in ('Wg', 'bg', 'We', 'be')}
    del _L0_ffn_all

    def _L1_attn_setup():
        import jax, jax.numpy as jnp
        import numpy as np
        B, S, E, H, W = (4, 256, 128, 16, 128)
        HD = E // H
        key = jax.random.key(seed)
        ks = jax.random.split(key, 5)
        scale = 1.0 / np.sqrt(E)
        x = jax.random.normal(ks[0], (B, S, E), dtype=jnp.float32)
        w_in = jax.random.uniform(ks[1], (3 * E, E), dtype=jnp.float32, minval=-scale, maxval=scale)
        b_in = jnp.zeros((3 * E,), dtype=jnp.float32)
        w_out = jax.random.uniform(ks[2], (E, E), dtype=jnp.float32, minval=-scale, maxval=scale)
        b_out = jnp.zeros((E,), dtype=jnp.float32)
        return {'x': x, 'w_in': w_in, 'b_in': b_in, 'w_out': w_out, 'b_out': b_out}
    _L1_attn_all = _L1_attn_setup()
    _L1_attn_in = {k: v for k, v in _L1_attn_all.items() if k in ('w_in', 'b_in', 'w_out', 'b_out')}
    del _L1_attn_all

    def _L1_xattn_setup():
        import jax, jax.numpy as jnp
        import numpy as np
        import math
        D_MODEL = 128
        NUM_HEADS = 8
        D_HEAD = D_MODEL // NUM_HEADS
        D_FF = 4 * D_MODEL
        LN_EPS = 1e-05

        def _layer_norm(x, g, b):
            mu = jnp.mean(x, axis=-1, keepdims=True)
            var = jnp.mean((x - mu) ** 2, axis=-1, keepdims=True)
            return (x - mu) * jax.lax.rsqrt(var + LN_EPS) * g + b
        key = jax.random.key(seed)
        ks = jax.random.split(key, 16)
        B, Sq, Sk = (2, 256, 256)
        s = 1.0 / math.sqrt(D_MODEL)
        inp = {'query': jax.random.normal(ks[0], (B, Sq, D_MODEL), jnp.float32), 'key': jax.random.normal(ks[1], (B, Sk, D_MODEL), jnp.float32), 'value': jax.random.normal(ks[2], (B, Sk, D_MODEL), jnp.float32), 'Wq': jax.random.normal(ks[3], (D_MODEL, D_MODEL), jnp.float32) * s, 'Wk': jax.random.normal(ks[4], (D_MODEL, D_MODEL), jnp.float32) * s, 'Wv': jax.random.normal(ks[5], (D_MODEL, D_MODEL), jnp.float32) * s, 'Wo': jax.random.normal(ks[6], (D_MODEL, D_MODEL), jnp.float32) * s, 'lambda_param': jnp.asarray(0.8, jnp.float32), 'ln1_g': jnp.ones((D_MODEL,), jnp.float32), 'ln1_b': jnp.zeros((D_MODEL,), jnp.float32), 'ln2_g': jnp.ones((D_MODEL,), jnp.float32), 'ln2_b': jnp.zeros((D_MODEL,), jnp.float32), 'ffn_w1': jax.random.normal(ks[7], (D_MODEL, D_FF), jnp.float32) * s, 'ffn_b1': jnp.zeros((D_FF,), jnp.float32), 'ffn_w2': jax.random.normal(ks[8], (D_FF, D_MODEL), jnp.float32) * (1.0 / math.sqrt(D_FF)), 'ffn_b2': jnp.zeros((D_MODEL,), jnp.float32)}
        return inp
    _L1_xattn_all = _L1_xattn_setup()
    _L1_xattn_in = {k: v for k, v in _L1_xattn_all.items() if k in ('Wq', 'Wk', 'Wv', 'Wo', 'lambda_param', 'ln1_g', 'ln1_b', 'ln2_g', 'ln2_b', 'ffn_w1', 'ffn_b1', 'ffn_w2', 'ffn_b2')}
    del _L1_xattn_all

    def _L1_ffn_setup():
        import jax, jax.numpy as jnp
        import numpy as np
        EPS = 1e-08

        def _ternary_linear(x, w):
            alpha = jnp.mean(jnp.abs(w))
            w_t = jnp.sign(w) * (jnp.abs(w) > 0.5 * alpha).astype(w.dtype)
            w_q = w + jax.lax.stop_gradient(w_t - w)
            d = x.shape[-1]
            rms = jnp.sqrt(jnp.sum(x * x, axis=-1, keepdims=True)) / jnp.sqrt(jnp.asarray(d, x.dtype))
            x_norm = x / (rms + EPS)
            return jnp.einsum('bsd,fd->bsf', x_norm, w_q)
        key = jax.random.key(seed)
        k1, k2, k3 = jax.random.split(key, 3)
        d_model, d_ff = (128, 512)
        B, S = (4, 512)
        x = jax.random.normal(k1, (B, S, d_model), dtype=jnp.float32)
        w_up = jax.random.normal(k2, (d_ff, d_model), dtype=jnp.float32) * 0.02
        w_down = jax.random.normal(k3, (d_model, d_ff), dtype=jnp.float32) * 0.02
        return {'x': x, 'w_up': w_up, 'w_down': w_down}
    _L1_ffn_all = _L1_ffn_setup()
    _L1_ffn_in = {k: v for k, v in _L1_ffn_all.items() if k in ('w_up', 'w_down')}
    del _L1_ffn_all
    return {'x': x, 'ctx_1024': ctx_1024, 'mask_SxS2_bk1': mask_SxS2_bk1, 'L0_attn_Wq': _L0_attn_in['Wq'], 'L0_attn_bq': _L0_attn_in['bq'], 'L0_attn_Wk': _L0_attn_in['Wk'], 'L0_attn_bk': _L0_attn_in['bk'], 'L0_attn_Wv': _L0_attn_in['Wv'], 'L0_attn_bv': _L0_attn_in['bv'], 'L0_attn_Wo': _L0_attn_in['Wo'], 'L0_attn_bo': _L0_attn_in['bo'], 'L0_xattn_q_w': _L0_xattn_in['q_w'], 'L0_xattn_q_b': _L0_xattn_in['q_b'], 'L0_xattn_k_w': _L0_xattn_in['k_w'], 'L0_xattn_k_b': _L0_xattn_in['k_b'], 'L0_xattn_v_w': _L0_xattn_in['v_w'], 'L0_xattn_v_b': _L0_xattn_in['v_b'], 'L0_xattn_o_w': _L0_xattn_in['o_w'], 'L0_xattn_o_b': _L0_xattn_in['o_b'], 'L0_ffn_Wg': _L0_ffn_in['Wg'], 'L0_ffn_bg': _L0_ffn_in['bg'], 'L0_ffn_We': _L0_ffn_in['We'], 'L0_ffn_be': _L0_ffn_in['be'], 'L1_attn_w_in': _L1_attn_in['w_in'], 'L1_attn_b_in': _L1_attn_in['b_in'], 'L1_attn_w_out': _L1_attn_in['w_out'], 'L1_attn_b_out': _L1_attn_in['b_out'], 'L1_xattn_Wq': _L1_xattn_in['Wq'], 'L1_xattn_Wk': _L1_xattn_in['Wk'], 'L1_xattn_Wv': _L1_xattn_in['Wv'], 'L1_xattn_Wo': _L1_xattn_in['Wo'], 'L1_xattn_lambda_param': _L1_xattn_in['lambda_param'], 'L1_xattn_ln1_g': _L1_xattn_in['ln1_g'], 'L1_xattn_ln1_b': _L1_xattn_in['ln1_b'], 'L1_xattn_ln2_g': _L1_xattn_in['ln2_g'], 'L1_xattn_ln2_b': _L1_xattn_in['ln2_b'], 'L1_xattn_ffn_w1': _L1_xattn_in['ffn_w1'], 'L1_xattn_ffn_b1': _L1_xattn_in['ffn_b1'], 'L1_xattn_ffn_w2': _L1_xattn_in['ffn_w2'], 'L1_xattn_ffn_b2': _L1_xattn_in['ffn_b2'], 'L1_ffn_w_up': _L1_ffn_in['w_up'], 'L1_ffn_w_down': _L1_ffn_in['w_down']}

def reference(x, ctx_1024, mask_SxS2_bk1, L0_attn_Wq, L0_attn_bq, L0_attn_Wk, L0_attn_bk, L0_attn_Wv, L0_attn_bv, L0_attn_Wo, L0_attn_bo, L0_xattn_q_w, L0_xattn_q_b, L0_xattn_k_w, L0_xattn_k_b, L0_xattn_v_w, L0_xattn_v_b, L0_xattn_o_w, L0_xattn_o_b, L0_ffn_Wg, L0_ffn_bg, L0_ffn_We, L0_ffn_be, L1_attn_w_in, L1_attn_b_in, L1_attn_w_out, L1_attn_b_out, L1_xattn_Wq, L1_xattn_Wk, L1_xattn_Wv, L1_xattn_Wo, L1_xattn_lambda_param, L1_xattn_ln1_g, L1_xattn_ln1_b, L1_xattn_ln2_g, L1_xattn_ln2_b, L1_xattn_ffn_w1, L1_xattn_ffn_b1, L1_xattn_ffn_w2, L1_xattn_ffn_b2, L1_ffn_w_up, L1_ffn_w_down):
    import jax
    import jax.numpy as jnp

    def _L0_attn_ref(x, Wq, bq, Wk, bk, Wv, bv, Wo, bo):
        import jax, jax.numpy as jnp
        import numpy as np
        EPS = 1e-06
        NUM_HEADS = 16

        def _phi(x):
            return jax.nn.elu(x) + 1.0
        B, S, D = x.shape
        H = NUM_HEADS
        hd = D // H
        q = (x @ Wq.T + bq).reshape(B, S, H, hd).transpose(0, 2, 1, 3)
        k = (x @ Wk.T + bk).reshape(B, S, H, hd).transpose(0, 2, 1, 3)
        v = (x @ Wv.T + bv).reshape(B, S, H, hd).transpose(0, 2, 1, 3)
        q = _phi(q)
        k = _phi(k)
        kv_cum = jnp.cumsum(k[..., :, None] * v[..., None, :], axis=2)
        k_cum = jnp.cumsum(k, axis=2)
        num = jnp.einsum('bhsd,bhsde->bhse', q, kv_cum)
        den = jnp.einsum('bhsd,bhsd->bhs', q, k_cum)
        out = num / (den[..., None] + EPS)
        out = out.transpose(0, 2, 1, 3).reshape(B, S, D)
        return out @ Wo.T + bo

    def _L0_xattn_ref(query, key, value, attn_mask, q_w, q_b, k_w, k_b, v_w, v_b, o_w, o_b):
        import math
        import jax, jax.numpy as jnp
        import numpy as np
        EMBED_DIM = 128
        NUM_HEADS = 16
        HEAD_DIM = EMBED_DIM // NUM_HEADS
        B, S = (4, 256)

        def _split_heads(x):
            b, s, _ = x.shape
            return x.reshape(b, s, NUM_HEADS, HEAD_DIM).transpose(0, 2, 1, 3)
        q = _split_heads(query @ q_w.T + q_b)
        k = _split_heads(key @ k_w.T + k_b)
        v = _split_heads(value @ v_w.T + v_b)
        scale = math.sqrt(HEAD_DIM)
        scores = jnp.einsum('bhqd,bhkd->bhqk', q, k) / scale
        scores = jnp.where(attn_mask[None, None, :, :], -jnp.inf, scores)
        attn = jax.nn.softmax(scores, axis=-1)
        ctx = jnp.einsum('bhqk,bhkd->bhqd', attn, v)
        ctx = ctx.transpose(0, 2, 1, 3).reshape(query.shape[0], query.shape[1], EMBED_DIM)
        return ctx @ o_w.T + o_b

    def _L0_ffn_ref(x, Wg, bg, We, be):
        import jax, jax.numpy as jnp
        import numpy as np
        IN_DIM = 128
        OUT_DIM = 128
        NUM_EXPERTS = 8
        TOP_K = 2
        gate = jax.nn.softmax(x @ Wg + bg, axis=-1)
        topk_vals, topk_idx = jax.lax.top_k(gate, TOP_K)
        onehot = jax.nn.one_hot(topk_idx, NUM_EXPERTS, dtype=gate.dtype)
        gate_sparse = jnp.einsum('bsk,bske->bse', topk_vals, onehot)
        gate_sparse = gate_sparse / jnp.sum(gate_sparse, axis=-1, keepdims=True)
        y = jnp.einsum('bsi,eoi->bseo', x, We) + be[None, None, :, :].transpose(0, 1, 2, 3)
        out = jnp.einsum('bseo,bse->bso', y, gate_sparse)
        return out

    def _L1_attn_ref(x, w_in, b_in, w_out, b_out):
        import jax, jax.numpy as jnp
        import numpy as np
        B, S, E, H, W = (4, 256, 128, 16, 128)
        HD = E // H
        b, s, e = x.shape
        qkv = x @ w_in.T + b_in
        q, k, v = jnp.split(qkv, 3, axis=-1)
        q = q.reshape(b, s, H, HD).transpose(0, 2, 1, 3)
        k = k.reshape(b, s, H, HD).transpose(0, 2, 1, 3)
        v = v.reshape(b, s, H, HD).transpose(0, 2, 1, 3)
        scores = jnp.einsum('bhqd,bhkd->bhqk', q, k) / jnp.sqrt(jnp.asarray(HD, x.dtype))
        i = jnp.arange(s)[:, None]
        j = jnp.arange(s)[None, :]
        allowed = (j <= i) & (j >= i - W)
        scores = jnp.where(allowed[None, None], scores, jnp.asarray(-1000000000.0, x.dtype))
        attn = jax.nn.softmax(scores, axis=-1)
        out = jnp.einsum('bhqk,bhkd->bhqd', attn, v)
        out = out.transpose(0, 2, 1, 3).reshape(b, s, e)
        return out @ w_out.T + b_out

    def _L1_xattn_ref(query, key, value, Wq, Wk, Wv, Wo, lambda_param, ln1_g, ln1_b, ln2_g, ln2_b, ffn_w1, ffn_b1, ffn_w2, ffn_b2):
        import jax, jax.numpy as jnp
        import numpy as np
        import math
        D_MODEL = 128
        NUM_HEADS = 8
        D_HEAD = D_MODEL // NUM_HEADS
        D_FF = 4 * D_MODEL
        LN_EPS = 1e-05

        def _layer_norm(x, g, b):
            mu = jnp.mean(x, axis=-1, keepdims=True)
            var = jnp.mean((x - mu) ** 2, axis=-1, keepdims=True)
            return (x - mu) * jax.lax.rsqrt(var + LN_EPS) * g + b
        B, Sq, _ = query.shape
        Sk = key.shape[1]
        Q = (query @ Wq).reshape(B, Sq, NUM_HEADS, D_HEAD)
        K = (key @ Wk).reshape(B, Sk, NUM_HEADS, D_HEAD)
        V = (value @ Wv).reshape(B, Sk, NUM_HEADS, D_HEAD)
        scale = 1.0 / math.sqrt(D_HEAD)
        scores = jnp.einsum('bqhd,bkhd->bhqk', Q, K) * scale
        attn1 = jax.nn.softmax(scores, axis=-1)
        attn2 = jax.nn.softmax(scores - 1.0, axis=-1)
        lam = jax.nn.sigmoid(lambda_param)
        attn = attn1 - lam * attn2
        attn_out = jnp.einsum('bhqk,bkhd->bqhd', attn, V).reshape(B, Sq, D_MODEL)
        attn_out = attn_out @ Wo
        q_enh = _layer_norm(query + attn_out, ln1_g, ln1_b)
        ffn = jax.nn.relu(q_enh @ ffn_w1 + ffn_b1) @ ffn_w2 + ffn_b2
        return _layer_norm(q_enh + ffn, ln2_g, ln2_b)

    def _L1_ffn_ref(x, w_up, w_down):
        import jax, jax.numpy as jnp
        import numpy as np
        EPS = 1e-08

        def _ternary_linear(x, w):
            alpha = jnp.mean(jnp.abs(w))
            w_t = jnp.sign(w) * (jnp.abs(w) > 0.5 * alpha).astype(w.dtype)
            w_q = w + jax.lax.stop_gradient(w_t - w)
            d = x.shape[-1]
            rms = jnp.sqrt(jnp.sum(x * x, axis=-1, keepdims=True)) / jnp.sqrt(jnp.asarray(d, x.dtype))
            x_norm = x / (rms + EPS)
            return jnp.einsum('bsd,fd->bsf', x_norm, w_q)
        h = jax.nn.gelu(_ternary_linear(x, w_up), approximate=False)
        return _ternary_linear(h, w_down)
    x = x + _L0_attn_ref(_layernorm(x, axis=-1), L0_attn_Wq, L0_attn_bq, L0_attn_Wk, L0_attn_bk, L0_attn_Wv, L0_attn_bv, L0_attn_Wo, L0_attn_bo)
    x = x + _L0_xattn_ref(_layernorm(x, axis=-1), ctx_1024, ctx_1024, mask_SxS2_bk1, L0_xattn_q_w, L0_xattn_q_b, L0_xattn_k_w, L0_xattn_k_b, L0_xattn_v_w, L0_xattn_v_b, L0_xattn_o_w, L0_xattn_o_b)
    x = x + _L0_ffn_ref(_layernorm(x, axis=-1), L0_ffn_Wg, L0_ffn_bg, L0_ffn_We, L0_ffn_be)
    x = x + _L1_attn_ref(_layernorm(x, axis=-1), L1_attn_w_in, L1_attn_b_in, L1_attn_w_out, L1_attn_b_out)
    x = x + _L1_xattn_ref(_layernorm(x, axis=-1), ctx_1024, ctx_1024, L1_xattn_Wq, L1_xattn_Wk, L1_xattn_Wv, L1_xattn_Wo, L1_xattn_lambda_param, L1_xattn_ln1_g, L1_xattn_ln1_b, L1_xattn_ln2_g, L1_xattn_ln2_b, L1_xattn_ffn_w1, L1_xattn_ffn_b1, L1_xattn_ffn_w2, L1_xattn_ffn_b2)
    x = x + _L1_ffn_ref(_layernorm(x, axis=-1), L1_ffn_w_up, L1_ffn_w_down)
    return x

_drawn_inputs = setup_inputs


def setup_inputs(seed=0):
    import zlib

    import numpy as np

    out = dict(_drawn_inputs(seed))
    spreads = {'L0_attn_bq': (0.0, 0.8),
     'L0_attn_bk': (0.0, 0.8),
     'L0_attn_bv': (0.0, 0.1),
     'L0_attn_bo': (0.0, 0.1),
     'L0_ffn_bg': (0.0, 0.1),
     'L1_attn_b_in': (0.0, 0.1),
     'L1_attn_b_out': (0.0, 0.1),
     'L1_xattn_ln1_g': (1.0, 0.2),
     'L1_xattn_ln1_b': (0.0, 0.1),
     'L1_xattn_ln2_g': (1.0, 0.2),
     'L1_xattn_ln2_b': (0.0, 0.1),
     'L1_xattn_ffn_b1': (0.0, 0.335),
     'L1_xattn_ffn_b2': (0.0, 0.1)}
    factors = {'L0_xattn_k_b': 8.0}
    for name, (base, spread) in spreads.items():
        noise = np.random.default_rng([zlib.crc32(name.encode()), seed]).standard_normal(out[name].shape)
        drawn = base * np.exp(spread * noise) if base else spread * noise
        out[name] = jnp.asarray(drawn.astype(out[name].dtype))
    for name, factor in factors.items():
        out[name] = (out[name] * factor).astype(out[name].dtype)
    return out
```

```python
from contextlib import ExitStack

import numpy as np

import concourse.bass as bass
from concourse import mybir

F32 = mybir.dt.float32
BF16 = mybir.dt.bfloat16
U8 = mybir.dt.uint8
ALU = mybir.AluOpType
ACT = mybir.ActivationFunctionType
AX = mybir.AxisListType

P = 128
B, S, D, SK = 8, 256, 128, 512
TQ, TK = S // P, SK // P
NE, FF = 8, 512
FC = FF // P
PARTS = 3
Q_OF = (0, 1, 2, 0, 1, 0)
K_OF = (0, 0, 0, 1, 1, 2)
NPROD = len(Q_OF)
NEG_MAX = -1.0e30
NEG_EXP = -3.0e38
LN_EPS, DEN_EPS, RMS_EPS = 1e-5, 1e-6, 1e-8
VW = 32

HEADS = (16, 16, 16, 8)
HD = tuple(D // h for h in HEADS)
KEYS = (S, SK, S, SK)
GROUPS = tuple(h // 4 for h in HEADS)
SCALE = (1.0, 8 ** -0.5, 8 ** -0.5, 16 ** -0.5)
MAX_UNITS = (0, 8, 4, 8)
KEEP_AFTER = (0, 4, 2, 4)
EXP_UNITS = (2, 8, 4, 8)
PHASES = range(4)
ORDER = [(p, s) for s in range(2) for p in PHASES]

W_COLS = {}
_at = 0
for _n, _w in (("q0", D), ("k0", D), ("v0", D), ("o0", D), ("q1", D), ("k1", D), ("v1", D), ("o1", D),
               ("gate", NE), ("experts", NE * D), ("q2", D), ("k2", D), ("v2", D), ("o2", D),
               ("q3", D), ("k3", D), ("v3", D), ("o3", D), ("ffn1", FF), ("ffn2", FF),
               ("up", FF), ("down", FF)):
    W_COLS[_n] = (_at, _at + _w)
    _at += _w
W_TOTAL = _at
W_LOADS = (0, W_COLS["q1"][0], W_COLS["q2"][0], W_COLS["up"][0], W_TOTAL)
C_COLS = {n: i for i, n in enumerate(("q0", "k0", "q1", "k1", "q2", "k2", "zero", "ffn1"))}
C_TOTAL = C_COLS["ffn1"] + FC
R_COLS = {}
_at = 0
for _n, _w in (("v0", D), ("o0", D), ("v1", D), ("o1", D), ("v2", D), ("o2", D), ("ln1_g", D),
               ("ln1_b", D), ("ln2_g", D), ("ln2_b", D), ("ffn2", D), ("gate", NE), ("lambda", 1)):
    R_COLS[_n] = (_at, _at + _w)
    _at += _w
R_TOTAL = _at


def unit_starts(units):
    at, found = 0, {}
    for key in ORDER:
        found[key] = at
        at += GROUPS[key[0]] * units[key[0]]
    return found, at


MAX_START, MAX_TOTAL = unit_starts([n + 1 if n else 0 for n in MAX_UNITS])
EXP_START, EXP_TOTAL = unit_starts(EXP_UNITS)
OUT_START, OUT_TOTAL = unit_starts((1, 1, 1, 1))


def core_order(p):
    n1, n2, ng = MAX_UNITS[p], EXP_UNITS[p], GROUPS[p]
    if not n1:
        return [("exp", g, i) for g in range(ng) for i in range(n2)]
    out = [("max", 0, i) for i in range(n1)]
    if ng > 1:
        out += [("max", 1, i) for i in range(3)] + [("turn", 0)] + [("max", 1, i) for i in range(3, n1)]
    for g in range(ng):
        ahead = [("max", g + 2, i) for i in range(n1)] if g + 2 < ng else []
        if g + 1 < ng:
            ahead.insert(0, ("turn", g + 1))
        for i in range(n2):
            out.append(("exp", g, i))
            take = len(ahead) * (i + 1) // n2 - len(ahead) * i // n2
            at = len(ahead) * i // n2
            out += ahead[at:at + take]
    return out


def decoder(nc, x, ctxT, maskq, maskk, weights, columns, rows_in, experts_bias, out):
    with ExitStack() as ctx:
        def sb(name, shape, dt=F32):
            return ctx.enter_context(nc.sbuf_tensor(name, shape, dt))

        def psum(name, shape, dt=F32):
            return ctx.enter_context(nc.psum_tensor(name, shape, dt))

        def sem(name):
            return ctx.enter_context(nc.semaphore(name))

        def pair(name):
            return [sem(f"{name}_{s}") for s in range(2)]

        W = sb("W", [P, W_TOTAL])
        col = sb("col", [P, C_TOTAL])
        rows = sb("rows", [P, R_TOTAL])
        ebias = sb("ebias", [NE, D])
        ident = sb("ident", [P, P])
        identb = sb("identb", [P, P], BF16)
        zero = sb("zero", [P, FF])
        tri = sb("tri", [P, P])
        head_of = sb("head_of", [P, 8, 16])
        own = sb("own", [P, 16])
        first = sb("first", [P, NE, NE])
        maskq8 = sb("maskq8", [P, TQ, SK], U8)
        maskk8 = sb("maskk8", [P, TK, S], U8)
        maskq_add = sb("maskq_add", [P, TQ, SK], BF16)
        maskk_add = sb("maskk_add", [P, TK, S], BF16)
        winq_add = sb("winq_add", [P, 3, P], BF16)
        wink_add = sb("wink_add", [P, 2, P], BF16)
        half = sb("half", [P, 2 * TQ])
        keep = sb("keep", [P, 1])
        absum = sb("absum", [P, 2])
        alpha = sb("alpha", [P, 2])
        wtmp = sb("wtmp", [P, 2, FF])
        ones_col = sb("ones_col", [P, P])
        X = [sb(f"X{s}", [P, TQ, D]) for s in range(2)]
        qn = [sb(f"qn{s}", [P, TQ, D]) for s in range(2)]
        QS = [sb(f"QS{s}", [P, 8, S], BF16) for s in range(2)]
        KS8 = [sb(f"KS8{s}", [P, 8, SK], BF16) for s in range(2)]
        KS16 = [sb(f"KS16{s}", [P, 8, SK], BF16) for s in range(2)]
        V8 = [sb(f"V8{s}", [P, TK, 16, VW]) for s in range(2)]
        V16 = [sb(f"V16{s}", [P, TK, 8, VW]) for s in range(2)]
        OT = [sb(f"OT{s}", [P, 4, S]) for s in range(2)]
        KV = [sb(f"KV{s}", [P, 16, VW]) for s in range(2)]
        xs = [sb(f"xs{s}", [P, S + SK]) for s in range(2)]
        cT = [sb(f"cT{s}", [P, SK]) for s in range(2)]
        mx = [sb(f"mx{s}", [P, TQ, 16]) for s in range(2)]
        nmr = [sb(f"nmr{s}", [P, TQ, 16]) for s in range(2)]
        nm = [sb(f"nm{s}", [P, TQ, 16, PARTS], BF16) for s in range(2)]
        mrow = [sb(f"mrow{s}", [12, 4, S], BF16) for s in range(2)]
        stats = sb("stats", [P, TQ, 6])
        mv = sb("mv", [P, TQ, 2])
        var = sb("var", [P, TQ])
        rstd = sb("rstd", [P, TQ])
        hn = sb("hn", [P, TQ, D])
        hT = sb("hT", [P, S])
        es = sb("es", [P, 2 * S])
        rs = sb("rs", [P, 2 * S])
        parts = sb("parts", [P, PARTS, S + SK], BF16)
        rest = sb("rest", [P, S + SK])
        kTM = sb("kTM", [P, P])
        rden = sb("rden", [P, TQ * 16])
        An = sb("An", [P, TQ, D])
        AT = sb("AT", [P, S])
        gl = sb("gl", [P, TQ, NE])
        gm = sb("gm", [P, TQ])
        gp = sb("gp", [P, TQ, NE])
        gsum = sb("gsum", [P, TQ])
        grec = sb("grec", [P, TQ])
        cmp_gt = sb("cmp_gt", [P, TQ * NE, NE])
        cmp_eq = sb("cmp_eq", [P, TQ * NE, NE])
        rank = sb("rank", [P, TQ, NE])
        gate = sb("gate", [P, TQ, NE])
        gateT = sb("gateT", [NE, S])
        acc = sb("acc", [P, TQ, D])
        f1 = sb("f1", [P, FC, S])
        sq = sb("sq", [P, FC, S])
        ssum = sb("ssum", [P, TQ])
        rms = sb("rms", [P, TQ])
        irms = sb("irms", [P, TQ])
        junk = sb("junk", [P, 2, SK], BF16)
        junk32 = sb("junk32", [P, TQ, P])
        probs = sb("probs", [P, 4, FF])
        bounce = [nc.dram_tensor(f"bounce{s}", (PARTS, P, S + SK), BF16, kind="Internal").ap() for s in range(2)]

        mb = psum("mb", [P, 2, 512])
        eb = psum("eb", [P, 2, 512])
        ob = psum("ob", [P, 2, 512])
        side = psum("side", [P, 2, 512])

        w_in = [sem(f"w_in{i}") for i in range(len(W_LOADS) - 1)]
        const_in = sem("const_in")
        pool_const, dve_const, pe_const, act_const = sem("pool_const"), sem("dve_const"), sem("pe_const"), sem("act_const")
        dve_step, act_step, pool_step, pe_step = sem("dve_step"), sem("act_step"), sem("pool_step"), sem("pe_step")
        x_in, ctx_in, x_out = pair("x_in"), pair("ctx_in"), pair("x_out")
        ln_stats, ln_rstd, ln_rows, ln_turned, hT_ready = (pair(n) for n in ("ln_stats", "ln_rstd", "ln_rows", "ln_turned", "hT_ready"))
        proj_done, exp_in, xs_act, xs_ready, v_ready, split_done = (pair(n) for n in ("proj_done", "exp_in", "xs_act", "xs_ready", "v_ready", "split_done"))
        bounce_in, stack_in, mrow_in = pair("bounce_in"), pair("stack_in"), pair("mrow_in")
        k_turned, kTM_ready, kv_done, kv_ready = (pair(n) for n in ("k_turned", "kTM_ready", "kv_done", "kv_ready"))
        nm_ready, qk_raw = pair("nm_ready"), pair("qk_raw")
        max_scores, max_used = sem("max_scores"), sem("max_used")
        exp_scores, probs_ready, av_done = sem("exp_scores"), sem("probs_ready"), sem("av_done")
        out_kept = sem("out_kept")
        o_turned, an_ready, an_turned, at_ready, o_proj = (pair(n) for n in ("o_turned", "an_ready", "an_turned", "at_ready", "o_proj"))
        x_updated = pair("x_updated")
        gate_done, gate_ready, gateT_done, gateT_ready, experts_done, experts_used, moe_bias = (
            pair(n) for n in ("gate_done", "gate_ready", "gateT_done", "gateT_ready", "experts_done", "experts_used", "moe_bias"))
        gexp_in, gexp_out = pair("gexp_in"), pair("gexp_out")
        ffn_h, ffn_act, ffn_y = pair("ffn_h"), pair("ffn_act"), pair("ffn_y")
        rms_sum, rms_root = pair("rms_sum"), pair("rms_root")
        sq_ready, sq_sum = pair("sq_ready"), pair("sq_sum")

        def w(name, lo=0, n=None):
            a, b = W_COLS[name]
            return W[:, a + lo:(a + lo + n) if n else b]

        def row(name):
            return rows[:, R_COLS[name][0]:R_COLS[name][1]]

        def c(name, i=0):
            return col[:, C_COLS[name] + i:C_COLS[name] + i + 1]

        def stack_rows(p, h, extra=0):
            if p == 3:
                return slice(0, NPROD * 16 + extra), h
            half = h % 4 // 2
            return slice(64 * half, 64 * half + NPROD * 8 + extra), h // 4 * 2 + h % 2

        KS = (KS8, KS8, KS8, KS16)
        V = (V8, V8, V8, V16)
        PAIRS = B // 2
        counts = dict(chain_counts)

        def wait_alone(eng):
            eng.nop(nofuse=True)

        class Chain:

            def __init__(self, name, eng, sem_):
                self.name, self.eng, self.sem = name, eng, sem_
                self.n, self.before, self.it = 0, 0, None

            def enter(self, it):
                self.before, self.n, self.it = self.n, 0, it
                self.total = counts.get(self.name, 1)

            def leave(self):
                chain_counts[self.name] = self.n

            def done(self, ins):
                self.n += 1
                ins.then_inc(self.sem, 1)

            def wait(self):
                if self.it is None:
                    self.eng.wait_ge(self.sem, self.n)
                else:
                    self.eng.wait_ge(self.sem, self.it * self.total + (self.before + self.n))

            def link(self, ins, plain=False):
                self.done(ins)
                self.wait()
                if plain:
                    wait_alone(self.eng)

        block = ctx.enter_context(nc.Block())

        NORMS = 8
        TURNED = 6
        TURN_OF = {0: 0, 1: 1, 2: 2, 3: 3, 4: 4, 5: 5, 7: 6}
        NT = len(TURN_OF)

        @block.sync
        def _(sp):
            sp.dma_start(col[:], columns).then_inc(const_in, 16)
            sp.dma_start(rows[:], rows_in.to_broadcast([P, R_TOTAL])).then_inc(const_in, 16)
            sp.dma_start(W[:, W_LOADS[0]:W_LOADS[1]], weights[:, W_LOADS[0]:W_LOADS[1]]).then_inc(w_in[0], 16)
            sp.dma_start(maskq8[:], maskq.rearrange("(t p) k -> p t k", p=P)).then_inc(const_in, 16)
            sp.dma_start(maskk8[:], maskk.rearrange("(t p) q -> p t q", p=P)).then_inc(const_in, 16)
            sp.dma_start(ebias[:], experts_bias).then_inc(const_in, 16)
            for i in range(1, len(W_LOADS) - 1):
                sp.dma_start(W[:, W_LOADS[i]:W_LOADS[i + 1]], weights[:, W_LOADS[i]:W_LOADS[i + 1]]).then_inc(w_in[i], 16)
            with sp.Fori(0, PAIRS) as it:
                def load(s):
                    sp.wait_ge(x_out[s], it * 16 + 16)
                    sp.dma_start(X[s][:], x[bass.ds(it * 2 + s, 1)].rearrange("o (t p) d -> p (o t) d", p=P)).then_inc(x_in[s], 16)
                    sp.dma_start(cT[s][:], ctxT[bass.ds(it * 2 + s, 1)].rearrange("o p t -> p (o t)")).then_inc(ctx_in[s], 16)

                def stack(s, p):
                    width = S + KEYS[p]
                    hd, heads = HD[p], HEADS[p]
                    sp.wait_ge(split_done[s], it * 4 + p + 1)
                    sp.dma_start(bounce[s].rearrange("c p t -> p c t")[:, :, 0:width], parts[:, :, 0:width]).then_inc(bounce_in[s], 16)
                    sp.wait_ge(bounce_in[s], it * 64 + 16 * (p + 1))
                    for par in range(1 if p == 3 else 2):
                        def src(part, n, lo, T):
                            b = bounce[s][part:part + n]
                            b = b.rearrange("c (d h) t -> (c d) h t", h=heads)
                            if p == 3:
                                return b[:, :, lo:lo + T]
                            return b[:, par::2, lo:lo + T]
                        r = 64 * par
                        at = 0
                        for n in (3, 2, 1):
                            sp.dma_start(QS[s][r + at * hd:r + (at + n) * hd], src(0, n, 0, S)).then_inc(stack_in[s], 16)
                            at += n
                        for i, part in enumerate(K_OF):
                            sp.dma_start(KS[p][s][r + i * hd:r + (i + 1) * hd, :, 0:KEYS[p]], src(part, 1, S, KEYS[p])).then_inc(stack_in[s], 16)

                def maxima(s, p):
                    banks = [b for b in core_order(p) if b[0] != "exp"]
                    for n, (kind, g, *_) in enumerate(banks):
                        if kind != "turn":
                            continue
                        sp.wait_ge(max_used, it * MAX_TOTAL + MAX_START[p, s] + n + 3)
                        for j in range(4):
                            h = 4 * g + j
                            r, slot = stack_rows(p, h)
                            sp.dma_start(QS[s][r.stop:r.stop + PARTS, slot, :], mrow[s][3 * j:3 * j + 3, g, :]).then_inc(mrow_in[s], 16)

                for s in range(2):
                    load(s)
                    for p in PHASES:
                        stack(s, p)
                        if MAX_UNITS[p]:
                            maxima(s, p)
                    sp.wait_ge(x_updated[s], it * 5 + 5)
                    sp.dma_start(out[bass.ds(it * 2 + s, 1)].rearrange("o (t p) d -> p (o t) d", p=P), X[s][:]).then_inc(x_out[s], 16)
            for s in range(2):
                sp.wait_ge(x_out[s], PAIRS * 16 + 16)

        @block.gpsimd
        def _(pool):
            chain = Chain("pool", pool, pool_step)

            def select(out_, op, fill, pattern, mult):
                chain.link(nc.gpsimd.affine_select(out=out_, in_=out_, compare_op=op, fill=fill, base=0,
                                                   pattern=pattern, channel_multiplier=mult))

            for t, v in ((ident, 0.0), (identb, 0.0), (tri, 1.0), (head_of, 0.0), (first, 1.0),
                         (winq_add, 0.0), (wink_add, 0.0), (zero, 0.0), (ones_col, 1.0)):
                chain.done(nc.gpsimd.memset(t[:], v))
            chain.done(nc.gpsimd.memset(half[:, 0:TQ], -0.5))
            chain.link(nc.gpsimd.memset(half[:, TQ:2 * TQ], 0.5))
            select(ident[:], ALU.not_equal, 1.0, [[-1, P]], 1)
            select(identb[:], ALU.not_equal, 1.0, [[-1, P]], 1)
            select(tri[:], ALU.is_ge, 0.0, [[1, P]], -1)
            select(head_of[:].rearrange("p a (g r j) -> p a g r j", g=4, r=2), ALU.not_equal, 1.0,
                   [[-16, 8], [-4, 4], [-1, 2], [-2, 2]], 1)
            select(first[:], ALU.is_gt, 0.0, [[1, NE], [-1, NE]], 0)
            for i, sign in ((0, -1), (1, 1), (2, -1)):
                select(winq_add[:, i, :], ALU.is_ge, NEG_MAX, [[sign, P]], -sign)
            for i, sign in ((0, 1), (1, -1)):
                select(wink_add[:, i, :], ALU.is_ge, NEG_MAX, [[sign, P]], -sign)
            chain.link(nc.gpsimd.memset(KS8[0][:], 1.0))
            for t, v in ((KS8[1], 1.0), (KS16[0], 1.0), (KS16[1], 1.0), (V8[0], 0.0), (V8[1], 0.0), (V16[0], 0.0), (V16[1], 0.0)):
                chain.link(nc.gpsimd.memset(t[:], v))
            for s in range(2):
                nc.gpsimd.memset(V8[s][:, :, :, 8:9], 1.0)
                nc.gpsimd.memset(V16[s][:, :, :, 16:17], 1.0).then_inc(pool_const, 1)
            for s in range(2):
                nc.gpsimd.memset(X[s][:], 0.0).then_inc(x_out[s], 16)
            with pool.Fori(0, PAIRS) as it:
                chain.enter(it)
                for s in range(2):
                    roots = 0
                    for k in range(NORMS):
                        pool.wait_ge(ln_stats[s], it * NORMS + k + 1)
                        wait_alone(pool)
                        chain.link(nc.gpsimd.tensor_scalar(var[:], mv[:, :, 1], LN_EPS, None, ALU.add))
                        nc.gpsimd.tensor_tensor(rstd[:], var[:], half[:, 0:TQ], ALU.pow).then_inc(ln_rstd[s], 1)
                    for k in range(2):
                        pool.wait_ge(rms_sum[s], it * 2 + k + 1)
                        wait_alone(pool)
                        chain.link(nc.gpsimd.tensor_scalar(var[:], ssum[:], 1.0 / (D, FF)[k], None, ALU.mult))
                        chain.link(nc.gpsimd.tensor_tensor(rms[:], var[:], half[:, TQ:2 * TQ], ALU.pow), plain=True)
                        nc.gpsimd.tensor_scalar(rms[:], rms[:], RMS_EPS, None, ALU.add).then_inc(rms_root[s], 1)
                chain.leave()

        @block.tensor
        def _(pe):
            pe.wait_ge(pool_const, 2)
            pe.wait_ge(act_const, 2)
            nc.tensor.matmul(side[:, 0, 0:2], ones_col[:], absum[:], start=True, stop=True).then_inc(pe_const, 1)
            for q in w_in:
                pe.wait_ge(q, 16)
            pe.wait_ge(dve_const, 1)
            with pe.Fori(0, PAIRS) as it:
                def turn(s, k, src):
                    pe.wait_ge(ln_rows[s], it * NT + TURN_OF[k] + 1)
                    for t in range(TQ):
                        ins = nc.tensor.transpose(side[:, 0, t * P:(t + 1) * P], src[:, t, :], ident[:])
                    ins.then_inc(ln_turned[s], 1)
                    pe.wait_ge(hT_ready[s], it * NT + TURN_OF[k] + 1)

                def project(s, p):
                    nc.tensor.matmul(side[:, 0, 0:S], w(f"q{p}"), hT[:], start=True, stop=True)
                    src = hT
                    if KEYS[p] == SK:
                        pe.wait_ge(ctx_in[s], it * 16 + 16)
                        src = cT[s]
                        nc.tensor.matmul(side[:, 1, :], w(f"k{p}"), cT[s][:], start=True, stop=True).then_inc(proj_done[s], 1)
                        pe.wait_ge(xs_act[s], it * 4 + p + 1)
                        vb = side[:, 0, :]
                    else:
                        nc.tensor.matmul(side[:, 0, S:2 * S], w(f"k{p}"), hT[:], start=True, stop=True).then_inc(proj_done[s], 1)
                        vb = side[:, 1, :]
                    for t in range(KEYS[p] // P):
                        ins = nc.tensor.matmul(vb[:, t * D:(t + 1) * D], src[:, t * P:(t + 1) * P], w(f"v{p}"), start=True, stop=True)
                    ins.then_inc(proj_done[s], 1)

                def state(s):
                    pe.wait_ge(xs_ready[s], it + 1)
                    nc.tensor.transpose(side[:, 0, 0:P], xs[s][:, S:S + P], ident[:]).then_inc(k_turned[s], 1)
                    pe.wait_ge(kTM_ready[s], it + 1)
                    pe.wait_ge(v_ready[s], it * 4 + 1)
                    nc.tensor.matmul(side[:, 1, :], kTM[:], V8[s][:, 0, :, :].rearrange("p h e -> p (h e)"), start=True, stop=True).then_inc(kv_done[s], 1)

                def core(s, p):
                    ks, v = KS[p][s], V[p][s]
                    n1, n2 = MAX_UNITS[p] + 1, EXP_UNITS[p]
                    mu = MAX_START[p, s]
                    order = core_order(p)
                    pe.wait_ge(stack_in[s], it * STACK_TOTAL + STACK_UPTO[p])
                    pe.wait_ge(v_ready[s], it * 4 + p + 1)
                    if p == 0:
                        pe.wait_ge(kv_ready[s], it + 1)
                    pending = []

                    def free_max_bank(u):
                        pe.wait_ge(max_used, it * MAX_TOTAL + u + 1)

                    def av(g, i):
                        u = EXP_START[p, s] + g * n2 + i
                        og = OUT_START[p, s] + g
                        pe.wait_ge(probs_ready, it * EXP_TOTAL + u + 1)
                        if i == 0:
                            pe.wait_ge(out_kept, it * OUT_TOTAL + og + 1)
                        pr = probs[:, u % 4, :]
                        bank = ob[:, og % 2, :]
                        if p == 0:
                            for t in range(TQ):
                                for j in (2 * i, 2 * i + 1):
                                    at = ((j % 2) * TQ + t) * P
                                    ins = nc.tensor.matmul(bank[32 * j:32 * j + 32, t * P:(t + 1) * P], v[:, t, 4 * g + j, :], pr[:, at:at + P],
                                                           start=True, stop=(t == 0), skip_group_check=True)
                            for j in (2 * i, 2 * i + 1):
                                ins = nc.tensor.matmul(bank[32 * j:32 * j + 32, P:2 * P], KV[s][:, 4 * g + j, :], xs[s][:, P:2 * P],
                                                       start=False, stop=True, skip_group_check=True)
                        elif p == 2:
                            kt = i // 2
                            n = (S, P)[kt]
                            for j in (2 * (i % 2), 2 * (i % 2) + 1):
                                ins = nc.tensor.matmul(bank[32 * j:32 * j + 32, S - n:S], v[:, kt, 4 * g + j, :], pr[:, (j % 2) * n:(j % 2 + 1) * n],
                                                       start=(kt == 0), stop=(kt == 1), skip_group_check=True)
                        else:
                            kt = i // 2
                            for j in (2 * (i % 2), 2 * (i % 2) + 1):
                                ins = nc.tensor.matmul(bank[32 * j:32 * j + 32, 0:S], v[:, kt, 4 * g + j, :], pr[:, (j % 2) * S:(j % 2 + 1) * S],
                                                       start=(kt == 0), stop=(kt == TK - 1))
                        ins.then_inc(av_done, 1)

                    for blk in order:
                        if blk[0] == "max":
                            _, g, i = blk
                            free_max_bank(mu)
                            bank = mb[:, mu % 2, :]
                            if p == 2:
                                r, slot = stack_rows(p, 4 * g + i)
                                nc.tensor.matmul(bank[:, 0:P], QS[s][r, slot, 0:P], ks[r, slot, 0:P], start=True, stop=True)
                                ins = nc.tensor.matmul(bank[:, P:3 * P], QS[s][r, slot, P:2 * P], ks[r, slot, 0:S], start=True, stop=True)
                            else:
                                r, slot = stack_rows(p, 4 * g + i // 2)
                                t = i % 2
                                ins = nc.tensor.matmul(bank, QS[s][r, slot, t * P:(t + 1) * P], ks[r, slot, :], start=True, stop=True)
                            ins.then_inc(max_scores, 1)
                            mu += 1
                        elif blk[0] == "turn":
                            _, g = blk
                            pe.wait_ge(nm_ready[s], it * GRP_TOTAL + GRP_START[p] + g + 1)
                            free_max_bank(mu)
                            dst = mb[:, mu % 2, :].bitcast(BF16)
                            for t in range(TQ):
                                ins = nc.tensor.transpose(dst[0:12, t * P:(t + 1) * P],
                                                          nm[s][:, t, 4 * g:4 * g + 4, :].rearrange("p h c -> p (h c)"), identb[:])
                            ins.then_inc(max_scores, 1)
                            mu += 1
                        else:
                            _, g, i = blk
                            u = EXP_START[p, s] + g * n2 + i
                            if n1 > 1 and i == 0:
                                pe.wait_ge(mrow_in[s], it * GRP_TOTAL * 64 + 64 * (GRP_START[p] + g + 1))
                            if u >= 2:
                                pe.wait_ge(probs_ready, it * EXP_TOTAL + u - 1)
                            bank = eb[:, u % 2, :]
                            if p == 0:
                                for j in (2 * i, 2 * i + 1):
                                    r, slot = stack_rows(p, 4 * g + j)
                                    for t in range(TQ):
                                        at = ((j % 2) * TQ + t) * P
                                        ins = nc.tensor.matmul(bank[:, at:at + P], ks[r, slot, t * P:(t + 1) * P], QS[s][r, slot, t * P:(t + 1) * P],
                                                               start=True, stop=True)
                            elif p == 2:
                                kt = i // 2
                                n = (S, P)[kt]
                                part = bank[:, 0:2 * n]
                                nc.tensor.matmul(part.rearrange("p (j q) -> p j q", j=2), identb[:],
                                                 wink_add[:].rearrange("p a q -> p (a q)")[:, 0:n].unsqueeze(1).to_broadcast([P, 2, n]),
                                                 start=True, stop=False, skip_group_check=True)
                                for j in (2 * (i % 2), 2 * (i % 2) + 1):
                                    r, slot = stack_rows(p, 4 * g + j, PARTS)
                                    ins = nc.tensor.matmul(part[:, (j % 2) * n:(j % 2 + 1) * n], ks[r, slot, kt * P:(kt + 1) * P], QS[s][r, slot, S - n:S],
                                                           start=False, stop=True, skip_group_check=True)
                            else:
                                kt = i // 2
                                if p == 1:
                                    nc.tensor.matmul(bank.rearrange("p (j q) -> p j q", j=2), identb[:],
                                                     maskk_add[:, kt:kt + 1, :].to_broadcast([P, 2, S]), start=True, stop=False, skip_group_check=True)
                                for j in (2 * (i % 2), 2 * (i % 2) + 1):
                                    r, slot = stack_rows(p, 4 * g + j, PARTS)
                                    ins = nc.tensor.matmul(bank[:, (j % 2) * S:(j % 2 + 1) * S], ks[r, slot, kt * P:(kt + 1) * P], QS[s][r, slot, :],
                                                           start=(p == 3), stop=True, skip_group_check=(p == 1))
                            ins.then_inc(exp_scores, 1)
                            pending.append((g, i))
                            if len(pending) == 4:
                                av(*pending.pop(0))
                                av(*pending.pop(0))
                    for unit in pending:
                        av(*unit)

                def finish(s, p):
                    og = OUT_START[p, s] + GROUPS[p]
                    pe.wait_ge(out_kept, it * OUT_TOTAL + og + 2)
                    for t in range(TQ):
                        for g in range(GROUPS[p]):
                            ins = nc.tensor.transpose(side[:, t, g * P:(g + 1) * P], OT[s][:, g, t * P:(t + 1) * P], ident[:])
                    ins.then_inc(o_turned[s], 1)
                    pe.wait_ge(an_ready[s], it * 4 + p + 1)
                    for t in range(TQ):
                        ins = nc.tensor.transpose(side[:, 0, t * P:(t + 1) * P], An[:, t, :], ident[:])
                    ins.then_inc(an_turned[s], 1)
                    pe.wait_ge(at_ready[s], it * 4 + p + 1)
                    for t in range(TQ):
                        ins = nc.tensor.matmul(side[:, 1, t * D:(t + 1) * D], AT[:, t * P:(t + 1) * P], w(f"o{p}"), start=True, stop=True)
                    ins.then_inc(o_proj[s], 1)

                def experts(s):
                    turn(s, 2, hn)
                    for t in range(TQ):
                        ins = nc.tensor.matmul(side[:, 1, t * NE:(t + 1) * NE], hT[:, t * P:(t + 1) * P], w("gate"), start=True, stop=True)
                    ins.then_inc(gate_done[s], 1)
                    pe.wait_ge(gate_ready[s], it + 1)
                    for t in range(TQ):
                        ins = nc.tensor.transpose(side[0:NE, 0, t * P:(t + 1) * P], gate[:, t, :], ident[:])
                    ins.then_inc(gateT_done[s], 1)
                    pe.wait_ge(gateT_ready[s], it + 1)
                    for t in range(TQ):
                        ins = nc.tensor.matmul(side[:, 0, t * D:(t + 1) * D], gateT[:, t * P:(t + 1) * P], ebias[:], start=True, stop=True)
                    ins.then_inc(moe_bias[s], 1)
                    for i in range(4):
                        t, half_ = i // 2, i % 2
                        if i:
                            pe.wait_ge(experts_used[s], it * 5 + i)
                        ins = nc.tensor.matmul(side[:, (i + 1) % 2, :], hT[:, t * P:(t + 1) * P], w("experts", half_ * 512, 512), start=True, stop=True)
                        ins.then_inc(experts_done[s], 1)

                def feed_forward(s):
                    turn(s, 5, qn[s])
                    for n in range(FC):
                        ins = nc.tensor.matmul(side[:, 1 - n // 2, (n % 2) * S:(n % 2 + 1) * S], w("ffn1", n * P, P), hT[:], start=True, stop=True)
                    ins.then_inc(ffn_h[s], 1)
                    pe.wait_ge(ffn_act[s], it * 2 + 1)
                    for t in range(TQ):
                        for n in range(FC):
                            ins = nc.tensor.matmul(side[:, 0, t * D:(t + 1) * D], f1[:, n, t * P:(t + 1) * P], w("ffn2", n * D, D), start=(n == 0), stop=(n == FC - 1))
                    ins.then_inc(ffn_y[s], 1)

                def ternary(s):
                    turn(s, 7, hn)
                    for n in range(FC):
                        ins = nc.tensor.matmul(side[:, 1 - n // 2, (n % 2) * S:(n % 2 + 1) * S], w("up", n * P, P), hT[:], start=True, stop=True)
                    ins.then_inc(ffn_h[s], 1)
                    pe.wait_ge(ffn_act[s], it * 2 + 2)
                    for t in range(TQ):
                        for n in range(FC):
                            ins = nc.tensor.matmul(side[:, 0, t * D:(t + 1) * D], f1[:, n, t * P:(t + 1) * P], w("down", n * D, D), start=(n == 0), stop=(n == FC - 1))
                    ins.then_inc(ffn_y[s], 1)
                    pe.wait_ge(sq_ready[s], it + 1)
                    for t in range(TQ):
                        for n in range(FC):
                            ins = nc.tensor.matmul(side[:, 1, t:t + 1], sq[:, n, t * P:(t + 1) * P], ones_col[:, 0:1], start=(n == 0), stop=(n == FC - 1))
                    ins.then_inc(sq_sum[s], 1)

                for s in range(2):
                    turn(s, 0, hn)
                    project(s, 0)
                    state(s)
                    core(s, 0)
                    finish(s, 0)
                    turn(s, 1, hn)
                    project(s, 1)
                    core(s, 1)
                    finish(s, 1)
                    experts(s)
                    turn(s, 3, hn)
                    project(s, 2)
                    core(s, 2)
                    finish(s, 2)
                    turn(s, 4, qn[s])
                    project(s, 3)
                    core(s, 3)
                    finish(s, 3)
                    feed_forward(s)
                    ternary(s)

        @block.scalar
        def _(act):
            act.wait_ge(const_in, 5 * 16)
            nc.scalar.activation(keep[:], row("lambda"), ACT.Exp, scale=1.0).then_inc(act_const, 1)
            act.wait_ge(pool_const, 2)
            act.wait_ge(w_in[3], 16)
            for i in range(2):
                ins = nc.scalar.activation(wtmp[:, i, :], w(("up", "down")[i]), ACT.Abs, accum_out=absum[:, i:i + 1])
            ins.then_inc(act_const, 1)
            act.wait_ge(dve_const, 1)
            with act.Fori(0, PAIRS) as it:
                def turned(s, k):
                    act.wait_ge(ln_turned[s], it * NT + TURN_OF[k] + 1)
                    nc.scalar.copy(hT[:], side[:, 0, 0:S]).then_inc(hT_ready[s], 1)

                def take(s, p):
                    act.wait_ge(proj_done[s], it * 8 + 2 * p + 1)
                    if p == 0:
                        nc.scalar.activation(rs[:, 0:S], side[:, 0, 0:S], ACT.Identity, bias=c("q0"))
                        nc.scalar.activation(rs[:, S:2 * S], side[:, 0, S:2 * S], ACT.Identity, bias=c("k0")).then_inc(qk_raw[s], 1)
                        act.wait_ge(qk_raw[s], it + 1)
                        nc.scalar.activation(es[:], rs[:], ACT.Exp).then_inc(xs_act[s], 1)
                        act.wait_ge(k_turned[s], it + 1)
                        nc.scalar.copy(kTM[:], side[:, 0, 0:P]).then_inc(kTM_ready[s], 1)
                        return
                    cq, ck = (c("zero"), c("zero")) if p == 3 else (c(f"q{p}"), c(f"k{p}"))
                    kb = side[:, 1, :] if KEYS[p] == SK else side[:, 0, S:2 * S]
                    nc.scalar.activation(xs[s][:, 0:S], side[:, 0, 0:S], ACT.Identity, bias=cq)
                    nc.scalar.activation(xs[s][:, S:S + KEYS[p]], kb, ACT.Identity, bias=ck).then_inc(xs_act[s], 1)

                def keep_outputs(s, p, g):
                    act.wait_ge(av_done, it * EXP_TOTAL + EXP_START[p, s] + (g + 1) * EXP_UNITS[p])
                    nc.scalar.copy(OT[s][:, g, :], ob[:, (OUT_START[p, s] + g) % 2, 0:S]).then_inc(out_kept, 1)

                def core(s, p):
                    n2 = EXP_UNITS[p]
                    for g in range(GROUPS[p]):
                        for i in range(n2 if p else 0):
                            u = EXP_START[p, s] + g * n2 + i
                            act.wait_ge(exp_scores, it * EXP_TOTAL + u + 1)
                            if u >= 4:
                                act.wait_ge(av_done, it * EXP_TOTAL + u - 3)
                            n = 2 * P if p == 2 and i >= 2 else FF
                            nc.scalar.activation(probs[:, u % 4, 0:n], eb[:, u % 2, 0:n], ACT.Exp, scale=SCALE[p]).then_inc(probs_ready, 1)
                            if g and i == KEEP_AFTER[p]:
                                keep_outputs(s, p, g - 1)
                        if not p:
                            keep_outputs(s, p, g)
                    if p:
                        keep_outputs(s, p, GROUPS[p] - 1)

                def finish(s, p):
                    act.wait_ge(an_turned[s], it * 4 + p + 1)
                    nc.scalar.copy(AT[:], side[:, 0, 0:S]).then_inc(at_ready[s], 1)

                for s in range(2):
                    turned(s, 0)
                    take(s, 0)
                    core(s, 0)
                    finish(s, 0)
                    turned(s, 1)
                    take(s, 1)
                    core(s, 1)
                    finish(s, 1)
                    turned(s, 2)
                    act.wait_ge(gexp_in[s], it + 1)
                    for t in range(TQ):
                        ins = nc.scalar.activation(gp[:, t, :], gl[:, t, :], ACT.Exp, bias=gm[:, t:t + 1], accum_out=gsum[:, t:t + 1])
                    ins.then_inc(gexp_out[s], 1)
                    act.wait_ge(gateT_done[s], it + 1)
                    nc.scalar.copy(gateT[:], side[0:NE, 0, 0:S]).then_inc(gateT_ready[s], 1)
                    turned(s, 3)
                    take(s, 2)
                    core(s, 2)
                    finish(s, 2)
                    turned(s, 4)
                    take(s, 3)
                    core(s, 3)
                    finish(s, 3)
                    turned(s, 5)
                    act.wait_ge(ffn_h[s], it * 2 + 1)
                    for n in range(FC):
                        ins = nc.scalar.activation(f1[:, n, :], side[:, 1 - n // 2, (n % 2) * S:(n % 2 + 1) * S], ACT.Relu, bias=c("ffn1", n))
                    ins.then_inc(ffn_act[s], 1)
                    turned(s, 7)
                    act.wait_ge(ffn_h[s], it * 2 + 2)
                    for n in range(0, FC, 2):
                        ins = nc.scalar.activation(f1[:, n:n + 2, :].rearrange("p a t -> p (a t)"), side[:, 1 - n // 2, :], ACT.Gelu)
                    ins.then_inc(ffn_act[s], 1)
                    act.wait_ge(ffn_act[s], it * 2 + 2)
                    nc.scalar.activation(sq[:], f1[:], ACT.Square).then_inc(sq_ready[s], 1)

        @block.vector
        def _(dve):
            chain = Chain("dve", dve, dve_step)
            link, done = chain.link, chain.done
            V_ = nc.vector
            dve.wait_ge(pool_const, 2)
            dve.wait_ge(const_in, 5 * 16)
            V_.tensor_scalar(maskq_add[:], maskq8[:], NEG_MAX, None, ALU.mult)
            V_.tensor_scalar(maskk_add[:], maskk8[:], NEG_EXP, None, ALU.mult)
            V_.tensor_reduce(own[:], head_of[:].rearrange("p a h -> p h a"), AX.X, ALU.add)
            dve.wait_ge(act_const, 1)
            link(V_.tensor_scalar(keep[:], keep[:], 1.0, None, ALU.add))
            link(V_.reciprocal(keep[:], keep[:]))
            dve.wait_ge(act_const, 2)
            dve.wait_ge(pe_const, 1)
            link(V_.tensor_scalar(alpha[:], side[:, 0, 0:2], 0.5 / (D * FF), None, ALU.mult))
            for i, n in enumerate(("up", "down")):
                link(V_.tensor_scalar(wtmp[:, i, :], w(n), alpha[:, i:i + 1], None, ALU.is_gt))
                link(V_.tensor_scalar(sq[:, 0:2, :].rearrange("p a t -> p (a t)"), w(n), -1.0, alpha[:, i:i + 1], ALU.mult, ALU.is_gt))
                link(V_.tensor_tensor(wtmp[:, i, :], wtmp[:, i, :], sq[:, 0:2, :].rearrange("p a t -> p (a t)"), ALU.subtract))
                link(V_.tensor_tensor(wtmp[:, i, :], wtmp[:, i, :], w(n), ALU.subtract))
                link(V_.tensor_tensor(w(n), w(n), wtmp[:, i, :], ALU.add))
            V_.memset(junk32[:], 0.0).then_inc(dve_const, 1)
            for i in range(2):
                V_.memset(junk[:, 0, i:i + 1], 0.0).then_inc(max_used, 1)
                V_.memset(junk[:, 1, i:i + 1], 0.0).then_inc(out_kept, 1)
            with dve.Fori(0, PAIRS) as it:
                chain.enter(it)

                def norm(s, k, src, dst, dst_is_final=True):
                    for t in range(TQ):
                        ins = V_.bn_stats(stats[:, t, :], src[:, t, :])
                    link(ins, plain=True)
                    for t in range(TQ):
                        ins = V_.bn_aggr(mv[:, t, :], stats[:, t, :])
                    ins.then_inc(ln_stats[s], 1)
                    dve.wait_ge(ln_rstd[s], it * NORMS + k + 1)
                    for t in range(TQ):
                        ins = V_.tensor_scalar(dst[:, t, :], src[:, t, :], mv[:, t, 0:1], rstd[:, t:t + 1], ALU.subtract, ALU.mult)
                    return ins

                def take(s, p):
                    keys, heads, hd = KEYS[p], HEADS[p], HD[p]
                    tk = keys // P
                    if p == 0:
                        dve.wait_ge(xs_act[s], it * 4 + 1)
                        link(V_.tensor_scalar(rs[:], rs[:], 0.0, None, ALU.max))
                        V_.scalar_tensor_tensor(xs[s][:, 0:2 * S], es[:], 1.0, rs[:], ALU.min, ALU.add).then_inc(xs_ready[s], 1)
                    dve.wait_ge(proj_done[s], it * 8 + 2 * p + 2)
                    vb = side[:, 0 if keys == SK else 1, 0:tk * D].rearrange("p (t h d) -> p (t h) d", t=tk, h=heads)
                    dst = V[p][s][:, 0:tk, :, 0:hd].rearrange("p t h d -> p (t h) d")
                    if p == 3:
                        V_.tensor_copy(dst, vb).then_inc(v_ready[s], 1)
                    else:
                        bias = row(f"v{p}").rearrange("p (h d) -> p h d", h=heads)
                        for t in range(tk):
                            ins = V_.tensor_tensor(dst[:, t * heads:(t + 1) * heads, :], vb[:, t * heads:(t + 1) * heads, :], bias, ALU.add)
                        ins.then_inc(v_ready[s], 1)
                    if p == 0:
                        dve.wait_ge(xs_ready[s], it + 1)
                    else:
                        dve.wait_ge(xs_act[s], it * 4 + p + 1)
                    n = S + keys
                    link(V_.tensor_copy(parts[:, 0, 0:n], xs[s][:, 0:n]))
                    link(V_.tensor_tensor(rest[:, 0:n], xs[s][:, 0:n], parts[:, 0, 0:n], ALU.subtract))
                    link(V_.tensor_copy(parts[:, 1, 0:n], rest[:, 0:n]))
                    V_.tensor_tensor(parts[:, 2, 0:n], rest[:, 0:n], parts[:, 1, 0:n], ALU.subtract).then_inc(split_done[s], 1)
                    if p == 0:
                        dve.wait_ge(kv_done[s], it + 1)
                        V_.tensor_tensor(KV[s][:], side[:, 1, :].rearrange("p (h e) -> p h e", h=16),
                                         own[:].unsqueeze(2).to_broadcast([P, 16, VW]), ALU.mult).then_inc(kv_ready[s], 1)

                def core(s, p):
                    n2 = EXP_UNITS[p]
                    mu = MAX_START[p, s]
                    if p == 0:
                        for g in range(GROUPS[p]):
                            for i in range(n2):
                                u = EXP_START[p, s] + g * n2 + i
                                dve.wait_ge(exp_scores, it * EXP_TOTAL + u + 1)
                                if u >= 4:
                                    dve.wait_ge(av_done, it * EXP_TOTAL + u - 3)
                                V_.tensor_tensor(probs[:, u % 4, :].rearrange("p (j q) -> p j q", j=4), eb[:, u % 2, :].rearrange("p (j q) -> p j q", j=4),
                                                 tri[:].unsqueeze(1).to_broadcast([P, 4, P]), ALU.mult).then_inc(probs_ready, 1)
                        return
                    for blk in core_order(p):
                        if blk[0] == "max":
                            _, g, i = blk
                            dve.wait_ge(max_scores, it * MAX_TOTAL + mu + 1)
                            wait_alone(dve)
                            bank = mb[:, mu % 2, :]
                            if p == 1:
                                h, t = 4 * g + i // 2, i % 2
                                ins = V_.tensor_tensor_reduce(junk[:, mu % 2, :], bank, maskq_add[:, t, :], 1.0, NEG_EXP, ALU.add, ALU.max, mx[s][:, t, h:h + 1])
                            elif p == 2:
                                h = 4 * g + i
                                V_.tensor_tensor_reduce(junk[:, mu % 2, 0:P], bank[:, 0:P], winq_add[:, 0, :], 1.0, NEG_EXP, ALU.add, ALU.max, mx[s][:, 0, h:h + 1])
                                ins = V_.tensor_tensor_reduce(junk[:, mu % 2, P:3 * P], bank[:, P:3 * P], winq_add[:, 1:3, :].rearrange("p a k -> p (a k)"), 1.0, NEG_EXP,
                                                              ALU.add, ALU.max, mx[s][:, 1, h:h + 1])
                            else:
                                h, t = 4 * g + i // 2, i % 2
                                ins = V_.tensor_reduce(mx[s][:, t, h:h + 1], bank, AX.X, ALU.max)
                            ins.then_inc(max_used, 1)
                            mu += 1
                            if i == MAX_UNITS[p] - 1:
                                dve.wait_ge(max_used, it * MAX_TOTAL + mu + 2)
                                m = mx[s][:, :, 4 * g:4 * g + 4]
                                r = nmr[s][:, :, 4 * g:4 * g + 4]
                                n = [nm[s][:, :, 4 * g:4 * g + 4, a] for a in range(PARTS)]
                                link(V_.tensor_scalar(n[0], m, -1.0, None, ALU.mult))
                                link(V_.tensor_scalar(r, m, -1.0, None, ALU.mult))
                                link(V_.tensor_tensor(r, r, n[0], ALU.subtract))
                                link(V_.tensor_copy(n[1], r))
                                V_.tensor_tensor(n[2], r, n[1], ALU.subtract).then_inc(nm_ready[s], 1)
                        elif blk[0] == "turn":
                            _, g = blk
                            dve.wait_ge(max_scores, it * MAX_TOTAL + mu + 1)
                            V_.tensor_copy(mrow[s][:, g, :], mb[:, mu % 2, :].bitcast(BF16)[0:12, 0:S]).then_inc(max_used, 1)
                            mu += 1

                def finish(s, p):
                    heads, hd = HEADS[p], HD[p]
                    dve.wait_ge(o_turned[s], it * 4 + p + 1)
                    n = GROUPS[p] * 4
                    for t in range(TQ):
                        o = side[:, t, 0:n * VW].rearrange("p (h e) -> p h e", h=n)
                        r = rden[:, t * n:(t + 1) * n]
                        if p == 0:
                            link(V_.tensor_scalar(r.unsqueeze(2), o[:, :, hd:hd + 1], DEN_EPS, None, ALU.add))
                            link(V_.reciprocal(r, r))
                        else:
                            link(V_.reciprocal(r.unsqueeze(2), o[:, :, hd:hd + 1]))
                        if p == 3:
                            link(V_.tensor_scalar(r, r, keep[:], None, ALU.mult))
                        ins = V_.tensor_tensor(An[:, t, :].rearrange("p (h d) -> p h d", h=heads), o[:, :, 0:hd],
                                               r.unsqueeze(2).to_broadcast([P, n, hd]), ALU.mult)
                    ins.then_inc(an_ready[s], 1)
                    dve.wait_ge(o_proj[s], it * 4 + p + 1)
                    y = side[:, 1, 0:S].rearrange("p (t d) -> p t d", t=TQ)
                    if p < 3:
                        link(V_.tensor_tensor(X[s][:], X[s][:], y, ALU.add))
                        V_.tensor_tensor(X[s][:], X[s][:], row(f"o{p}").unsqueeze(1).to_broadcast([P, TQ, D]), ALU.add).then_inc(x_updated[s], 1)
                    else:
                        link(V_.tensor_tensor(acc[:], qn[s][:], y, ALU.add))

                def affine(dst, g, b):
                    link(V_.tensor_tensor(dst, dst, row(g).unsqueeze(1).to_broadcast([P, TQ, D]), ALU.mult))
                    return V_.tensor_tensor(dst, dst, row(b).unsqueeze(1).to_broadcast([P, TQ, D]), ALU.add)

                def experts(s):
                    norm(s, 2, X[s], hn).then_inc(ln_rows[s], 1)
                    dve.wait_ge(gate_done[s], it + 1)
                    link(V_.tensor_tensor(gl[:], side[:, 1, 0:TQ * NE].rearrange("p (t e) -> p t e", t=TQ),
                                          row("gate").unsqueeze(1).to_broadcast([P, TQ, NE]), ALU.add))
                    V_.tensor_reduce(gm[:], gl[:], AX.X, ALU.max, negate=True).then_inc(gexp_in[s], 1)
                    dve.wait_ge(gexp_out[s], it + 1)
                    link(V_.reciprocal(grec[:], gsum[:]))
                    link(V_.tensor_tensor(gp[:], gp[:], grec[:].unsqueeze(2).to_broadcast([P, TQ, NE]), ALU.mult))
                    flat = gp[:].rearrange("p t e -> p (t e)")
                    for t in range(TQ):
                        pj = gp[:, t:t + 1, :].to_broadcast([P, NE, NE])
                        pe_ = gp[:, t, :].unsqueeze(2).to_broadcast([P, NE, NE])
                        sl = slice(t * NE, (t + 1) * NE)
                        V_.tensor_tensor(cmp_gt[:, sl, :], pj, pe_, ALU.is_gt)
                        link(V_.tensor_tensor(cmp_eq[:, sl, :], pj, pe_, ALU.is_equal))
                        link(V_.tensor_tensor(cmp_eq[:, sl, :], cmp_eq[:, sl, :], first[:], ALU.mult))
                        link(V_.tensor_tensor(cmp_gt[:, sl, :], cmp_gt[:, sl, :], cmp_eq[:, sl, :], ALU.add))
                    link(V_.tensor_reduce(rank[:].rearrange("p t e -> p (t e)"), cmp_gt[:], AX.X, ALU.add))
                    link(V_.scalar_tensor_tensor(gate[:].rearrange("p t e -> p (t e)"), rank[:].rearrange("p t e -> p (t e)"), 2.0, flat, ALU.is_lt, ALU.mult))
                    link(V_.tensor_reduce(gsum[:], gate[:], AX.X, ALU.add))
                    link(V_.reciprocal(grec[:], gsum[:]))
                    V_.tensor_tensor(gate[:], gate[:], grec[:].unsqueeze(2).to_broadcast([P, TQ, NE]), ALU.mult).then_inc(gate_ready[s], 1)
                    dve.wait_ge(moe_bias[s], it + 1)
                    V_.tensor_tensor(acc[:], X[s][:], side[:, 0, 0:S].rearrange("p (t d) -> p t d", t=TQ), ALU.add).then_inc(experts_used[s], 1)
                    dve.wait_ge(experts_used[s], it * 5 + 1)
                    for i in range(4):
                        t, half_ = i // 2, i % 2
                        dve.wait_ge(experts_done[s], it * 4 + i + 1)
                        for e in range(4):
                            last = half_ == 1 and e == 3
                            ins = V_.scalar_tensor_tensor((X[s] if last else acc)[:, t, :], side[:, (i + 1) % 2, e * D:(e + 1) * D],
                                                          gate[:, t, half_ * 4 + e:half_ * 4 + e + 1], acc[:, t, :], ALU.mult, ALU.add)
                            if e < 3:
                                link(ins)
                        ins.then_inc(experts_used[s], 1)
                        dve.wait_ge(experts_used[s], it * 5 + i + 2)

                for s in range(2):
                    dve.wait_ge(x_in[s], it * 16 + 16)
                    norm(s, 0, X[s], hn).then_inc(ln_rows[s], 1)
                    take(s, 0)
                    core(s, 0)
                    finish(s, 0)
                    dve.wait_ge(x_updated[s], it * 5 + 1)
                    norm(s, 1, X[s], hn).then_inc(ln_rows[s], 1)
                    take(s, 1)
                    core(s, 1)
                    finish(s, 1)
                    dve.wait_ge(x_updated[s], it * 5 + 2)
                    experts(s)
                    norm(s, 3, X[s], hn).then_inc(ln_rows[s], 1)
                    take(s, 2)
                    core(s, 2)
                    finish(s, 2)
                    dve.wait_ge(x_updated[s], it * 5 + 3)
                    norm(s, 4, X[s], qn[s]).then_inc(ln_rows[s], 1)
                    take(s, 3)
                    core(s, 3)
                    finish(s, 3)
                    link(norm(s, 5, acc, qn[s]))
                    affine(qn[s][:], "ln1_g", "ln1_b").then_inc(ln_rows[s], 1)
                    dve.wait_ge(ffn_y[s], it * 2 + 1)
                    link(V_.tensor_tensor(acc[:], qn[s][:], side[:, 0, 0:S].rearrange("p (t d) -> p t d", t=TQ), ALU.add))
                    link(V_.tensor_tensor(acc[:], acc[:], row("ffn2").unsqueeze(1).to_broadcast([P, TQ, D]), ALU.add))
                    link(norm(s, 6, acc, hn))
                    link(affine(hn[:], "ln2_g", "ln2_b"))
                    V_.tensor_tensor(X[s][:], X[s][:], hn[:], ALU.add).then_inc(x_updated[s], 1)
                    dve.wait_ge(x_updated[s], it * 5 + 4)
                    link(norm(s, 7, X[s], hn))
                    for t in range(TQ):
                        ins = V_.tensor_tensor_reduce(junk32[:, t, :], hn[:, t, :], hn[:, t, :], 1.0, 0.0, ALU.mult, ALU.add, ssum[:, t:t + 1])
                    ins.then_inc(rms_sum[s], 1)
                    dve.wait_ge(rms_root[s], it * 2 + 1)
                    link(V_.reciprocal(irms[:], rms[:]))
                    for t in range(TQ):
                        ins = V_.tensor_scalar(hn[:, t, :], hn[:, t, :], irms[:, t:t + 1], None, ALU.mult)
                    ins.then_inc(ln_rows[s], 1)
                    dve.wait_ge(sq_sum[s], it + 1)
                    V_.tensor_copy(ssum[:], side[:, 1, 0:TQ]).then_inc(rms_sum[s], 1)
                    dve.wait_ge(rms_root[s], it * 2 + 2)
                    link(V_.reciprocal(irms[:], rms[:]))
                    for t in range(TQ):
                        ins = V_.scalar_tensor_tensor(X[s][:, t, :], side[:, 0, t * D:(t + 1) * D], irms[:, t:t + 1], X[s][:, t, :], ALU.mult, ALU.add)
                    ins.then_inc(x_updated[s], 1)
                    dve.wait_ge(x_updated[s], it * 5 + 5)
                chain.leave()


GRP_START, _n = [], 0
for _p in PHASES:
    GRP_START.append(_n)
    _n += GROUPS[_p] if MAX_UNITS[_p] else 0
GRP_TOTAL = _n
STACK_UPTO, _n = [], 0
for _p in PHASES:
    _n += 16 * (3 + NPROD) * (1 if _p == 3 else 2)
    STACK_UPTO.append(_n)
STACK_TOTAL = _n
chain_counts = {}


def in_order(w, heads):
    w = w.reshape(heads, D // heads, -1)
    if heads == 16:
        w = w.reshape(4, 2, 2, D // heads, -1).transpose(0, 2, 1, 3, 4).reshape(heads, D // heads, -1)
    return w.transpose(1, 0, 2).reshape(D, -1)


def kernel(**a):
    import concourse.bacc as bacc
    from concourse.bass_utils import run_bass_kernel_spmd

    a = {k: np.asarray(v) for k, v in a.items()}

    def turned(w, heads):
        return in_order(w, heads).T

    def chunks(w):
        return w.reshape(FC, P, D).transpose(1, 0, 2).reshape(P, FC * D)

    wi, bi = a["L1_attn_w_in"], a["L1_attn_b_in"]
    parts = {
        "q0": turned(a["L0_attn_Wq"], 16), "k0": turned(a["L0_attn_Wk"], 16), "v0": a["L0_attn_Wv"].T, "o0": a["L0_attn_Wo"].T,
        "q1": turned(a["L0_xattn_q_w"], 16), "k1": turned(a["L0_xattn_k_w"], 16), "v1": a["L0_xattn_v_w"].T, "o1": a["L0_xattn_o_w"].T,
        "gate": a["L0_ffn_Wg"], "experts": a["L0_ffn_We"].transpose(2, 0, 1).reshape(D, NE * D),
        "q2": turned(wi[0:D], 16), "k2": turned(wi[D:2 * D], 16), "v2": wi[2 * D:].T, "o2": a["L1_attn_w_out"].T,
        "q3": turned(a["L1_xattn_Wq"].T, 8), "k3": turned(a["L1_xattn_Wk"].T, 8), "v3": a["L1_xattn_Wv"], "o3": a["L1_xattn_Wo"],
        "ffn1": a["L1_xattn_ffn_w1"], "ffn2": chunks(a["L1_xattn_ffn_w2"]),
        "up": a["L1_ffn_w_up"].T, "down": chunks(a["L1_ffn_w_down"].T),
    }
    columns = {
        "q0": in_order(a["L0_attn_bq"], 16), "k0": in_order(a["L0_attn_bk"], 16),
        "q1": in_order(a["L0_xattn_q_b"], 16), "k1": in_order(a["L0_xattn_k_b"], 16),
        "q2": in_order(bi[0:D], 16), "k2": in_order(bi[D:2 * D], 16), "zero": np.zeros((D, 1), np.float32),
        "ffn1": a["L1_xattn_ffn_b1"].reshape(FC, P).T,
    }
    rows = {
        "v0": a["L0_attn_bv"], "o0": a["L0_attn_bo"], "v1": a["L0_xattn_v_b"], "o1": a["L0_xattn_o_b"],
        "v2": bi[2 * D:], "o2": a["L1_attn_b_out"], "ln1_g": a["L1_xattn_ln1_g"], "ln1_b": a["L1_xattn_ln1_b"],
        "ln2_g": a["L1_xattn_ln2_g"], "ln2_b": a["L1_xattn_ln2_b"], "ffn2": a["L1_xattn_ffn_b2"], "gate": a["L0_ffn_bg"],
        "lambda": a["L1_xattn_lambda_param"].reshape(1),
    }
    mask = a["mask_SxS2_bk1"]
    arrays = {
        "x": a["x"],
        "ctxT": a["ctx_1024"].transpose(0, 2, 1),
        "maskq": mask,
        "maskk": mask.T,
        "weights": np.concatenate([parts[n] for n in W_COLS], axis=1),
        "columns": np.concatenate([columns[n] for n in C_COLS], axis=1),
        "rows": np.concatenate([rows[n] for n in R_COLS]).reshape(1, R_TOTAL),
        "experts_bias": a["L0_ffn_be"],
    }
    arrays = {k: np.ascontiguousarray(v) for k, v in arrays.items()}

    def program():
        nc = bacc.Bacc("TRN2", target_bir_lowering=False, num_devices=1)
        args = [nc.dram_tensor(f"{k}_dram", v.shape, mybir.dt.from_np(v.dtype), kind="ExternalInput").ap() for k, v in arrays.items()]
        args.append(nc.dram_tensor("out_dram", (B, S, D), F32, kind="ExternalOutput").ap())
        decoder(nc, *args)
        return nc

    program()
    nc = program()
    r = run_bass_kernel_spmd(nc, [{f"{k}_dram": v for k, v in arrays.items()}], core_ids=[0])
    return r.results[0]["out_dram"]
```

```python
from contextlib import ExitStack

import numpy as np

import concourse.bass as bass
from concourse import mybir

F32 = mybir.dt.float32
BF16 = mybir.dt.bfloat16
U8 = mybir.dt.uint8
ALU = mybir.AluOpType
ACT = mybir.ActivationFunctionType
AX = mybir.AxisListType

P = 128
B, S, D, SK = 8, 256, 128, 512
TQ, TK = S // P, SK // P
NE, FF = 8, 512
FC = FF // P
PARTS = 3
Q_OF = (0, 1, 2, 0, 1, 0)
K_OF = (0, 1, 0, 2, 0, 1)
NPROD = len(Q_OF)
NEG_MAX = -1.0e30
NEG_EXP = -3.0e38
LN_EPS, DEN_EPS, RMS_EPS = 1e-5, 1e-6, 1e-8
VW = 32

HEADS = (16, 16, 16, 8)
HD = tuple(D // h for h in HEADS)
KEYS = (S, SK, S, SK)
GROUPS = tuple(h // 4 for h in HEADS)
SCALE = (1.0, 8 ** -0.5, 8 ** -0.5, 16 ** -0.5)
MAX_UNITS = (0, 8, 4, 8)
KEEP_AFTER = (0, 4, 2, 4)
EXP_UNITS = (2, 8, 4, 8)
PHASES = range(4)
MAX_ROWS = 4 * PARTS

FIRST_STEPS = ((None, (("load", 0), ("to0", 0))), ((0, 0), (("load", 1), ("to0", 1))))
STEPS = (
    ((0, 1), (("to1", 0),)),
    ((1, 0), (("to1", 1),)),
    ((1, 1), (("to2", 0),)),
    ((2, 0), (("to2", 1),)),
    ((2, 1), (("to3", 0),)),
    ((3, 0), (("to3", 1),)),
    ((3, 1), (("end", 0), ("next load", 0), ("next to0", 0))),
    (("next", 0), (("end", 1), ("next load", 1), ("next to0", 1))),
)
TICKS = {"load": 1, "to0": 17, "to1": 21, "to2": 42, "to3": 21, "end": 36}

W_COLS = {}
_at = 0
for _n, _w in (("q0", D), ("k0", D), ("v0", D), ("o0", D), ("q1", D), ("k1", D), ("v1", D), ("o1", D),
               ("gate", NE), ("experts", NE * D), ("q2", D), ("k2", D), ("v2", D), ("o2", D),
               ("q3", D), ("k3", D), ("v3", D), ("o3", D), ("ffn1", FF), ("ffn2", FF),
               ("up", FF), ("down", FF)):
    W_COLS[_n] = (_at, _at + _w)
    _at += _w
W_TOTAL = _at
W_LOADS = (0, W_COLS["q1"][0], W_COLS["q2"][0], W_COLS["up"][0], W_TOTAL)
C_COLS = {n: i for i, n in enumerate(("q0", "k0", "q1", "k1", "q2", "k2", "zero", "ffn1"))}
C_TOTAL = C_COLS["ffn1"] + FC
R_COLS = {}
_at = 0
for _n, _w in (("v0", D), ("o0", D), ("v1", D), ("o1", D), ("v2", D), ("o2", D), ("ln1_g", D),
               ("ln1_b", D), ("ln2_g", D), ("ln2_b", D), ("ffn2", D), ("gate", NE), ("lambda", 1)):
    R_COLS[_n] = (_at, _at + _w)
    _at += _w
R_TOTAL = _at


CORES = [(0 if c[0] == "next" else c[0], c[1]) for c, _ in STEPS]


def unit_starts(units):
    at, found = 0, {}
    for key in CORES:
        found[key] = at
        at += GROUPS[key[0]] * units[key[0]]
    return found, at, GROUPS[0] * units[0]


MAX_START, MAX_TOTAL, MAX_FIRST = unit_starts([n + 1 if n else 0 for n in MAX_UNITS])
EXP_START, EXP_TOTAL, EXP_FIRST = unit_starts(EXP_UNITS)
OUT_START, OUT_TOTAL, OUT_FIRST = unit_starts((1, 1, 1, 1))
assert not (EXP_FIRST % 4 or EXP_TOTAL % 4 or OUT_FIRST % 2 or OUT_TOTAL % 2 or MAX_FIRST % 2 or MAX_TOTAL % 2)


def core_order(p):
    n1, n2, ng = MAX_UNITS[p], EXP_UNITS[p], GROUPS[p]
    if not n1:
        return [("exp", g, i) for g in range(ng) for i in range(n2)]
    out = [("max", 0, i) for i in range(n1)]
    if ng > 1:
        out += [("max", 1, i) for i in range(3)] + [("turn", 0)] + [("max", 1, i) for i in range(3, n1)]
    for g in range(ng):
        ahead = [("max", g + 2, i) for i in range(n1)] if g + 2 < ng else []
        if g + 1 < ng:
            ahead.insert(0, ("turn", g + 1))
        for i in range(n2):
            out.append(("exp", g, i))
            take = len(ahead) * (i + 1) // n2 - len(ahead) * i // n2
            at = len(ahead) * i // n2
            out += ahead[at:at + take]
    return out


def weave(core, chains, blocks, ticks):
    hop = next(chains, None)
    for block in core:
        while hop is not None and hop * blocks <= block * ticks:
            hop = next(chains, None)
    while hop is not None:
        hop = next(chains, None)


def decoder(nc, x, ctxT, maskq, maskk, weights, columns, rows_in, experts_bias, out):
    with ExitStack() as ctx:
        def sb(name, shape, dt=F32):
            return ctx.enter_context(nc.sbuf_tensor(name, shape, dt))

        def psum(name, shape, dt=F32):
            return ctx.enter_context(nc.psum_tensor(name, shape, dt))

        def sem(name):
            return ctx.enter_context(nc.semaphore(name))

        def pair(name):
            return [sem(f"{name}_{s}") for s in range(2)]

        W = sb("W", [P, W_TOTAL])
        col = sb("col", [P, C_TOTAL])
        rows = sb("rows", [P, R_TOTAL])
        ebias = sb("ebias", [NE, D])
        ident = sb("ident", [P, P])
        identb = sb("identb", [P, P], BF16)
        zero = sb("zero", [P, FF])
        tri = sb("tri", [P, P])
        head_of = sb("head_of", [P, 8, 16])
        own = sb("own", [P, 16])
        first = sb("first", [P, NE, NE])
        maskq8 = sb("maskq8", [P, TQ, SK], U8)
        maskk8 = sb("maskk8", [P, TK, S], U8)
        maskq_add = sb("maskq_add", [P, TQ, SK], BF16)
        maskk_add = sb("maskk_add", [P, TK, S], BF16)
        winq_add = sb("winq_add", [P, 3, P], BF16)
        wink_add = sb("wink_add", [P, 2, P], BF16)
        half = sb("half", [P, 2 * TQ])
        keep = sb("keep", [P, 1])
        absum = sb("absum", [P, 2])
        alpha = sb("alpha", [P, 2])
        wtmp = sb("wtmp", [P, 2, FF])
        ones_col = sb("ones_col", [P, P])
        X = [sb(f"X{s}", [P, TQ, D]) for s in range(2)]
        qn = [sb(f"qn{s}", [P, TQ, D]) for s in range(2)]
        QS = [sb(f"QS{s}", [P, 8, S], BF16) for s in range(2)]
        KS8 = [sb(f"KS8{s}", [P, 8, SK], BF16) for s in range(2)]
        KS16 = [sb(f"KS16{s}", [P, 8, SK], BF16) for s in range(2)]
        V8 = [sb(f"V8{s}", [P, TK, 16, VW]) for s in range(2)]
        V16 = [sb(f"V16{s}", [P, TK, 8, VW]) for s in range(2)]
        OT = [sb(f"OT{s}", [P, 4, S]) for s in range(2)]
        KV = [sb(f"KV{s}", [P, 16, VW]) for s in range(2)]
        xs = [sb(f"xs{s}", [P, S + SK]) for s in range(2)]
        cT = [sb(f"cT{s}", [P, SK]) for s in range(2)]
        mx = [sb(f"mx{s}", [P, TQ, 16]) for s in range(2)]
        nmr = [sb(f"nmr{s}", [P, TQ, 16]) for s in range(2)]
        nm = [sb(f"nm{s}", [P, TQ, 16, PARTS], BF16) for s in range(2)]
        mrow = [sb(f"mrow{s}", [12, 4, S], BF16) for s in range(2)]
        stats = sb("stats", [P, TQ, 6])
        mv = sb("mv", [P, TQ, 2])
        var = sb("var", [P, TQ])
        rstd = sb("rstd", [P, TQ])
        hn = sb("hn", [P, TQ, D])
        hT = sb("hT", [P, S])
        es = sb("es", [P, 2 * S])
        rs = sb("rs", [P, 2 * S])
        parts = [sb(f"parts{s}", [P, NPROD, S + SK], BF16) for s in range(2)]
        rest = sb("rest", [P, S + SK])
        kTM = sb("kTM", [P, P])
        rden = sb("rden", [P, TQ * 16])
        An = sb("An", [P, TQ, D])
        AT = sb("AT", [P, S])
        gl = sb("gl", [P, TQ, NE])
        gm = sb("gm", [P, TQ])
        gp = sb("gp", [P, TQ, NE])
        gsum = sb("gsum", [P, TQ])
        grec = sb("grec", [P, TQ])
        cmp_gt = sb("cmp_gt", [P, TQ * NE, NE])
        cmp_eq = sb("cmp_eq", [P, TQ * NE, NE])
        rank = sb("rank", [P, TQ, NE])
        gate = sb("gate", [P, TQ, NE])
        gateT = sb("gateT", [NE, S])
        acc = sb("acc", [P, TQ, D])
        f1 = sb("f1", [P, FC, S])
        sq = sb("sq", [P, FC, S])
        ssum = sb("ssum", [P, TQ])
        rms = sb("rms", [P, TQ])
        irms = sb("irms", [P, TQ])
        junk = sb("junk", [P, 2, SK], BF16)
        junk32 = sb("junk32", [P, TQ, P])
        probs = sb("probs", [P, 4, FF])
        bounce = [nc.dram_tensor(f"bounce{s}", (NPROD, P, S + SK), BF16, kind="Internal").ap() for s in range(2)]

        mb = psum("mb", [P, 2, 512])
        eb = psum("eb", [P, 2, 512])
        ob = psum("ob", [P, 2, 512])
        side = psum("side", [P, 2, 512])

        w_in = [sem(f"w_in{i}") for i in range(len(W_LOADS) - 1)]
        const_in = sem("const_in")
        pool_const, dve_const, pe_const, act_const = sem("pool_const"), sem("dve_const"), sem("pe_const"), sem("act_const")
        dve_step, act_step, pool_step, pe_step = sem("dve_step"), sem("act_step"), sem("pool_step"), sem("pe_step")
        x_in, ctx_in, x_out = pair("x_in"), pair("ctx_in"), pair("x_out")
        ln_stats, ln_rstd, ln_rows, ln_turned, hT_ready = (pair(n) for n in ("ln_stats", "ln_rstd", "ln_rows", "ln_turned", "hT_ready"))
        proj_done, exp_in, xs_act, xs_ready, v_ready, split_done = (pair(n) for n in ("proj_done", "exp_in", "xs_act", "xs_ready", "v_ready", "split_done"))
        bounce_in, stack_in, mrow_in = pair("bounce_in"), pair("stack_in"), pair("mrow_in")
        k_turned, kTM_ready, kv_done, kv_ready = (pair(n) for n in ("k_turned", "kTM_ready", "kv_done", "kv_ready"))
        first_part, spread = pair("first_part"), pair("spread")
        nm_ready, qk_raw = pair("nm_ready"), pair("qk_raw")
        max_scores, max_used = sem("max_scores"), sem("max_used")
        exp_scores, probs_ready, av_done = sem("exp_scores"), sem("probs_ready"), sem("av_done")
        out_kept = sem("out_kept")
        o_turned, an_ready, an_turned, at_ready, o_proj = (pair(n) for n in ("o_turned", "an_ready", "an_turned", "at_ready", "o_proj"))
        x_updated = pair("x_updated")
        gate_done, gate_ready, gateT_done, gateT_ready, experts_done, experts_used, moe_bias = (
            pair(n) for n in ("gate_done", "gate_ready", "gateT_done", "gateT_ready", "experts_done", "experts_used", "moe_bias"))
        gexp_in, gexp_out = pair("gexp_in"), pair("gexp_out")
        ffn_h, ffn_act, ffn_y = pair("ffn_h"), pair("ffn_act"), pair("ffn_y")
        rms_sum, rms_root = pair("rms_sum"), pair("rms_root")
        sq_ready, sq_sum = pair("sq_ready"), pair("sq_sum")

        def w(name, lo=0, n=None):
            a, b = W_COLS[name]
            return W[:, a + lo:(a + lo + n) if n else b]

        def row(name):
            return rows[:, R_COLS[name][0]:R_COLS[name][1]]

        def c(name, i=0):
            return col[:, C_COLS[name] + i:C_COLS[name] + i + 1]

        def stack_rows(p, h, extra=0):
            if p == 3:
                return slice(0, NPROD * 16 + extra), h
            half = h % 4 // 2
            return slice(64 * half, 64 * half + NPROD * 8 + extra), h // 4 * 2 + h % 2

        KS = (KS8, KS8, KS8, KS16)
        V = (V8, V8, V8, V16)
        PAIRS = B // 2
        LAST = LOOPS = PAIRS - 1
        counts = dict(chain_counts)

        def wait_alone(eng):
            eng.nop(nofuse=True)

        class Chain:

            def __init__(self, name, eng, sem_):
                self.name, self.eng, self.sem = name, eng, sem_
                self.n, self.before, self.it = 0, 0, None

            def enter(self, it):
                self.before, self.n, self.it = self.n, 0, it
                self.total = counts.get(self.name, 1)

            def leave(self):
                chain_counts[self.name] = self.n
                self.n += self.before + (LOOPS - 1) * self.n
                self.it = None

            def done(self, ins):
                self.n += 1
                ins.then_inc(self.sem, 1)

            def wait(self):
                if self.it is None:
                    self.eng.wait_ge(self.sem, self.n)
                else:
                    self.eng.wait_ge(self.sem, self.it * self.total + (self.before + self.n))

            def link(self, ins, plain=False):
                self.done(ins)
                self.wait()
                if plain:
                    wait_alone(self.eng)

        def run_steps(steps, it, core, chain_of):
            for what, chains in steps:
                chains = [c_ for c_ in chains if it is not LAST or not c_[0].startswith("next")]

                def woven():
                    at = 0
                    for name, s in chains:
                        short = name.removeprefix("next ")
                        for hop in chain_of(short, s, it + 1 if short != name else it):
                            yield at + hop
                        at += TICKS[short]

                if what is None or (what[0] == "next" and it is LAST):
                    weave(iter(()), woven(), 1, 1)
                    continue
                p, s = what
                if steps is FIRST_STEPS:
                    body = core(s, 0, it, 0, 0, 0)
                elif p == "next":
                    body = core(s, 0, it + 1, *bases(it, 0, s))
                else:
                    body = core(s, p, it, *bases(it, p, s))
                q = 0 if p == "next" else p
                weave(body, woven(), len(core_order(q)), sum(TICKS[n.removeprefix("next ")] for n, _ in chains))

        def bases(it, p, s):
            return (it * MAX_TOTAL + (MAX_FIRST + MAX_START[p, s]), it * EXP_TOTAL + (EXP_FIRST + EXP_START[p, s]),
                    it * OUT_TOTAL + (OUT_FIRST + OUT_START[p, s]))

        def outs_kept(it, p, s):
            if (p, s) == (0, 0):
                return it * OUT_TOTAL + (GROUPS[0] + 2)
            return it * OUT_TOTAL + (OUT_FIRST + OUT_START[p, s] + GROUPS[p] + 2)

        def program(eng, chain, core, chain_of):
            run_steps(FIRST_STEPS, 0, core, chain_of)
            with eng.Fori(0, LOOPS) as it:
                if chain:
                    chain.enter(it)
                run_steps(STEPS, it, core, chain_of)
            if chain:
                chain.leave()
            run_steps(STEPS, LAST, core, chain_of)

        block = ctx.enter_context(nc.Block())

        NORMS = 8
        TURNED = 6
        TURN_OF = {0: 0, 1: 1, 2: 2, 3: 3, 4: 4, 5: 5, 7: 6}
        NT = len(TURN_OF)

        @block.sync
        def _(sp):
            sp.dma_start(col[:], columns).then_inc(const_in, 16)
            sp.dma_start(rows[:], rows_in.to_broadcast([P, R_TOTAL])).then_inc(const_in, 16)
            sp.dma_start(W[:, W_LOADS[0]:W_LOADS[1]], weights[:, W_LOADS[0]:W_LOADS[1]]).then_inc(w_in[0], 16)
            sp.dma_start(maskq8[:], maskq.rearrange("(t p) k -> p t k", p=P)).then_inc(const_in, 16)
            sp.dma_start(maskk8[:], maskk.rearrange("(t p) q -> p t q", p=P)).then_inc(const_in, 16)
            sp.dma_start(ebias[:], experts_bias).then_inc(const_in, 16)
            for i in range(1, len(W_LOADS) - 1):
                sp.dma_start(W[:, W_LOADS[i]:W_LOADS[i + 1]], weights[:, W_LOADS[i]:W_LOADS[i + 1]]).then_inc(w_in[i], 16)

            def load(s, it):
                sp.wait_ge(x_out[s], it * 16 + 16)
                sp.dma_start(X[s][:], x[bass.ds(it * 2 + s, 1)].rearrange("o (t p) d -> p (o t) d", p=P)).then_inc(x_in[s], 16)
                sp.dma_start(cT[s][:], ctxT[bass.ds(it * 2 + s, 1)].rearrange("o p t -> p (o t)")).then_inc(ctx_in[s], 16)

            def stack(s, p, it):
                width = S + KEYS[p]
                sp.wait_ge(split_done[s], it * 4 + (p + 1))
                sp.wait_ge(spread[s], it * 4 + (p + 1))
                sp.dma_start(bounce[s].rearrange("c p t -> p c t")[:, :, 0:width], parts[s][:, :, 0:width]).then_inc(bounce_in[s], 16)
                sp.wait_ge(bounce_in[s], it * 64 + 16 * (p + 1))
                back = bounce[s].rearrange("c (d h) t -> (c d) h t", h=HEADS[p])
                halves = 1 if p == 3 else 2
                for r in range(halves):
                    to = slice(64 * r, 64 * r + NPROD * HD[p])
                    sp.dma_start(QS[s][to], back[:, r::halves, 0:S]).then_inc(stack_in[s], 16)
                    sp.dma_start(KS[p][s][to, :, 0:KEYS[p]], back[:, r::halves, S:width]).then_inc(stack_in[s], 16)

            def core(s, p, it, max_base, exp_base, out_base):
                n = 0
                for b, (kind, g, *_) in enumerate(core_order(p)):
                    yield b
                    n += kind != "exp"
                    if kind != "turn":
                        continue
                    sp.wait_ge(max_used, max_base + (n + 2))
                    for r in range(1 if p == 3 else 2):
                        at, n_slots = (NPROD * 16, 4) if p == 3 else (64 * r + NPROD * 8, 2)
                        sp.dma_start(QS[s][at:at + MAX_ROWS, n_slots * g:n_slots * (g + 1), :],
                                     mrow[s][:, g, :].unsqueeze(1).to_broadcast([MAX_ROWS, n_slots, S])).then_inc(mrow_in[s], 16)

            def chain_of(name, s, it):
                if name == "load":
                    yield 0
                    load(s, it)
                elif name == "end":
                    yield 35
                    sp.wait_ge(x_updated[s], it * 5 + 5)
                    sp.dma_start(out[bass.ds(it * 2 + s, 1)].rearrange("o (t p) d -> p (o t) d", p=P), X[s][:]).then_inc(x_out[s], 16)
                else:
                    yield TICKS[name] - 3
                    stack(s, int(name[2:]), it)

            program(sp, None, core, chain_of)
            for s in range(2):
                sp.wait_ge(x_out[s], PAIRS * 16 + 16)

        @block.gpsimd
        def _(pool):
            chain = Chain("pool", pool, pool_step)

            def select(out_, op, fill, pattern, mult):
                chain.link(nc.gpsimd.affine_select(out=out_, in_=out_, compare_op=op, fill=fill, base=0,
                                                   pattern=pattern, channel_multiplier=mult))

            def select_box(out_, pattern, base):
                chain.link(nc.gpsimd.affine_select(out=out_, in_=out_, compare_op=ALU.is_ge, fill=0.0, base=base,
                                                   pattern=pattern, channel_multiplier=1))
                chain.link(nc.gpsimd.affine_select(out=out_, in_=out_, compare_op=ALU.is_gt, fill=0.0, base=PARTS - base,
                                                   pattern=[[-a_, n_] for a_, n_ in pattern], channel_multiplier=-1))

            for t, v in ((ident, 0.0), (identb, 0.0), (tri, 1.0), (head_of, 0.0), (first, 1.0),
                         (winq_add, 0.0), (wink_add, 0.0), (zero, 0.0), (ones_col, 1.0)):
                chain.done(nc.gpsimd.memset(t[:], v))
            chain.done(nc.gpsimd.memset(half[:, 0:TQ], -0.5))
            chain.link(nc.gpsimd.memset(half[:, TQ:2 * TQ], 0.5))
            select(ident[:], ALU.not_equal, 1.0, [[-1, P]], 1)
            select(identb[:], ALU.not_equal, 1.0, [[-1, P]], 1)
            select(tri[:], ALU.is_ge, 0.0, [[1, P]], -1)
            select(head_of[:].rearrange("p a (g r j) -> p a g r j", g=4, r=2), ALU.not_equal, 1.0,
                   [[-16, 8], [-4, 4], [-1, 2], [-2, 2]], 1)
            select(first[:], ALU.is_gt, 0.0, [[1, NE], [-1, NE]], 0)
            for i, sign in ((0, -1), (1, 1), (2, -1)):
                select(winq_add[:, i, :], ALU.is_ge, NEG_MAX, [[sign, P]], -sign)
            for i, sign in ((0, 1), (1, -1)):
                select(wink_add[:, i, :], ALU.is_ge, NEG_MAX, [[sign, P]], -sign)
            chain.link(nc.gpsimd.memset(KS8[0][:], 1.0))
            for t, v in ((KS8[1], 1.0), (KS16[0], 1.0), (KS16[1], 1.0), (V8[0], 0.0), (V8[1], 0.0), (V16[0], 0.0), (V16[1], 0.0)):
                chain.link(nc.gpsimd.memset(t[:], v))
            for s in range(2):
                for r in range(2):
                    ks = KS8[s][64 * r:64 * r + 64].rearrange("p (g j) t -> p g j t", j=2)
                    at = NPROD * 8 + 2 * PARTS * r
                    select_box(ks, [[0, 4], [-PARTS, 2], [0, SK]], -at)
                select_box(KS16[s][:].rearrange("p (g j) t -> p g j t", j=4), [[0, 2], [-PARTS, 4], [0, SK]], -NPROD * 16)
            for s in range(2):
                nc.gpsimd.memset(V8[s][:, :, :, 8:9], 1.0)
                nc.gpsimd.memset(V16[s][:, :, :, 16:17], 1.0).then_inc(pool_const, 1)
            for s in range(2):
                nc.gpsimd.memset(X[s][:], 0.0).then_inc(x_out[s], 16)

            def root(s, it, k):
                pool.wait_ge(ln_stats[s], it * NORMS + k + 1)
                wait_alone(pool)
                chain.link(nc.gpsimd.tensor_scalar(var[:], mv[:, :, 1], LN_EPS, None, ALU.add))
                nc.gpsimd.tensor_tensor(rstd[:], var[:], half[:, 0:TQ], ALU.pow).then_inc(ln_rstd[s], 1)

            def rms_of(s, it, k):
                pool.wait_ge(rms_sum[s], it * 2 + k + 1)
                wait_alone(pool)
                chain.link(nc.gpsimd.tensor_scalar(var[:], ssum[:], 1.0 / (D, FF)[k], None, ALU.mult))
                chain.link(nc.gpsimd.tensor_tensor(rms[:], var[:], half[:, TQ:2 * TQ], ALU.pow), plain=True)
                nc.gpsimd.tensor_scalar(rms[:], rms[:], RMS_EPS, None, ALU.add).then_inc(rms_root[s], 1)

            def core(s, p, it, max_base, exp_base, out_base):
                yield from range(len(core_order(p)))

            def chain_of(name, s, it):
                for hop, f, k in {"load": (), "to0": ((1, root, 0),), "to1": ((7, root, 1),), "to2": ((7, root, 2), (27, root, 3)),
                                  "to3": ((7, root, 4),),
                                  "end": ((6, root, 5), (14, root, 6), (17, root, 7), (20, rms_of, 0), (32, rms_of, 1))}[name]:
                    yield hop
                    f(s, it, k)

            program(pool, chain, core, chain_of)

        @block.tensor
        def _(pe):
            pe.wait_ge(pool_const, 2)
            pe.wait_ge(act_const, 2)
            nc.tensor.matmul(side[:, 0, 0:2], ones_col[:], absum[:], start=True, stop=True).then_inc(pe_const, 1)
            for q in w_in:
                pe.wait_ge(q, 16)
            pe.wait_ge(dve_const, 1)

            def turn(s, it, k, src):
                pe.wait_ge(ln_rows[s], it * NT + (TURN_OF[k] + 1))
                for t in range(TQ):
                    ins = nc.tensor.transpose(side[:, 0, t * P:(t + 1) * P], src[:, t, :], ident[:])
                ins.then_inc(ln_turned[s], 1)

            def project(s, it, p):
                pe.wait_ge(hT_ready[s], it * NT + (TURN_OF[(0, 1, 3, 4)[p]] + 1))
                nc.tensor.matmul(side[:, 0, 0:S], w(f"q{p}"), hT[:], start=True, stop=True)
                if KEYS[p] == SK:
                    pe.wait_ge(ctx_in[s], it * 16 + 16)
                    ins = nc.tensor.matmul(side[:, 1, :], w(f"k{p}"), cT[s][:], start=True, stop=True)
                else:
                    ins = nc.tensor.matmul(side[:, 0, S:2 * S], w(f"k{p}"), hT[:], start=True, stop=True)
                ins.then_inc(proj_done[s], 1)

            def project_v(s, it, p):
                if KEYS[p] == SK:
                    pe.wait_ge(xs_act[s], it * 4 + (p + 1))
                    src, vb = cT[s], side[:, 0, :]
                else:
                    src, vb = hT, side[:, 1, :]
                for t in range(KEYS[p] // P):
                    ins = nc.tensor.matmul(vb[:, t * D:(t + 1) * D], src[:, t * P:(t + 1) * P], w(f"v{p}"), start=True, stop=True)
                ins.then_inc(proj_done[s], 1)

            def core(s, p, it, max_base, exp_base, out_base):
                ks, v = KS[p][s], V[p][s]
                n1, n2 = MAX_UNITS[p] + 1, EXP_UNITS[p]
                at_zero = isinstance(exp_base, int) and exp_base == 0
                pending = []

                def av(g, i):
                    u = g * n2 + i
                    pe.wait_ge(probs_ready, exp_base + (u + 1))
                    if i == 0:
                        pe.wait_ge(out_kept, out_base + (g + 1))
                    pr = probs[:, u % 4, :]
                    bank = ob[:, g % 2, :]
                    if p == 0:
                        for t in range(TQ):
                            for j in (2 * i, 2 * i + 1):
                                at = ((j % 2) * TQ + t) * P
                                nc.tensor.matmul(bank[32 * j:32 * j + 32, t * P:(t + 1) * P], v[:, t, 4 * g + j, :], pr[:, at:at + P],
                                                 start=True, stop=(t == 0), skip_group_check=True)
                        for j in (2 * i, 2 * i + 1):
                            ins = nc.tensor.matmul(bank[32 * j:32 * j + 32, P:2 * P], KV[s][:, 4 * g + j, :], xs[s][:, P:2 * P],
                                                   start=False, stop=True, skip_group_check=True)
                    elif p == 2:
                        kt = i // 2
                        n = (S, P)[kt]
                        for j in (2 * (i % 2), 2 * (i % 2) + 1):
                            ins = nc.tensor.matmul(bank[32 * j:32 * j + 32, S - n:S], v[:, kt, 4 * g + j, :], pr[:, (j % 2) * n:(j % 2 + 1) * n],
                                                   start=(kt == 0), stop=(kt == 1), skip_group_check=True)
                    else:
                        kt = i // 2
                        for j in (2 * (i % 2), 2 * (i % 2) + 1):
                            ins = nc.tensor.matmul(bank[32 * j:32 * j + 32, 0:S], v[:, kt, 4 * g + j, :], pr[:, (j % 2) * S:(j % 2 + 1) * S],
                                                   start=(kt == 0), stop=(kt == TK - 1))
                    ins.then_inc(av_done, 1)

                n_max = 0
                for b, blk in enumerate(core_order(p)):
                    yield b
                    if b == 0:
                        pe.wait_ge(stack_in[s], it * STACK_TOTAL + STACK_UPTO[p])
                        pe.wait_ge(v_ready[s], it * 4 + (p + 1))
                        if p == 0:
                            pe.wait_ge(kv_ready[s], it + 1)
                    if blk[0] == "max":
                        _, g, i = blk
                        pe.wait_ge(max_used, max_base + (n_max + 1))
                        bank = mb[:, n_max % 2, :]
                        if p == 2:
                            r, slot = stack_rows(p, 4 * g + i)
                            nc.tensor.matmul(bank[:, 0:P], QS[s][r, slot, 0:P], ks[r, slot, 0:P], start=True, stop=True)
                            ins = nc.tensor.matmul(bank[:, P:3 * P], QS[s][r, slot, P:2 * P], ks[r, slot, 0:S], start=True, stop=True)
                        else:
                            r, slot = stack_rows(p, 4 * g + i // 2)
                            t = i % 2
                            ins = nc.tensor.matmul(bank, QS[s][r, slot, t * P:(t + 1) * P], ks[r, slot, :], start=True, stop=True)
                        ins.then_inc(max_scores, 1)
                        n_max += 1
                    elif blk[0] == "turn":
                        _, g = blk
                        pe.wait_ge(nm_ready[s], it * GRP_TOTAL + (GRP_START[p] + g + 1))
                        pe.wait_ge(max_used, max_base + (n_max + 1))
                        dst = mb[:, n_max % 2, :].bitcast(BF16)
                        for t in range(TQ):
                            ins = nc.tensor.transpose(dst[0:MAX_ROWS, t * P:(t + 1) * P],
                                                      nm[s][:, t, 4 * g:4 * g + 4, :].rearrange("p h c -> p (h c)"), identb[:])
                        ins.then_inc(max_scores, 1)
                        n_max += 1
                    else:
                        _, g, i = blk
                        u = g * n2 + i
                        if n1 > 1 and i == 0:
                            pe.wait_ge(mrow_in[s], it * MROW_TOTAL + MROW_UPTO[p][g])
                        if not at_zero or u >= 2:
                            pe.wait_ge(probs_ready, exp_base + (u - 1))
                        bank = eb[:, u % 2, :]
                        if p == 0:
                            for j in (2 * i, 2 * i + 1):
                                r, slot = stack_rows(p, 4 * g + j)
                                for t in range(TQ):
                                    at = ((j % 2) * TQ + t) * P
                                    ins = nc.tensor.matmul(bank[:, at:at + P], ks[r, slot, t * P:(t + 1) * P], QS[s][r, slot, t * P:(t + 1) * P],
                                                           start=True, stop=True)
                        elif p == 2:
                            kt = i // 2
                            n = (S, P)[kt]
                            part = bank[:, 0:2 * n]
                            nc.tensor.matmul(part.rearrange("p (j q) -> p j q", j=2), identb[:],
                                             wink_add[:].rearrange("p a q -> p (a q)")[:, 0:n].unsqueeze(1).to_broadcast([P, 2, n]),
                                             start=True, stop=False, skip_group_check=True)
                            for j in (2 * (i % 2), 2 * (i % 2) + 1):
                                r, slot = stack_rows(p, 4 * g + j, MAX_ROWS)
                                ins = nc.tensor.matmul(part[:, (j % 2) * n:(j % 2 + 1) * n], ks[r, slot, kt * P:(kt + 1) * P], QS[s][r, slot, S - n:S],
                                                       start=False, stop=True, skip_group_check=True)
                        else:
                            kt = i // 2
                            if p == 1:
                                nc.tensor.matmul(bank.rearrange("p (j q) -> p j q", j=2), identb[:],
                                                 maskk_add[:, kt:kt + 1, :].to_broadcast([P, 2, S]), start=True, stop=False, skip_group_check=True)
                            for j in (2 * (i % 2), 2 * (i % 2) + 1):
                                r, slot = stack_rows(p, 4 * g + j, MAX_ROWS)
                                ins = nc.tensor.matmul(bank[:, (j % 2) * S:(j % 2 + 1) * S], ks[r, slot, kt * P:(kt + 1) * P], QS[s][r, slot, :],
                                                       start=(p == 3), stop=True, skip_group_check=(p == 1))
                        ins.then_inc(exp_scores, 1)
                        pending.append((g, i))
                        if len(pending) == 4:
                            av(*pending.pop(0))
                            av(*pending.pop(0))
                for unit in pending:
                    av(*unit)

            def take(s, it, p, at):
                k = (0, 1, 3, 4)[p]
                yield at + 3
                turn(s, it, k, qn[s] if p == 3 else hn)
                yield at + 5
                project(s, it, p)
                yield at + 7
                project_v(s, it, p)

            def finish(s, it, p):
                yield 0
                pe.wait_ge(out_kept, outs_kept(it, p, s))
                for t in range(TQ):
                    for g in range(GROUPS[p]):
                        ins = nc.tensor.transpose(side[:, t, g * P:(g + 1) * P], OT[s][:, g, t * P:(t + 1) * P], ident[:])
                ins.then_inc(o_turned[s], 1)
                yield 2
                pe.wait_ge(an_ready[s], it * 4 + (p + 1))
                for t in range(TQ):
                    ins = nc.tensor.transpose(side[:, 0, t * P:(t + 1) * P], An[:, t, :], ident[:])
                ins.then_inc(an_turned[s], 1)
                yield 4
                pe.wait_ge(at_ready[s], it * 4 + (p + 1))
                for t in range(TQ):
                    ins = nc.tensor.matmul(side[:, 1, t * D:(t + 1) * D], AT[:, t * P:(t + 1) * P], w(f"o{p}"), start=True, stop=True)
                ins.then_inc(o_proj[s], 1)

            def experts(s, it):
                yield 9
                turn(s, it, 2, hn)
                yield 11
                pe.wait_ge(hT_ready[s], it * NT + (TURN_OF[2] + 1))
                for t in range(TQ):
                    ins = nc.tensor.matmul(side[:, 1, t * NE:(t + 1) * NE], hT[:, t * P:(t + 1) * P], w("gate"), start=True, stop=True)
                ins.then_inc(gate_done[s], 1)
                yield 16
                pe.wait_ge(gate_ready[s], it + 1)
                for t in range(TQ):
                    ins = nc.tensor.transpose(side[0:NE, 0, t * P:(t + 1) * P], gate[:, t, :], ident[:])
                ins.then_inc(gateT_done[s], 1)
                yield 18
                pe.wait_ge(gateT_ready[s], it + 1)
                for t in range(TQ):
                    ins = nc.tensor.matmul(side[:, 0, t * D:(t + 1) * D], gateT[:, t * P:(t + 1) * P], ebias[:], start=True, stop=True)
                ins.then_inc(moe_bias[s], 1)
                for i in range(4):
                    t, half_ = i // 2, i % 2
                    if i:
                        yield 18 + 2 * i
                        pe.wait_ge(experts_used[s], it * 5 + i)
                    nc.tensor.matmul(side[:, (i + 1) % 2, :], hT[:, t * P:(t + 1) * P], w("experts", half_ * 512, 512),
                                     start=True, stop=True).then_inc(experts_done[s], 1)

            def hidden(s, it, name, k, n_th):
                pe.wait_ge(hT_ready[s], it * NT + (TURN_OF[k] + 1))
                for n in range(FC):
                    ins = nc.tensor.matmul(side[:, 1 - n // 2, (n % 2) * S:(n % 2 + 1) * S], w(name, n * P, P), hT[:], start=True, stop=True)
                ins.then_inc(ffn_h[s], 1)

            def out_of_hidden(s, it, name, n_th):
                pe.wait_ge(ffn_act[s], it * 2 + n_th)
                for t in range(TQ):
                    for n in range(FC):
                        ins = nc.tensor.matmul(side[:, 0, t * D:(t + 1) * D], f1[:, n, t * P:(t + 1) * P], w(name, n * D, D), start=(n == 0), stop=(n == FC - 1))
                ins.then_inc(ffn_y[s], 1)

            def after_the_chain_before(name, s, it):
                o = 1 - s
                if name == "to0":
                    if not isinstance(it, int):
                        pe.wait_ge(x_updated[s], it * 5)
                    elif s:
                        pe.wait_ge(kv_ready[o], 1)
                elif name == "end":
                    if s == 0:
                        pe.wait_ge(split_done[o], it * 4 + 4)
                    elif it is LAST:
                        pe.wait_ge(x_updated[o], it * 5 + 5)
                    else:
                        pe.wait_ge(kv_ready[o], it + 2)
                elif (name, s) == ("to1", 0):
                    pe.wait_ge(kv_ready[o], it + 1)
                else:
                    pe.wait_ge(split_done[o], it * 4 + (int(name[2:]) + s))

            def chain_of(name, s, it):
                if name != "load":
                    yield 0
                    after_the_chain_before(name, s, it)
                if name == "to0":
                    yield from take(s, it, 0, 0)
                    yield 9
                    pe.wait_ge(xs_ready[s], it + 1)
                    nc.tensor.transpose(side[:, 0, 0:P], xs[s][:, S:S + P], ident[:]).then_inc(k_turned[s], 1)
                    yield 12
                    pe.wait_ge(kTM_ready[s], it + 1)
                    pe.wait_ge(v_ready[s], it * 4 + 1)
                    nc.tensor.matmul(side[:, 1, :], kTM[:], V8[s][:, 0, :, :].rearrange("p h e -> p (h e)"), start=True, stop=True).then_inc(kv_done[s], 1)
                elif name == "to1":
                    yield from finish(s, it, 0)
                    yield from take(s, it, 1, 6)
                elif name == "to2":
                    yield from finish(s, it, 1)
                    yield from experts(s, it)
                    yield from take(s, it, 2, 26)
                elif name == "to3":
                    yield from finish(s, it, 2)
                    yield from take(s, it, 3, 6)
                elif name == "end":
                    yield from finish(s, it, 3)
                    yield 8
                    turn(s, it, 5, qn[s])
                    yield 10
                    hidden(s, it, "ffn1", 5, 1)
                    yield 12
                    out_of_hidden(s, it, "ffn2", 1)
                    yield 22
                    turn(s, it, 7, hn)
                    yield 24
                    hidden(s, it, "up", 7, 2)
                    yield 26
                    out_of_hidden(s, it, "down", 2)
                    yield 29
                    pe.wait_ge(sq_ready[s], it + 1)
                    for t in range(TQ):
                        for n in range(FC):
                            ins = nc.tensor.matmul(side[:, 1, t:t + 1], sq[:, n, t * P:(t + 1) * P], ones_col[:, 0:1], start=(n == 0), stop=(n == FC - 1))
                    ins.then_inc(sq_sum[s], 1)

            program(pe, None, core, chain_of)

        @block.scalar
        def _(act):
            act.wait_ge(const_in, 5 * 16)
            nc.scalar.activation(keep[:], row("lambda"), ACT.Exp, scale=1.0).then_inc(act_const, 1)
            act.wait_ge(pool_const, 2)
            act.wait_ge(w_in[3], 16)
            for i in range(2):
                ins = nc.scalar.activation(wtmp[:, i, :], w(("up", "down")[i]), ACT.Abs, accum_out=absum[:, i:i + 1])
            ins.then_inc(act_const, 1)
            act.wait_ge(dve_const, 1)

            def turned(s, it, k):
                act.wait_ge(ln_turned[s], it * NT + (TURN_OF[k] + 1))
                nc.scalar.copy(hT[:], side[:, 0, 0:S]).then_inc(hT_ready[s], 1)

            def first_parts(s, p):
                n = S + KEYS[p]
                nc.scalar.copy(parts[s][:, 0, 0:n], xs[s][:, 0:n]).then_inc(first_part[s], 1)
                nc.scalar.copy(parts[s][:, 3:6:2, 0:S], xs[s][:, 0:S].unsqueeze(1).to_broadcast([P, 2, S]))
                nc.scalar.copy(parts[s][:, 2:5:2, S:n], xs[s][:, S:n].unsqueeze(1).to_broadcast([P, 2, KEYS[p]])).then_inc(spread[s], 1)

            def take(s, it, p, at):
                yield at + 4
                turned(s, it, (0, 1, 3, 4)[p])
                yield at + 6
                act.wait_ge(proj_done[s], it * 8 + (2 * p + 1))
                if p == 0:
                    nc.scalar.activation(rs[:, 0:S], side[:, 0, 0:S], ACT.Identity, bias=c("q0"))
                    nc.scalar.activation(rs[:, S:2 * S], side[:, 0, S:2 * S], ACT.Identity, bias=c("k0")).then_inc(qk_raw[s], 1)
                    act.wait_ge(qk_raw[s], it + 1)
                    nc.scalar.activation(es[:], rs[:], ACT.Exp).then_inc(xs_act[s], 1)
                    yield at + 10
                    act.wait_ge(k_turned[s], it + 1)
                    nc.scalar.copy(kTM[:], side[:, 0, 0:P]).then_inc(kTM_ready[s], 1)
                    act.wait_ge(xs_ready[s], it + 1)
                    first_parts(s, 0)
                    return
                cq, ck = (c("zero"), c("zero")) if p == 3 else (c(f"q{p}"), c(f"k{p}"))
                kb = side[:, 1, :] if KEYS[p] == SK else side[:, 0, S:2 * S]
                nc.scalar.activation(xs[s][:, 0:S], side[:, 0, 0:S], ACT.Identity, bias=cq)
                nc.scalar.activation(xs[s][:, S:S + KEYS[p]], kb, ACT.Identity, bias=ck).then_inc(xs_act[s], 1)
                act.wait_ge(xs_act[s], it * 4 + (p + 1))
                first_parts(s, p)

            def core(s, p, it, max_base, exp_base, out_base):
                n2 = EXP_UNITS[p]
                at_zero = isinstance(exp_base, int) and exp_base == 0

                def keep_outputs(g):
                    act.wait_ge(av_done, exp_base + (g + 1) * n2)
                    nc.scalar.copy(OT[s][:, g, :], ob[:, g % 2, 0:S]).then_inc(out_kept, 1)

                for b, (kind, g, *rest_) in enumerate(core_order(p)):
                    yield b
                    if kind != "exp":
                        continue
                    i, = rest_
                    u = g * n2 + i
                    if p:
                        act.wait_ge(exp_scores, exp_base + (u + 1))
                        if not at_zero or u >= 4:
                            act.wait_ge(av_done, exp_base + (u - 3))
                        n = 2 * P if p == 2 and i >= 2 else FF
                        nc.scalar.activation(probs[:, u % 4, 0:n], eb[:, u % 2, 0:n], ACT.Exp, scale=SCALE[p]).then_inc(probs_ready, 1)
                        if g and i == KEEP_AFTER[p]:
                            keep_outputs(g - 1)
                    elif g > 1 and i == n2 - 1:
                        keep_outputs(g - 2)
                if p:
                    keep_outputs(GROUPS[p] - 1)
                else:
                    keep_outputs(GROUPS[p] - 2)
                    keep_outputs(GROUPS[p] - 1)

            def finish(s, it, p):
                yield 3
                act.wait_ge(an_turned[s], it * 4 + (p + 1))
                nc.scalar.copy(AT[:], side[:, 0, 0:S]).then_inc(at_ready[s], 1)

            def chain_of(name, s, it):
                if name == "to0":
                    yield from take(s, it, 0, 0)
                elif name == "to1":
                    yield from finish(s, it, 0)
                    yield from take(s, it, 1, 6)
                elif name == "to2":
                    yield from finish(s, it, 1)
                    yield 10
                    turned(s, it, 2)
                    yield 13
                    act.wait_ge(gexp_in[s], it + 1)
                    for t in range(TQ):
                        ins = nc.scalar.activation(gp[:, t, :], gl[:, t, :], ACT.Exp, bias=gm[:, t:t + 1], accum_out=gsum[:, t:t + 1])
                    ins.then_inc(gexp_out[s], 1)
                    yield 17
                    act.wait_ge(gateT_done[s], it + 1)
                    nc.scalar.copy(gateT[:], side[0:NE, 0, 0:S]).then_inc(gateT_ready[s], 1)
                    yield from take(s, it, 2, 26)
                elif name == "to3":
                    yield from finish(s, it, 2)
                    yield from take(s, it, 3, 6)
                elif name == "end":
                    yield from finish(s, it, 3)
                    yield 9
                    turned(s, it, 5)
                    yield 11
                    act.wait_ge(ffn_h[s], it * 2 + 1)
                    for n in range(FC):
                        ins = nc.scalar.activation(f1[:, n, :], side[:, 1 - n // 2, (n % 2) * S:(n % 2 + 1) * S], ACT.Relu, bias=c("ffn1", n))
                    ins.then_inc(ffn_act[s], 1)
                    yield 23
                    turned(s, it, 7)
                    yield 25
                    act.wait_ge(ffn_h[s], it * 2 + 2)
                    for n in range(0, FC, 2):
                        ins = nc.scalar.activation(f1[:, n:n + 2, :].rearrange("p a t -> p (a t)"), side[:, 1 - n // 2, :], ACT.Gelu)
                    ins.then_inc(ffn_act[s], 1)
                    yield 27
                    act.wait_ge(ffn_act[s], it * 2 + 2)
                    nc.scalar.activation(sq[:], f1[:], ACT.Square).then_inc(sq_ready[s], 1)

            program(act, None, core, chain_of)

        @block.vector
        def _(dve):
            chain = Chain("dve", dve, dve_step)
            link, done = chain.link, chain.done
            V_ = nc.vector
            dve.wait_ge(pool_const, 2)
            dve.wait_ge(const_in, 5 * 16)
            V_.tensor_scalar(maskq_add[:], maskq8[:], NEG_MAX, None, ALU.mult)
            V_.tensor_scalar(maskk_add[:], maskk8[:], NEG_EXP, None, ALU.mult)
            V_.tensor_reduce(own[:], head_of[:].rearrange("p a h -> p h a"), AX.X, ALU.add)
            dve.wait_ge(act_const, 1)
            link(V_.tensor_scalar(keep[:], keep[:], 1.0, None, ALU.add))
            link(V_.reciprocal(keep[:], keep[:]))
            dve.wait_ge(act_const, 2)
            dve.wait_ge(pe_const, 1)
            link(V_.tensor_scalar(alpha[:], side[:, 0, 0:2], 0.5 / (D * FF), None, ALU.mult))
            for i, n in enumerate(("up", "down")):
                link(V_.tensor_scalar(wtmp[:, i, :], w(n), alpha[:, i:i + 1], None, ALU.is_gt))
                link(V_.tensor_scalar(sq[:, 0:2, :].rearrange("p a t -> p (a t)"), w(n), -1.0, alpha[:, i:i + 1], ALU.mult, ALU.is_gt))
                link(V_.tensor_tensor(wtmp[:, i, :], wtmp[:, i, :], sq[:, 0:2, :].rearrange("p a t -> p (a t)"), ALU.subtract))
                link(V_.tensor_tensor(wtmp[:, i, :], wtmp[:, i, :], w(n), ALU.subtract))
                link(V_.tensor_tensor(w(n), w(n), wtmp[:, i, :], ALU.add))
            V_.memset(junk32[:], 0.0).then_inc(dve_const, 1)
            for i in range(2):
                V_.memset(junk[:, 0, i:i + 1], 0.0).then_inc(max_used, 1)
                V_.memset(junk[:, 1, i:i + 1], 0.0).then_inc(out_kept, 1)

            def norm(s, it, k, src, dst, at):
                for t in range(TQ):
                    ins = V_.bn_stats(stats[:, t, :], src[:, t, :])
                link(ins, plain=True)
                for t in range(TQ):
                    ins = V_.bn_aggr(mv[:, t, :], stats[:, t, :])
                ins.then_inc(ln_stats[s], 1)
                yield at + 2
                dve.wait_ge(ln_rstd[s], it * NORMS + (k + 1))
                for t in range(TQ):
                    ins = V_.tensor_scalar(dst[:, t, :], src[:, t, :], mv[:, t, 0:1], rstd[:, t:t + 1], ALU.subtract, ALU.mult)
                norm_last.append(ins)

            norm_last = []

            def take(s, it, p, at):
                keys, heads, hd = KEYS[p], HEADS[p], HD[p]
                tk = keys // P
                yield at
                if p == 0:
                    dve.wait_ge(x_in[s], it * 16 + 16)
                elif p != 2:
                    dve.wait_ge(x_updated[s], it * 5 + (1, None, 3)[p - 1])
                yield from norm(s, it, (0, 1, 3, 4)[p], X[s], qn[s] if p == 3 else hn, at)
                norm_last.pop().then_inc(ln_rows[s], 1)
                if p == 0:
                    yield at + 8
                    dve.wait_ge(xs_act[s], it * 4 + 1)
                    link(V_.tensor_scalar(rs[:], rs[:], 0.0, None, ALU.max))
                    V_.scalar_tensor_tensor(xs[s][:, 0:2 * S], es[:], 1.0, rs[:], ALU.min, ALU.add).then_inc(xs_ready[s], 1)
                yield at + (11 if p == 0 else 8)
                dve.wait_ge(proj_done[s], it * 8 + (2 * p + 2))
                vb = side[:, 0 if keys == SK else 1, 0:tk * D].rearrange("p (t h d) -> p (t h) d", t=tk, h=heads)
                dst = V[p][s][:, 0:tk, :, 0:hd].rearrange("p t h d -> p (t h) d")
                if p == 3:
                    V_.tensor_copy(dst, vb).then_inc(v_ready[s], 1)
                else:
                    bias = row(f"v{p}").rearrange("p (h d) -> p h d", h=heads)
                    for t in range(tk):
                        ins = V_.tensor_tensor(dst[:, t * heads:(t + 1) * heads, :], vb[:, t * heads:(t + 1) * heads, :], bias, ALU.add)
                    ins.then_inc(v_ready[s], 1)
                yield at + (13 if p == 0 else 10)
                n = S + keys
                dve.wait_ge(first_part[s], it * 4 + (p + 1))
                link(V_.tensor_tensor(rest[:, 0:n], xs[s][:, 0:n], parts[s][:, 0, 0:n], ALU.subtract))
                link(V_.tensor_copy(parts[s][:, 1, 0:n], rest[:, 0:n]))
                V_.tensor_tensor(parts[s][:, 2, 0:S], rest[:, 0:S], parts[s][:, 1, 0:S], ALU.subtract)
                V_.tensor_tensor(parts[s][:, 3, S:n], rest[:, S:n], parts[s][:, 1, S:n], ALU.subtract)
                V_.tensor_copy(parts[s][:, 4, 0:S], parts[s][:, 1, 0:S])
                V_.tensor_copy(parts[s][:, 5, S:n], parts[s][:, 1, S:n]).then_inc(split_done[s], 1)
                if p == 0:
                    dve.wait_ge(kv_done[s], it + 1)
                    V_.tensor_tensor(KV[s][:], side[:, 1, :].rearrange("p (h e) -> p h e", h=16),
                                     own[:].unsqueeze(2).to_broadcast([P, 16, VW]), ALU.mult).then_inc(kv_ready[s], 1)

            def core(s, p, it, max_base, exp_base, out_base):
                n2 = EXP_UNITS[p]
                at_zero = isinstance(exp_base, int) and exp_base == 0
                n_max = 0
                for b, blk in enumerate(core_order(p)):
                    yield b
                    if p == 0:
                        _, g, i = blk
                        u = g * n2 + i
                        dve.wait_ge(exp_scores, exp_base + (u + 1))
                        if not at_zero or u >= 4:
                            dve.wait_ge(av_done, exp_base + (u - 3))
                        V_.tensor_tensor(probs[:, u % 4, :].rearrange("p (j q) -> p j q", j=4), eb[:, u % 2, :].rearrange("p (j q) -> p j q", j=4),
                                         tri[:].unsqueeze(1).to_broadcast([P, 4, P]), ALU.mult).then_inc(probs_ready, 1)
                    elif blk[0] == "max":
                        _, g, i = blk
                        dve.wait_ge(max_scores, max_base + (n_max + 1))
                        wait_alone(dve)
                        bank = mb[:, n_max % 2, :]
                        if p == 1:
                            h, t = 4 * g + i // 2, i % 2
                            ins = V_.tensor_tensor_reduce(junk[:, n_max % 2, :], bank, maskq_add[:, t, :], 1.0, NEG_EXP, ALU.add, ALU.max, mx[s][:, t, h:h + 1])
                        elif p == 2:
                            h = 4 * g + i
                            V_.tensor_tensor_reduce(junk[:, n_max % 2, 0:P], bank[:, 0:P], winq_add[:, 0, :], 1.0, NEG_EXP, ALU.add, ALU.max, mx[s][:, 0, h:h + 1])
                            ins = V_.tensor_tensor_reduce(junk[:, n_max % 2, P:3 * P], bank[:, P:3 * P], winq_add[:, 1:3, :].rearrange("p a k -> p (a k)"), 1.0, NEG_EXP,
                                                          ALU.add, ALU.max, mx[s][:, 1, h:h + 1])
                        else:
                            h, t = 4 * g + i // 2, i % 2
                            ins = V_.tensor_reduce(mx[s][:, t, h:h + 1], bank, AX.X, ALU.max)
                        ins.then_inc(max_used, 1)
                        n_max += 1
                        if i == MAX_UNITS[p] - 1:
                            dve.wait_ge(max_used, max_base + (n_max + 2))
                            m = mx[s][:, :, 4 * g:4 * g + 4]
                            r = nmr[s][:, :, 4 * g:4 * g + 4]
                            n = [nm[s][:, :, 4 * g:4 * g + 4, a] for a in range(PARTS)]
                            V_.tensor_scalar(n[0], m, -1.0, None, ALU.mult)
                            link(V_.tensor_scalar(r, m, -1.0, None, ALU.mult))
                            link(V_.tensor_tensor(r, r, n[0], ALU.subtract))
                            link(V_.tensor_copy(n[1], r))
                            V_.tensor_tensor(n[2], r, n[1], ALU.subtract).then_inc(nm_ready[s], 1)
                    elif blk[0] == "turn":
                        _, g = blk
                        dve.wait_ge(max_scores, max_base + (n_max + 1))
                        V_.tensor_copy(mrow[s][:, g, :], mb[:, n_max % 2, :].bitcast(BF16)[0:MAX_ROWS, 0:S]).then_inc(max_used, 1)
                        n_max += 1

            def finish(s, it, p):
                heads, hd = HEADS[p], HD[p]
                yield 1
                dve.wait_ge(o_turned[s], it * 4 + (p + 1))
                n = GROUPS[p] * 4
                o = side[:, :, 0:n * VW].rearrange("p t (h e) -> p t h e", h=n)
                r = rden[:, 0:TQ * n].rearrange("p (t h) -> p t h", t=TQ)
                if p == 0:
                    link(V_.tensor_scalar(r, o[:, :, :, hd], DEN_EPS, None, ALU.add))
                    link(V_.reciprocal(r, r))
                else:
                    link(V_.reciprocal(r, o[:, :, :, hd]))
                if p == 3:
                    link(V_.tensor_scalar(r, r, keep[:], None, ALU.mult))
                for t in range(TQ):
                    ins = V_.tensor_tensor(An[:, t, :].rearrange("p (h d) -> p h d", h=heads), o[:, t, :, 0:hd],
                                           r[:, t, :].unsqueeze(2).to_broadcast([P, n, hd]), ALU.mult)
                ins.then_inc(an_ready[s], 1)
                yield 5
                dve.wait_ge(o_proj[s], it * 4 + (p + 1))
                y = side[:, 1, 0:S].rearrange("p (t d) -> p t d", t=TQ)
                if p < 3:
                    link(V_.tensor_tensor(X[s][:], X[s][:], y, ALU.add))
                    V_.tensor_tensor(X[s][:], X[s][:], row(f"o{p}").unsqueeze(1).to_broadcast([P, TQ, D]), ALU.add).then_inc(x_updated[s], 1)
                else:
                    link(V_.tensor_tensor(acc[:], qn[s][:], y, ALU.add))

            def affine(dst, g, b):
                link(V_.tensor_tensor(dst, dst, row(g).unsqueeze(1).to_broadcast([P, TQ, D]), ALU.mult))
                return V_.tensor_tensor(dst, dst, row(b).unsqueeze(1).to_broadcast([P, TQ, D]), ALU.add)

            def experts(s, it):
                yield 6
                dve.wait_ge(x_updated[s], it * 5 + 2)
                yield from norm(s, it, 2, X[s], hn, 6)
                norm_last.pop().then_inc(ln_rows[s], 1)
                yield 12
                dve.wait_ge(gate_done[s], it + 1)
                link(V_.tensor_tensor(gl[:], side[:, 1, 0:TQ * NE].rearrange("p (t e) -> p t e", t=TQ),
                                      row("gate").unsqueeze(1).to_broadcast([P, TQ, NE]), ALU.add))
                V_.tensor_reduce(gm[:], gl[:], AX.X, ALU.max, negate=True).then_inc(gexp_in[s], 1)
                yield 14
                dve.wait_ge(gexp_out[s], it + 1)
                link(V_.reciprocal(grec[:], gsum[:]))
                link(V_.tensor_tensor(gp[:], gp[:], grec[:].unsqueeze(2).to_broadcast([P, TQ, NE]), ALU.mult))
                flat = gp[:].rearrange("p t e -> p (t e)")
                for t in range(TQ):
                    pj = gp[:, t:t + 1, :].to_broadcast([P, NE, NE])
                    pe_ = gp[:, t, :].unsqueeze(2).to_broadcast([P, NE, NE])
                    sl = slice(t * NE, (t + 1) * NE)
                    V_.tensor_tensor(cmp_gt[:, sl, :], pj, pe_, ALU.is_gt)
                    ins = V_.tensor_tensor(cmp_eq[:, sl, :], pj, pe_, ALU.is_equal)
                link(ins)
                eq = cmp_eq[:].rearrange("p (t e) j -> p t e j", t=TQ)
                link(V_.tensor_tensor(eq, eq, first[:].unsqueeze(1).to_broadcast([P, TQ, NE, NE]), ALU.mult))
                link(V_.tensor_tensor(cmp_gt[:], cmp_gt[:], cmp_eq[:], ALU.add))
                link(V_.tensor_reduce(rank[:].rearrange("p t e -> p (t e)"), cmp_gt[:], AX.X, ALU.add))
                link(V_.scalar_tensor_tensor(gate[:].rearrange("p t e -> p (t e)"), rank[:].rearrange("p t e -> p (t e)"), 2.0, flat, ALU.is_lt, ALU.mult))
                link(V_.tensor_reduce(gsum[:], gate[:], AX.X, ALU.add))
                link(V_.reciprocal(grec[:], gsum[:]))
                V_.tensor_tensor(gate[:], gate[:], grec[:].unsqueeze(2).to_broadcast([P, TQ, NE]), ALU.mult).then_inc(gate_ready[s], 1)
                yield 19
                dve.wait_ge(moe_bias[s], it + 1)
                V_.tensor_tensor(acc[:], X[s][:], side[:, 0, 0:S].rearrange("p (t d) -> p t d", t=TQ), ALU.add).then_inc(experts_used[s], 1)
                dve.wait_ge(experts_used[s], it * 5 + 1)
                for i in range(4):
                    t, half_ = i // 2, i % 2
                    if i:
                        yield 19 + 2 * i
                    dve.wait_ge(experts_done[s], it * 4 + (i + 1))
                    for e in range(4):
                        last = half_ == 1 and e == 3
                        ins = V_.scalar_tensor_tensor((X[s] if last else acc)[:, t, :], side[:, (i + 1) % 2, e * D:(e + 1) * D],
                                                      gate[:, t, half_ * 4 + e:half_ * 4 + e + 1], acc[:, t, :], ALU.mult, ALU.add)
                        if e < 3:
                            link(ins)
                    ins.then_inc(experts_used[s], 1)
                    dve.wait_ge(experts_used[s], it * 5 + (i + 2))

            def chain_of(name, s, it):
                if name == "to0":
                    yield from take(s, it, 0, 0)
                elif name == "to1":
                    yield from finish(s, it, 0)
                    yield from take(s, it, 1, 6)
                elif name == "to2":
                    yield from finish(s, it, 1)
                    yield from experts(s, it)
                    yield from take(s, it, 2, 26)
                elif name == "to3":
                    yield from finish(s, it, 2)
                    yield from take(s, it, 3, 6)
                elif name == "end":
                    yield from finish(s, it, 3)
                    yield from norm(s, it, 5, acc, qn[s], 5)
                    link(norm_last.pop())
                    affine(qn[s][:], "ln1_g", "ln1_b").then_inc(ln_rows[s], 1)
                    yield 13
                    dve.wait_ge(ffn_y[s], it * 2 + 1)
                    link(V_.tensor_tensor(acc[:], qn[s][:], side[:, 0, 0:S].rearrange("p (t d) -> p t d", t=TQ), ALU.add))
                    link(V_.tensor_tensor(acc[:], acc[:], row("ffn2").unsqueeze(1).to_broadcast([P, TQ, D]), ALU.add))
                    yield from norm(s, it, 6, acc, hn, 13)
                    link(norm_last.pop())
                    link(affine(hn[:], "ln2_g", "ln2_b"))
                    V_.tensor_tensor(X[s][:], X[s][:], hn[:], ALU.add).then_inc(x_updated[s], 1)
                    dve.wait_ge(x_updated[s], it * 5 + 4)
                    yield 16
                    yield from norm(s, it, 7, X[s], hn, 16)
                    link(norm_last.pop(), plain=True)
                    for t in range(TQ):
                        ins = V_.tensor_tensor_reduce(junk32[:, t, :], hn[:, t, :], hn[:, t, :], 1.0, 0.0, ALU.mult, ALU.add, ssum[:, t:t + 1])
                    ins.then_inc(rms_sum[s], 1)
                    yield 21
                    dve.wait_ge(rms_root[s], it * 2 + 1)
                    link(V_.reciprocal(irms[:], rms[:]))
                    for t in range(TQ):
                        ins = V_.tensor_scalar(hn[:, t, :], hn[:, t, :], irms[:, t:t + 1], None, ALU.mult)
                    ins.then_inc(ln_rows[s], 1)
                    yield 31
                    dve.wait_ge(sq_sum[s], it + 1)
                    V_.tensor_copy(ssum[:], side[:, 1, 0:TQ]).then_inc(rms_sum[s], 1)
                    yield 33
                    dve.wait_ge(rms_root[s], it * 2 + 2)
                    link(V_.reciprocal(irms[:], rms[:]))
                    for t in range(TQ):
                        ins = V_.scalar_tensor_tensor(X[s][:, t, :], side[:, 0, t * D:(t + 1) * D], irms[:, t:t + 1], X[s][:, t, :], ALU.mult, ALU.add)
                    ins.then_inc(x_updated[s], 1)

            program(dve, chain, core, chain_of)


GRP_START, MROW_UPTO, STACK_UPTO = [], [], []
GRP_TOTAL = MROW_TOTAL = STACK_TOTAL = 0
for _p in PHASES:
    _halves = 1 if _p == 3 else 2
    GRP_START.append(GRP_TOTAL)
    GRP_TOTAL += GROUPS[_p] if MAX_UNITS[_p] else 0
    MROW_UPTO.append([MROW_TOTAL + 16 * _halves * (_g + 1) for _g in range(GROUPS[_p] if MAX_UNITS[_p] else 0)])
    MROW_TOTAL += 16 * _halves * len(MROW_UPTO[-1])
    STACK_TOTAL += 16 * 2 * _halves
    STACK_UPTO.append(STACK_TOTAL)
chain_counts = {}


def in_order(w, heads):
    w = w.reshape(heads, D // heads, -1)
    if heads == 16:
        w = w.reshape(4, 2, 2, D // heads, -1).transpose(0, 2, 1, 3, 4).reshape(heads, D // heads, -1)
    return w.transpose(1, 0, 2).reshape(D, -1)


def kernel(**a):
    import concourse.bacc as bacc
    from concourse.bass_utils import run_bass_kernel_spmd

    a = {k: np.asarray(v) for k, v in a.items()}

    def turned(w, heads):
        return in_order(w, heads).T

    def chunks(w):
        return w.reshape(FC, P, D).transpose(1, 0, 2).reshape(P, FC * D)

    wi, bi = a["L1_attn_w_in"], a["L1_attn_b_in"]
    parts = {
        "q0": turned(a["L0_attn_Wq"], 16), "k0": turned(a["L0_attn_Wk"], 16), "v0": a["L0_attn_Wv"].T, "o0": a["L0_attn_Wo"].T,
        "q1": turned(a["L0_xattn_q_w"], 16), "k1": turned(a["L0_xattn_k_w"], 16), "v1": a["L0_xattn_v_w"].T, "o1": a["L0_xattn_o_w"].T,
        "gate": a["L0_ffn_Wg"], "experts": a["L0_ffn_We"].transpose(2, 0, 1).reshape(D, NE * D),
        "q2": turned(wi[0:D], 16), "k2": turned(wi[D:2 * D], 16), "v2": wi[2 * D:].T, "o2": a["L1_attn_w_out"].T,
        "q3": turned(a["L1_xattn_Wq"].T, 8), "k3": turned(a["L1_xattn_Wk"].T, 8), "v3": a["L1_xattn_Wv"], "o3": a["L1_xattn_Wo"],
        "ffn1": a["L1_xattn_ffn_w1"], "ffn2": chunks(a["L1_xattn_ffn_w2"]),
        "up": a["L1_ffn_w_up"].T, "down": chunks(a["L1_ffn_w_down"].T),
    }
    columns = {
        "q0": in_order(a["L0_attn_bq"], 16), "k0": in_order(a["L0_attn_bk"], 16),
        "q1": in_order(a["L0_xattn_q_b"], 16), "k1": in_order(a["L0_xattn_k_b"], 16),
        "q2": in_order(bi[0:D], 16), "k2": in_order(bi[D:2 * D], 16), "zero": np.zeros((D, 1), np.float32),
        "ffn1": a["L1_xattn_ffn_b1"].reshape(FC, P).T,
    }
    rows = {
        "v0": a["L0_attn_bv"], "o0": a["L0_attn_bo"], "v1": a["L0_xattn_v_b"], "o1": a["L0_xattn_o_b"],
        "v2": bi[2 * D:], "o2": a["L1_attn_b_out"], "ln1_g": a["L1_xattn_ln1_g"], "ln1_b": a["L1_xattn_ln1_b"],
        "ln2_g": a["L1_xattn_ln2_g"], "ln2_b": a["L1_xattn_ln2_b"], "ffn2": a["L1_xattn_ffn_b2"], "gate": a["L0_ffn_bg"],
        "lambda": a["L1_xattn_lambda_param"].reshape(1),
    }
    mask = a["mask_SxS2_bk1"]
    arrays = {
        "x": a["x"],
        "ctxT": a["ctx_1024"].transpose(0, 2, 1),
        "maskq": mask,
        "maskk": mask.T,
        "weights": np.concatenate([parts[n] for n in W_COLS], axis=1),
        "columns": np.concatenate([columns[n] for n in C_COLS], axis=1),
        "rows": np.concatenate([rows[n] for n in R_COLS]).reshape(1, R_TOTAL),
        "experts_bias": a["L0_ffn_be"],
    }
    arrays = {k: np.ascontiguousarray(v) for k, v in arrays.items()}

    def program():
        nc = bacc.Bacc("TRN2", target_bir_lowering=False, num_devices=1)
        args = [nc.dram_tensor(f"{k}_dram", v.shape, mybir.dt.from_np(v.dtype), kind="ExternalInput").ap() for k, v in arrays.items()]
        args.append(nc.dram_tensor("out_dram", (B, S, D), F32, kind="ExternalOutput").ap())
        decoder(nc, *args)
        return nc

    program()
    nc = program()
    r = run_bass_kernel_spmd(nc, [{f"{k}_dram": v for k, v in arrays.items()}], core_ids=[0])
    return r.results[0]["out_dram"]
```

```python
from contextlib import ExitStack

import numpy as np

import concourse.bass as bass
from concourse import mybir

F32 = mybir.dt.float32
BF16 = mybir.dt.bfloat16
U8 = mybir.dt.uint8
ALU = mybir.AluOpType
ACT = mybir.ActivationFunctionType
AX = mybir.AxisListType

P = 128
B, S, D, SK = 8, 256, 128, 512
TQ, TK = S // P, SK // P
NE, FF = 8, 512
FC = FF // P
PARTS = 3
Q_OF = (0, 1, 2, 0, 1, 0)
K_OF = (0, 1, 0, 2, 0, 1)
NPROD = len(Q_OF)
NEG_MAX = -1.0e30
NEG_EXP = -3.0e38
LN_EPS, DEN_EPS, RMS_EPS = 1e-5, 1e-6, 1e-8
VW = 32

HEADS = (16, 16, 16, 8)
HD = tuple(D // h for h in HEADS)
KEYS = (S, SK, S, SK)
GROUPS = tuple(h // 4 for h in HEADS)
SCALE = (1.0, 8 ** -0.5, 8 ** -0.5, 16 ** -0.5)
MAX_UNITS = (0, 8, 4, 8)
KEEP_AFTER = (0, 3, 2, 3)
EXP_UNITS = (2, 8, 4, 8)
PHASES = range(4)
MAX_AHEAD = (0, 2, 3, 2)
TURN_AFTER, TURN_BEFORE = 3, 5
PROBS, AHEAD = 8, 4
MAX_ROWS = 4 * PARTS

CUT = 2
FIRST_STEPS = (((("load", 0), ("load", 1), ("to0", 0), ("pause", 7), ("core", 0, 0, (0, 4)), ("to1", 0)),),)
STEPS = (
    ((("pause", 10), ("core", 1, 0, (0, CUT))), (("to0", 1),)),
    ((("core", 0, 1, (0, 4)),),),
    ((("core", 1, 0, (CUT, 4)),), (("to1", 1),)),
    ((("core", 1, 1, (0, 4)),), (("to2", 0),)),
    ((("core", 2, 0, (0, 4)),), (("to2", 1),)),
    ((("pause", 7), ("core", 2, 1, (0, 4))), (("to3", 0),)),
    ((("core", 3, 0, (0, 2)),), (("next load", 0), ("to3", 1))),
    ((("core", 3, 1, (0, 2)),), (("next load", 1), ("end", 0))),
    ((("next to0", 0), ("pause", 7), ("next core", 0, 0, (0, 4)), ("next to1", 0)), (("end", 1),)),
)
TICKS = {"load": 1, "to0": 17, "to1": 21, "to2": 42, "to3": 21, "end": 36}
CHAIN_TIME = {"load": 0.1, "to0": 14, "to1": 22, "to2": 45, "to3": 20, "end": 48}
CORE_TIME = (13, 60, 28, 35)
CORE_LATE = 2

W_COLS = {}
_at = 0
for _n, _w in (("q0", D), ("k0", D), ("v0", D), ("o0", D), ("q1", D), ("k1", D), ("v1", D), ("o1", D),
               ("gate", NE), ("experts", NE * D), ("q2", D), ("k2", D), ("v2", D), ("o2", D),
               ("q3", D), ("k3", D), ("v3", D), ("o3", D), ("ffn1", FF), ("ffn2", FF),
               ("up", FF), ("down", FF)):
    W_COLS[_n] = (_at, _at + _w)
    _at += _w
W_TOTAL = _at
W_LOADS = (0, W_COLS["q1"][0], W_COLS["q2"][0], W_COLS["up"][0], W_TOTAL)
C_COLS = {n: i for i, n in enumerate(("q0", "k0", "q1", "k1", "q2", "k2", "zero", "ffn1"))}
C_TOTAL = C_COLS["ffn1"] + FC
R_COLS = {}
_at = 0
for _n, _w in (("v0", D), ("o0", D), ("v1", D), ("o1", D), ("v2", D), ("o2", D), ("ln1_g", D),
               ("ln1_b", D), ("ln2_g", D), ("ln2_b", D), ("ffn2", D), ("gate", NE), ("lambda", 1)):
    R_COLS[_n] = (_at, _at + _w)
    _at += _w
R_TOTAL = _at


CORES = [i[1:] for step in STEPS for lane in step for i in lane if i[0].endswith("core")]


def unit_starts(units, all_at_once=False):
    at, found = 0, {}
    for p, s, groups in CORES:
        if all_at_once:
            found[p, s, groups] = found[p, s, (0, CUT)] if groups[0] else at
            at += 0 if groups[0] else GROUPS[p] * units[p]
        else:
            found[p, s, groups] = at - groups[0] * units[p]
            at += (groups[1] - groups[0]) * units[p]
    return found, at, GROUPS[0] * units[0]


MAX_START, MAX_TOTAL, MAX_FIRST = unit_starts([n + 1 if n else 0 for n in MAX_UNITS], True)
EXP_START, EXP_TOTAL, EXP_FIRST = unit_starts(EXP_UNITS)
OUT_START, OUT_TOTAL, OUT_FIRST = unit_starts((1, 1, 1, 1))
assert not (EXP_FIRST % PROBS or EXP_TOTAL % PROBS or OUT_FIRST % 2 or OUT_TOTAL % 2 or MAX_FIRST % 2 or MAX_TOTAL % 2)


def core_order(p):
    n1, n2, ng = MAX_UNITS[p], EXP_UNITS[p], GROUPS[p]
    exps = [("exp", g, i) for g in range(ng) for i in range(n2)]
    if not n1:
        return exps
    maxima = []
    for g in range(ng):
        maxima += [("max", g, i) for i in range(n1)]
        if g:
            maxima.insert(len(maxima) - n1 + TURN_AFTER, ("turn", g - 1))
    maxima.append(("turn", ng - 1))
    n = min(MAX_AHEAD[p], ng) * n1 + min(MAX_AHEAD[p], ng) - 1
    out, rest, room = maxima[:n], maxima[n:], (ng - 1) * n2 - TURN_BEFORE
    for u, block in enumerate(exps):
        out.append(block)
        at, to = (min(len(rest) * v // room, len(rest)) for v in (u, u + 1))
        out += rest[at:to]
    return out


def core_blocks(p, groups):
    order = core_order(p)
    lo, hi = (order.index(("exp", g, 0)) if 0 < g < GROUPS[p] else (0, len(order))[g > 0] for g in groups)
    return order[lo:hi], sum(b[0] != "exp" for b in order[:lo])


def weave(lanes):
    at = [next(lane, None) for lane in lanes]
    while any(t is not None for t in at):
        i = min((t, i) for i, t in enumerate(at) if t is not None)[1]
        at[i] = next(lanes[i], None)


def decoder(nc, x, ctxT, maskq, maskk, weights, columns, rows_in, experts_bias, out):
    with ExitStack() as ctx:
        def sb(name, shape, dt=F32):
            return ctx.enter_context(nc.sbuf_tensor(name, shape, dt))

        def psum(name, shape, dt=F32):
            return ctx.enter_context(nc.psum_tensor(name, shape, dt))

        def sem(name):
            return ctx.enter_context(nc.semaphore(name))

        def pair(name):
            return [sem(f"{name}_{s}") for s in range(2)]

        W = sb("W", [P, W_TOTAL])
        col = sb("col", [P, C_TOTAL])
        rows = sb("rows", [P, R_TOTAL])
        ebias = sb("ebias", [NE, D])
        ident = sb("ident", [P, P])
        identb = sb("identb", [P, P], BF16)
        tri = sb("tri", [P, P])
        head_of = sb("head_of", [P, 8, 16])
        own = sb("own", [P, 16])
        first = sb("first", [P, NE, NE])
        maskq8 = sb("maskq8", [P, TQ, SK], U8)
        maskk8 = sb("maskk8", [P, TK, S], U8)
        maskq_add = sb("maskq_add", [P, TQ, SK], BF16)
        maskk_add = sb("maskk_add", [P, TK, S], BF16)
        winq_add = sb("winq_add", [P, 3, P], BF16)
        wink_add = sb("wink_add", [P, 2, P], BF16)
        constant = sb("constant", [P, 4, TQ])
        keep = sb("keep", [P, 1])
        absum = sb("absum", [P, 2])
        alpha = sb("alpha", [P, 2])
        wtmp = sb("wtmp", [P, 2, FF])
        ones_col = sb("ones_col", [P, P])
        own_max = sb("own_max", [P, 8])
        own_max16 = sb("own_max16", [P, 8])
        X_in = [sb(f"X_in{s}", [P, TQ, D]) for s in range(2)]
        X = [sb(f"X{s}", [P, TQ, D]) for s in range(2)]
        qn = [sb(f"qn{s}", [P, TQ, D]) for s in range(2)]
        QS = [sb(f"QS{s}", [P, 8, S], BF16) for s in range(2)]
        KS8 = [sb(f"KS8{s}", [P, 8, SK], BF16) for s in range(2)]
        KS16 = [sb(f"KS16{s}", [P, 8, SK], BF16) for s in range(2)]
        V8 = [sb(f"V8{s}", [P, TK, 16, VW]) for s in range(2)]
        V16 = [sb(f"V16{s}", [P, TK, 8, VW]) for s in range(2)]
        OT = [sb(f"OT{s}", [P, 4, S]) for s in range(2)]
        KV = [sb(f"KV{s}", [P, 16, VW]) for s in range(2)]
        xs = [sb(f"xs{s}", [P, S + SK]) for s in range(2)]
        cT = [sb(f"cT{s}", [P, SK]) for s in range(2)]
        mx = [sb(f"mx{s}", [P, TQ, 16]) for s in range(2)]
        nmr = [sb(f"nmr{s}", [P, TQ, 16]) for s in range(2)]
        nm = [sb(f"nm{s}", [P, TQ, 16, PARTS], BF16) for s in range(2)]
        mrow = [sb(f"mrow{s}", [12, 4, S], BF16) for s in range(2)]
        stats = [sb(f"stats{s}", [P, TQ, 6]) for s in range(2)]
        mv = [sb(f"mv{s}", [P, TQ, 2]) for s in range(2)]
        var_eps = [sb(f"var_eps{s}", [P, TQ]) for s in range(2)]
        rstd = [sb(f"rstd{s}", [P, TQ]) for s in range(2)]
        hn = [sb(f"hn{s}", [P, TQ, D]) for s in range(2)]
        hT = [sb(f"hT{s}", [P, S]) for s in range(2)]
        es = sb("es", [P, 2 * S])
        rs = sb("rs", [P, 2 * S])
        parts = [sb(f"parts{s}", [P, NPROD, S + SK], BF16) for s in range(2)]
        rest = sb("rest", [P, S + SK])
        kTM = sb("kTM", [P, P])
        rden = sb("rden", [P, TQ * 16])
        An = [sb(f"An{s}", [P, TQ, D]) for s in range(2)]
        AT = [sb(f"AT{s}", [P, S]) for s in range(2)]
        gl = sb("gl", [P, TQ, NE])
        gm = sb("gm", [P, TQ])
        gp = sb("gp", [P, TQ, NE])
        gsum = sb("gsum", [P, TQ])
        grec = sb("grec", [P, TQ])
        cmp_gt = sb("cmp_gt", [P, TQ * NE, NE])
        cmp_eq = sb("cmp_eq", [P, TQ * NE, NE])
        rank = sb("rank", [P, TQ, NE])
        gate = sb("gate", [P, TQ, NE])
        gateT = sb("gateT", [NE, S])
        acc = sb("acc", [P, TQ, D])
        f1 = sb("f1", [P, FC, S])
        sq = sb("sq", [P, FC, S])
        ssum = sb("ssum", [P, TQ])
        rms = sb("rms", [P, TQ])
        irms = sb("irms", [P, TQ])
        junk = sb("junk", [P, 2, SK], BF16)
        probs = sb("probs", [P, PROBS, FF])
        bounce = [nc.dram_tensor(f"bounce{s}", (NPROD, P, S + SK), BF16, kind="Internal").ap() for s in range(2)]

        mb = psum("mb", [P, 2, 512])
        eb = psum("eb", [P, 2, 512])
        ob = psum("ob", [P, 2, 512])
        side = psum("side", [P, 2, 512])

        w_in = [sem(f"w_in{i}") for i in range(len(W_LOADS) - 1)]
        const_in = sem("const_in")
        pool_const, dve_const, pe_const, act_const = sem("pool_const"), sem("dve_const"), sem("pe_const"), sem("act_const")
        dve_step, pool_step = sem("dve_step"), sem("pool_step")
        x_in, ctx_in, x_out = pair("x_in"), pair("ctx_in"), pair("x_out")
        ln_stats, ln_rstd, ln_rows, ln_turned, hT_ready = (pair(n) for n in ("ln_stats", "ln_rstd", "ln_rows", "ln_turned", "hT_ready"))
        proj_done, exp_in, xs_act, xs_ready, v_ready, split_done = (pair(n) for n in ("proj_done", "exp_in", "xs_act", "xs_ready", "v_ready", "split_done"))
        bounce_in, stack_in = pair("bounce_in"), pair("stack_in")
        mrow_in = [[sem(f"mrow_in_{s}_{g}") for g in range(max(GROUPS))] for s in range(2)]
        k_turned, kTM_ready, kv_done, kv_ready = (pair(n) for n in ("k_turned", "kTM_ready", "kv_done", "kv_ready"))
        first_part, spread = pair("first_part"), pair("spread")
        nm_ready, qk_raw = pair("nm_ready"), pair("qk_raw")
        max_scores, max_used = sem("max_scores"), sem("max_used")
        exp_scores, probs_ready, av_done = sem("exp_scores"), sem("probs_ready"), sem("av_done")
        ks16_made = sem("ks16_made")
        out_kept = sem("out_kept")
        o_turned, an_ready, an_turned, at_ready, o_proj = (pair(n) for n in ("o_turned", "an_ready", "an_turned", "at_ready", "o_proj"))
        x_updated = pair("x_updated")
        gate_done, gate_ready, gateT_done, gateT_ready, experts_done, experts_used, moe_bias = (
            pair(n) for n in ("gate_done", "gate_ready", "gateT_done", "gateT_ready", "experts_done", "experts_used", "moe_bias"))
        gexp_in, gexp_out = pair("gexp_in"), pair("gexp_out")
        ffn_h, ffn_act, ffn_y = pair("ffn_h"), pair("ffn_act"), pair("ffn_y")
        rms_sum, rms_root = pair("rms_sum"), pair("rms_root")
        sq_ready, sq_sum = pair("sq_ready"), pair("sq_sum")

        def w(name, lo=0, n=None):
            a, b = W_COLS[name]
            return W[:, a + lo:(a + lo + n) if n else b]

        def row(name):
            return rows[:, R_COLS[name][0]:R_COLS[name][1]]

        def c(name, i=0):
            return col[:, C_COLS[name] + i:C_COLS[name] + i + 1]

        def stack_rows(p, h, extra=0):
            if p == 3:
                return slice(0, NPROD * 16 + extra), h
            half = h % 4 // 2
            return slice(64 * half, 64 * half + NPROD * 8 + extra), h // 4 * 2 + h % 2

        KS = (KS8, KS8, KS8, KS16)
        V = (V8, V8, V8, V16)
        end_side = (side, mb)
        PAIRS = B // 2
        LAST = LOOPS = PAIRS - 1
        counts = dict(chain_counts)

        def wait_alone(eng):
            eng.nop(nofuse=True)

        class Chain:

            def __init__(self, name, eng, sem_):
                self.name, self.eng, self.sem = name, eng, sem_
                self.n, self.before, self.it = 0, 0, None

            def enter(self, it):
                self.before, self.n, self.it = self.n, 0, it
                self.total = counts.get(self.name, 1)

            def leave(self):
                chain_counts[self.name] = self.n
                self.n += self.before + (LOOPS - 1) * self.n
                self.it = None

            def done(self, ins):
                self.n += 1
                ins.then_inc(self.sem, 1)

            def wait(self):
                if self.it is None:
                    self.eng.wait_ge(self.sem, self.n)
                else:
                    self.eng.wait_ge(self.sem, self.it * self.total + (self.before + self.n))

            def link(self, ins, plain=False):
                self.done(ins)
                self.wait()
                if plain:
                    wait_alone(self.eng)

        def lane_of(items, it, start, core, chain_of, before_loop):
            at = start
            for name, *key in items:
                if name == "pause":
                    at += key[0]
                    continue
                now = it + 1 if name.startswith("next") else it
                name = name.removeprefix("next ")
                if name == "core":
                    p, s, groups = key
                    blocks, n_max = core_blocks(p, groups)
                    took = CORE_TIME[p] * (groups[1] - groups[0]) / GROUPS[p]
                    steps = len(blocks)
                    body = core(s, p, groups, blocks, n_max, now, *((0, 0, 0) if before_loop else bases(it, p, s, groups)))
                else:
                    took, steps = CHAIN_TIME[name], TICKS[name]
                    body = chain_of(name, key[0], now)
                for n in body:
                    yield at + n * took / steps
                at += took

        def run_steps(steps, it, core, chain_of):
            for lanes in steps:
                lanes = [[i for i in lane if it is not LAST or not i[0].startswith("next")] for lane in lanes]
                weave([lane_of(items, it, CORE_LATE if len(lanes) > 1 and items and items[0][0] == "core" else 0,
                               core, chain_of, steps is FIRST_STEPS) for items in lanes])

        def bases(it, p, s, groups):
            key = p, s, groups
            return (it * MAX_TOTAL + (MAX_FIRST + MAX_START[key]), it * EXP_TOTAL + (EXP_FIRST + EXP_START[key]),
                    it * OUT_TOTAL + (OUT_FIRST + OUT_START[key]))

        def outs_kept(it, p, s):
            if (p, s) == (0, 0):
                return it * OUT_TOTAL + (GROUPS[0] + 2)
            start = [v for k, v in OUT_START.items() if k[:2] == (p, s)][-1]
            return it * OUT_TOTAL + (OUT_FIRST + start + GROUPS[p] + 2)

        def program(eng, chain, core, chain_of):
            run_steps(FIRST_STEPS, 0, core, chain_of)
            with eng.Fori(0, LOOPS) as it:
                if chain:
                    chain.enter(it)
                run_steps(STEPS, it, core, chain_of)
            if chain:
                chain.leave()
            run_steps(STEPS, LAST, core, chain_of)

        block = ctx.enter_context(nc.Block())

        NORMS = 8
        TURNED = 6
        TURN_OF = {0: 0, 1: 1, 2: 2, 3: 3, 4: 4, 5: 5, 7: 6}
        NT = len(TURN_OF)

        @block.sync
        def _(sp):
            sp.dma_start(col[:], columns).then_inc(const_in, 16)
            sp.dma_start(rows[:], rows_in.to_broadcast([P, R_TOTAL])).then_inc(const_in, 16)
            sp.dma_start(W[:, W_LOADS[0]:W_LOADS[1]], weights[:, W_LOADS[0]:W_LOADS[1]]).then_inc(w_in[0], 16)
            sp.dma_start(maskq8[:], maskq.rearrange("(t p) k -> p t k", p=P)).then_inc(const_in, 16)
            sp.dma_start(maskk8[:], maskk.rearrange("(t p) q -> p t q", p=P)).then_inc(const_in, 16)
            sp.dma_start(ebias[:], experts_bias).then_inc(const_in, 16)
            for i in range(1, len(W_LOADS) - 1):
                sp.dma_start(W[:, W_LOADS[i]:W_LOADS[i + 1]], weights[:, W_LOADS[i]:W_LOADS[i + 1]]).then_inc(w_in[i], 16)

            def load(s, it):
                if not isinstance(it, int):
                    sp.wait_ge(x_updated[s], it * 5 - 4)
                    wait_alone(sp)
                    sp.wait_ge(proj_done[s], it * 8)
                sp.dma_start(X_in[s][:], x[bass.ds(it * 2 + s, 1)].rearrange("o (t p) d -> p (o t) d", p=P)).then_inc(x_in[s], 16)
                sp.dma_start(cT[s][:], ctxT[bass.ds(it * 2 + s, 1)].rearrange("o p t -> p (o t)")).then_inc(ctx_in[s], 16)

            def stack(s, p, it):
                width = S + KEYS[p]
                sp.wait_ge(split_done[s], it * 4 + (p + 1))
                sp.wait_ge(spread[s], it * 4 + (p + 1))
                sp.dma_start(bounce[s].rearrange("c p t -> p c t")[:, :, 0:width], parts[s][:, :, 0:width]).then_inc(bounce_in[s], 16)
                sp.wait_ge(bounce_in[s], it * 64 + 16 * (p + 1))
                back = bounce[s].rearrange("c (d h) t -> (c d) h t", h=HEADS[p])
                halves = 1 if p == 3 else 2
                if p == 3:
                    sp.wait_ge(ks16_made, 2)
                for r in range(halves):
                    to = slice(64 * r, 64 * r + NPROD * HD[p])
                    sp.dma_start(QS[s][to], back[:, r::halves, 0:S]).then_inc(stack_in[s], 16)
                    sp.dma_start(KS[p][s][to, :, 0:KEYS[p]], back[:, r::halves, S:width]).then_inc(stack_in[s], 16)

            def core(s, p, groups, blocks, n_max, it, max_base, exp_base, out_base):
                for b, (kind, g, *_) in enumerate(blocks):
                    yield b
                    n_max += kind != "exp"
                    if kind != "turn":
                        continue
                    sp.wait_ge(max_used, max_base + (n_max + 2))
                    for r in range(1 if p == 3 else 2):
                        at, n_slots = (NPROD * 16, 4) if p == 3 else (64 * r + NPROD * 8, 2)
                        sp.dma_start(QS[s][at:at + MAX_ROWS, n_slots * g:n_slots * (g + 1), :],
                                     mrow[s][:, g, :].unsqueeze(1).to_broadcast([MAX_ROWS, n_slots, S])).then_inc(mrow_in[s][g], 16)

            def chain_of(name, s, it):
                if name == "load":
                    yield 0
                    load(s, it)
                elif name == "end":
                    yield 35
                    sp.wait_ge(x_updated[s], it * 5 + 5)
                    sp.dma_start(out[bass.ds(it * 2 + s, 1)].rearrange("o (t p) d -> p (o t) d", p=P), X[s][:]).then_inc(x_out[s], 16)
                else:
                    yield TICKS[name] - 3
                    stack(s, int(name[2:]), it)

            program(sp, None, core, chain_of)
            for s in range(2):
                sp.wait_ge(x_out[s], PAIRS * 16 + 16)

        @block.gpsimd
        def _(pool):
            chain = Chain("pool", pool, pool_step)

            def select(out_, op, fill, pattern, mult):
                chain.link(nc.gpsimd.affine_select(out=out_, in_=out_, compare_op=op, fill=fill, base=0,
                                                   pattern=pattern, channel_multiplier=mult))

            def select_box(out_, pattern, base):
                chain.link(nc.gpsimd.affine_select(out=out_, in_=out_, compare_op=ALU.is_ge, fill=0.0, base=base,
                                                   pattern=pattern, channel_multiplier=1))
                chain.link(nc.gpsimd.affine_select(out=out_, in_=out_, compare_op=ALU.is_gt, fill=0.0, base=PARTS - base,
                                                   pattern=[[-a_, n_] for a_, n_ in pattern], channel_multiplier=-1))

            for t, v in ((ident, 0.0), (identb, 0.0), (tri, 1.0), (head_of, 0.0), (first, 1.0),
                         (winq_add, 0.0), (wink_add, 0.0), (ones_col, 1.0), (own_max, 1.0), (own_max16, 1.0)):
                chain.done(nc.gpsimd.memset(t[:], v))
            for i, v in enumerate((-0.5, 0.5, -1.0, RMS_EPS)):
                chain.link(nc.gpsimd.memset(constant[:, i, :], v))
            select(ident[:], ALU.not_equal, 1.0, [[-1, P]], 1)
            select(identb[:], ALU.not_equal, 1.0, [[-1, P]], 1)
            select(tri[:], ALU.is_ge, 0.0, [[1, P]], -1)
            select(head_of[:].rearrange("p a (g r j) -> p a g r j", g=4, r=2), ALU.not_equal, 1.0,
                   [[-16, 8], [-4, 4], [-1, 2], [-2, 2]], 1)
            select(first[:], ALU.is_gt, 0.0, [[1, NE], [-1, NE]], 0)
            for i, sign in ((0, -1), (1, 1), (2, -1)):
                select(winq_add[:, i, :], ALU.is_ge, NEG_MAX, [[sign, P]], -sign)
            for i, sign in ((0, 1), (1, -1)):
                select(wink_add[:, i, :], ALU.is_ge, NEG_MAX, [[sign, P]], -sign)
            for r in range(2):
                select_box(own_max[64 * r:64 * r + 64].rearrange("p (g j) -> p g j", j=2), [[0, 4], [-PARTS, 2]],
                           -(NPROD * 8 + 2 * PARTS * r))
            select_box(own_max16[:].rearrange("p (g j) -> p g j", j=4), [[0, 2], [-PARTS, 4]], -NPROD * 16)
            for s in range(2):
                nc.gpsimd.memset(X[s][:, 0, 0:1], 0.0).then_inc(x_out[s], 16)
            nc.gpsimd.memset(ssum[:], 0.0).then_inc(pool_const, 2)

            def power(out_, in_, i):
                return nc.gpsimd.tensor_tensor(out_, in_, constant[:, i, :], ALU.pow)

            def root(s, it, k):
                pool.wait_ge(ln_stats[s], it * NORMS + (k + 1))
                power(rstd[s][:], var_eps[s][:], 0).then_inc(ln_rstd[s], 1)

            def root_and_rms(s, it, k):
                pool.wait_ge(ln_stats[s], it * NORMS + (k + 1))
                power(rstd[s][:], var_eps[s][:], 0)
                chain.link(power(rms[:], mv[s][:, :, 1], 1))
                chain.link(nc.gpsimd.tensor_tensor(rms[:], rms[:], rstd[s][:], ALU.mult))
                chain.link(nc.gpsimd.tensor_tensor(rms[:], rms[:], constant[:, 3, :], ALU.add))
                chain.link(power(rms[:], rms[:], 2))
                nc.gpsimd.tensor_tensor(rstd[s][:], rms[:], rstd[s][:], ALU.mult).then_inc(ln_rstd[s], 1)

            def rms_of(s, it, k):
                pool.wait_ge(rms_sum[s], it + 1)
                chain.link(power(rms[:], ssum[:], 1))
                chain.link(nc.gpsimd.tensor_tensor(rms[:], rms[:], constant[:, 3, :], ALU.add))
                power(irms[:], rms[:], 2).then_inc(rms_root[s], 1)

            def core(s, p, groups, blocks, n_max, it, max_base, exp_base, out_base):
                yield from range(len(blocks))

            def chain_of(name, s, it):
                for hop, f, k in {"load": (), "to0": ((1, root, 0),), "to1": ((7, root, 1),), "to2": ((7, root, 2), (27, root, 3)),
                                  "to3": ((7, root, 4),),
                                  "end": ((6, root, 5), (14, root, 6), (17, root_and_rms, 7), (32, rms_of, 0))}[name]:
                    yield hop
                    f(s, it, k)

            program(pool, chain, core, chain_of)

        @block.tensor
        def _(pe):
            pe.wait_ge(pool_const, 2)
            pe.wait_ge(act_const, 2)
            nc.tensor.matmul(side[:, 0, 0:2], ones_col[:], absum[:], start=True, stop=True).then_inc(pe_const, 1)
            for q in w_in:
                pe.wait_ge(q, 16)
            pe.wait_ge(dve_const, 1)

            def turn(s, it, k, src):
                pe.wait_ge(ln_rows[s], it * NT + (TURN_OF[k] + 1))
                for t in range(TQ):
                    ins = nc.tensor.transpose((end_side[s] if k in (5, 7) else side)[:, 0, t * P:(t + 1) * P], src[:, t, :], ident[:])
                ins.then_inc(ln_turned[s], 1)

            def project(s, it, p):
                pe.wait_ge(hT_ready[s], it * NT + (TURN_OF[(0, 1, 3, 4)[p]] + 1))
                nc.tensor.matmul(side[:, 0, 0:S], w(f"q{p}"), hT[s][:], start=True, stop=True)
                if KEYS[p] == SK:
                    pe.wait_ge(ctx_in[s], it * 16 + 16)
                    ins = nc.tensor.matmul(side[:, 1, :], w(f"k{p}"), cT[s][:], start=True, stop=True)
                else:
                    ins = nc.tensor.matmul(side[:, 0, S:2 * S], w(f"k{p}"), hT[s][:], start=True, stop=True)
                ins.then_inc(proj_done[s], 1)

            def project_v(s, it, p):
                if KEYS[p] == SK:
                    pe.wait_ge(xs_act[s], it * 4 + (p + 1))
                    src, vb = cT[s], side[:, 0, :]
                else:
                    src, vb = hT[s], side[:, 1, :]
                for t in range(KEYS[p] // P):
                    ins = nc.tensor.matmul(vb[:, t * D:(t + 1) * D], src[:, t * P:(t + 1) * P], w(f"v{p}"), start=True, stop=True)
                ins.then_inc(proj_done[s], 1)

            def core(s, p, groups, blocks, n_max, it, max_base, exp_base, out_base):
                ks, v = KS[p][s], V[p][s]
                n1, n2 = MAX_UNITS[p] + 1, EXP_UNITS[p]
                at_zero = isinstance(exp_base, int) and exp_base == 0
                pending = []

                def av(g, i):
                    u = g * n2 + i
                    pe.wait_ge(probs_ready, exp_base + (u + 1))
                    if i == 0:
                        pe.wait_ge(out_kept, out_base + (g + 1))
                    pr = probs[:, u % PROBS, :]
                    bank = ob[:, g % 2, :]
                    if p == 0:
                        for t in range(TQ):
                            for j in (2 * i, 2 * i + 1):
                                at = ((j % 2) * TQ + t) * P
                                nc.tensor.matmul(bank[32 * j:32 * j + 32, t * P:(t + 1) * P], v[:, t, 4 * g + j, :], pr[:, at:at + P],
                                                 start=True, stop=(t == 0), skip_group_check=True)
                        for j in (2 * i, 2 * i + 1):
                            ins = nc.tensor.matmul(bank[32 * j:32 * j + 32, P:2 * P], KV[s][:, 4 * g + j, :], xs[s][:, P:2 * P],
                                                   start=False, stop=True, skip_group_check=True)
                    elif p == 2:
                        kt = i // 2
                        n = (S, P)[kt]
                        for j in (2 * (i % 2), 2 * (i % 2) + 1):
                            ins = nc.tensor.matmul(bank[32 * j:32 * j + 32, S - n:S], v[:, kt, 4 * g + j, :], pr[:, (j % 2) * n:(j % 2 + 1) * n],
                                                   start=(kt == 0), stop=(kt == 1), skip_group_check=True)
                    else:
                        kt = i // 2
                        for j in (2 * (i % 2), 2 * (i % 2) + 1):
                            ins = nc.tensor.matmul(bank[32 * j:32 * j + 32, 0:S], v[:, kt, 4 * g + j, :], pr[:, (j % 2) * S:(j % 2 + 1) * S],
                                                   start=(kt == 0), stop=(kt == TK - 1))
                    ins.then_inc(av_done, 1)

                for b, blk in enumerate(blocks):
                    yield b
                    if b == 0 and groups[0] == 0:
                        pe.wait_ge(stack_in[s], it * STACK_TOTAL + STACK_UPTO[p])
                        pe.wait_ge(v_ready[s], it * 4 + (p + 1))
                        if p == 0:
                            pe.wait_ge(kv_ready[s], it + 1)
                    if blk[0] == "max":
                        _, g, i = blk
                        pe.wait_ge(max_used, max_base + (n_max + 1))
                        bank = mb[:, n_max % 2, :]
                        if p == 2:
                            r, slot = stack_rows(p, 4 * g + i)
                            nc.tensor.matmul(bank[:, 0:P], QS[s][r, slot, 0:P], ks[r, slot, 0:P], start=True, stop=True)
                            ins = nc.tensor.matmul(bank[:, P:3 * P], QS[s][r, slot, P:2 * P], ks[r, slot, 0:S], start=True, stop=True)
                        else:
                            r, slot = stack_rows(p, 4 * g + i // 2)
                            t = i % 2
                            ins = nc.tensor.matmul(bank, QS[s][r, slot, t * P:(t + 1) * P], ks[r, slot, :], start=True, stop=True)
                        ins.then_inc(max_scores, 1)
                        n_max += 1
                    elif blk[0] == "turn":
                        _, g = blk
                        pe.wait_ge(nm_ready[s], it * GRP_TOTAL + (GRP_START[p] + g + 1))
                        pe.wait_ge(max_used, max_base + (n_max + 1))
                        dst = mb[:, n_max % 2, :].bitcast(BF16)
                        for t in range(TQ):
                            ins = nc.tensor.transpose(dst[0:MAX_ROWS, t * P:(t + 1) * P],
                                                      nm[s][:, t, 4 * g:4 * g + 4, :].rearrange("p h c -> p (h c)"), identb[:])
                        ins.then_inc(max_scores, 1)
                        n_max += 1
                    else:
                        _, g, i = blk
                        u = g * n2 + i
                        if n1 > 1 and i == 0:
                            pe.wait_ge(mrow_in[s][g], it * MROW_TOTAL[g] + MROW_UPTO[p][g])
                        if not at_zero or u >= 2:
                            pe.wait_ge(probs_ready, exp_base + (u - 1))
                        bank = eb[:, u % 2, :]
                        if p == 0:
                            for j in (2 * i, 2 * i + 1):
                                r, slot = stack_rows(p, 4 * g + j)
                                for t in range(TQ):
                                    at = ((j % 2) * TQ + t) * P
                                    ins = nc.tensor.matmul(bank[:, at:at + P], ks[r, slot, t * P:(t + 1) * P], QS[s][r, slot, t * P:(t + 1) * P],
                                                           start=True, stop=True)
                        elif p == 2:
                            kt = i // 2
                            n = (S, P)[kt]
                            part = bank[:, 0:2 * n]
                            nc.tensor.matmul(part.rearrange("p (j q) -> p j q", j=2), identb[:],
                                             wink_add[:].rearrange("p a q -> p (a q)")[:, 0:n].unsqueeze(1).to_broadcast([P, 2, n]),
                                             start=True, stop=False, skip_group_check=True)
                            for j in (2 * (i % 2), 2 * (i % 2) + 1):
                                r, slot = stack_rows(p, 4 * g + j, MAX_ROWS)
                                ins = nc.tensor.matmul(part[:, (j % 2) * n:(j % 2 + 1) * n], ks[r, slot, kt * P:(kt + 1) * P], QS[s][r, slot, S - n:S],
                                                       start=False, stop=True, skip_group_check=True)
                        else:
                            kt = i // 2
                            if p == 1:
                                nc.tensor.matmul(bank.rearrange("p (j q) -> p j q", j=2), identb[:],
                                                 maskk_add[:, kt:kt + 1, :].to_broadcast([P, 2, S]), start=True, stop=False, skip_group_check=True)
                            for j in (2 * (i % 2), 2 * (i % 2) + 1):
                                r, slot = stack_rows(p, 4 * g + j, MAX_ROWS)
                                ins = nc.tensor.matmul(bank[:, (j % 2) * S:(j % 2 + 1) * S], ks[r, slot, kt * P:(kt + 1) * P], QS[s][r, slot, :],
                                                       start=(p == 3), stop=True, skip_group_check=(p == 1))
                        ins.then_inc(exp_scores, 1)
                        pending.append((g, i))
                        if len(pending) == AHEAD:
                            av(*pending.pop(0))
                            av(*pending.pop(0))
                for unit in pending:
                    av(*unit)

            def take(s, it, p, at):
                k = (0, 1, 3, 4)[p]
                yield at + 3
                turn(s, it, k, qn[s] if p == 3 else hn[s])
                yield at + 5
                project(s, it, p)
                yield at + 7
                project_v(s, it, p)

            def finish(s, it, p):
                bank = end_side[s] if p == 3 else side
                yield 0
                pe.wait_ge(out_kept, outs_kept(it, p, s))
                for t in range(TQ):
                    for g in range(GROUPS[p]):
                        ins = nc.tensor.transpose(bank[:, t, g * P:(g + 1) * P], OT[s][:, g, t * P:(t + 1) * P], ident[:])
                ins.then_inc(o_turned[s], 1)
                yield 2
                pe.wait_ge(an_ready[s], it * 4 + (p + 1))
                for t in range(TQ):
                    ins = nc.tensor.transpose(bank[:, 0, t * P:(t + 1) * P], An[s][:, t, :], ident[:])
                ins.then_inc(an_turned[s], 1)
                yield 4
                pe.wait_ge(at_ready[s], it * 4 + (p + 1))
                for t in range(TQ):
                    ins = nc.tensor.matmul(bank[:, 1, t * D:(t + 1) * D], AT[s][:, t * P:(t + 1) * P], w(f"o{p}"), start=True, stop=True)
                ins.then_inc(o_proj[s], 1)

            def experts(s, it):
                yield 9
                turn(s, it, 2, hn[s])
                yield 11
                pe.wait_ge(hT_ready[s], it * NT + (TURN_OF[2] + 1))
                for t in range(TQ):
                    ins = nc.tensor.matmul(side[:, 1, t * NE:(t + 1) * NE], hT[s][:, t * P:(t + 1) * P], w("gate"), start=True, stop=True)
                ins.then_inc(gate_done[s], 1)
                yield 16
                pe.wait_ge(gate_ready[s], it + 1)
                for t in range(TQ):
                    ins = nc.tensor.transpose(side[0:NE, 0, t * P:(t + 1) * P], gate[:, t, :], ident[:])
                ins.then_inc(gateT_done[s], 1)
                yield 18
                pe.wait_ge(gateT_ready[s], it + 1)
                for t in range(TQ):
                    ins = nc.tensor.matmul(side[:, 0, t * D:(t + 1) * D], gateT[:, t * P:(t + 1) * P], ebias[:], start=True, stop=True)
                ins.then_inc(moe_bias[s], 1)
                for i in range(4):
                    t, half_ = i // 2, i % 2
                    if i:
                        yield 18 + 2 * i
                        pe.wait_ge(experts_used[s], it * 5 + i)
                    nc.tensor.matmul(side[:, (i + 1) % 2, :], hT[s][:, t * P:(t + 1) * P], w("experts", half_ * 512, 512),
                                     start=True, stop=True).then_inc(experts_done[s], 1)

            def hidden(s, it, name, k):
                pe.wait_ge(hT_ready[s], it * NT + (TURN_OF[k] + 1))
                for n in range(FC):
                    ins = nc.tensor.matmul(end_side[s][:, 1 - n // 2, (n % 2) * S:(n % 2 + 1) * S], w(name, n * P, P), hT[s][:], start=True, stop=True)
                    if n % 2:
                        ins.then_inc(ffn_h[s], 1)

            def out_of_hidden(s, it, name, n_th):
                pe.wait_ge(ffn_act[s], it * 2 + n_th)
                for t in range(TQ):
                    for n in range(FC):
                        ins = nc.tensor.matmul(end_side[s][:, 0, t * D:(t + 1) * D], f1[:, n, t * P:(t + 1) * P], w(name, n * D, D), start=(n == 0), stop=(n == FC - 1))
                ins.then_inc(ffn_y[s], 1)

            def after_the_chain_before(name, s, it):
                if name == "to0" and s == 0:
                    if not isinstance(it, int):
                        pe.wait_ge(x_updated[0], it * 5)
                elif name == "to0":
                    pe.wait_ge(split_done[0], it * 4 + 2)
                elif name in ("to2", "to3"):
                    pe.wait_ge(split_done[1 - s], it * 4 + (int(name[2:]) + s))
                elif (name, s) == ("end", 0):
                    pe.wait_ge(split_done[1], it * 4 + 4)

            def chain_of(name, s, it):
                if name != "load":
                    yield 0
                    after_the_chain_before(name, s, it)
                if name == "to0":
                    yield from take(s, it, 0, 0)
                    yield 9
                    pe.wait_ge(xs_ready[s], it + 1)
                    nc.tensor.transpose(side[:, 0, 0:P], xs[s][:, S:S + P], ident[:]).then_inc(k_turned[s], 1)
                    yield 12
                    pe.wait_ge(kTM_ready[s], it + 1)
                    pe.wait_ge(v_ready[s], it * 4 + 1)
                    nc.tensor.matmul(side[:, 1, :], kTM[:], V8[s][:, 0, :, :].rearrange("p h e -> p (h e)"), start=True, stop=True).then_inc(kv_done[s], 1)
                elif name == "to1":
                    yield from finish(s, it, 0)
                    yield from take(s, it, 1, 6)
                elif name == "to2":
                    yield from finish(s, it, 1)
                    yield from experts(s, it)
                    yield from take(s, it, 2, 26)
                elif name == "to3":
                    yield from finish(s, it, 2)
                    yield from take(s, it, 3, 6)
                elif name == "end":
                    yield from finish(s, it, 3)
                    yield 8
                    turn(s, it, 5, qn[s])
                    yield 10
                    hidden(s, it, "ffn1", 5)
                    yield 12
                    out_of_hidden(s, it, "ffn2", 1)
                    yield 22
                    turn(s, it, 7, hn[s])
                    yield 24
                    hidden(s, it, "up", 7)
                    yield 26
                    out_of_hidden(s, it, "down", 2)
                    yield 29
                    pe.wait_ge(sq_ready[s], it + 1)
                    for t in range(TQ):
                        for n in range(FC):
                            ins = nc.tensor.matmul(end_side[s][:, 1, t:t + 1], sq[:, n, t * P:(t + 1) * P], ones_col[:, 0:1], start=(n == 0), stop=(n == FC - 1))
                    ins.then_inc(sq_sum[s], 1)
                    if s:
                        yield 36
                        pe.wait_ge(x_updated[s], it * 5 + 5)

            program(pe, None, core, chain_of)

        @block.scalar
        def _(act):
            act.wait_ge(const_in, 5 * 16)
            nc.scalar.activation(keep[:], row("lambda"), ACT.Exp, scale=1.0).then_inc(act_const, 1)
            act.wait_ge(pool_const, 2)
            act.wait_ge(w_in[3], 16)
            for i in range(2):
                ins = nc.scalar.activation(wtmp[:, i, :], w(("up", "down")[i]), ACT.Abs, accum_out=absum[:, i:i + 1])
            ins.then_inc(act_const, 1)
            for s in range(2):
                nc.scalar.copy(KS16[s][:], own_max16[:].unsqueeze(2).to_broadcast([P, 8, SK])).then_inc(ks16_made, 1)
            act.wait_ge(dve_const, 1)

            def turned(s, it, k):
                act.wait_ge(ln_turned[s], it * NT + (TURN_OF[k] + 1))
                nc.scalar.copy(hT[s][:], (end_side[s] if k in (5, 7) else side)[:, 0, 0:S]).then_inc(hT_ready[s], 1)

            def first_parts(s, p):
                n = S + KEYS[p]
                nc.scalar.copy(parts[s][:, 0, 0:n], xs[s][:, 0:n]).then_inc(first_part[s], 1)
                nc.scalar.copy(parts[s][:, 3:6:2, 0:S], xs[s][:, 0:S].unsqueeze(1).to_broadcast([P, 2, S]))
                nc.scalar.copy(parts[s][:, 2:5:2, S:n], xs[s][:, S:n].unsqueeze(1).to_broadcast([P, 2, KEYS[p]])).then_inc(spread[s], 1)

            def take(s, it, p, at):
                yield at + 4
                turned(s, it, (0, 1, 3, 4)[p])
                yield at + 6
                act.wait_ge(proj_done[s], it * 8 + (2 * p + 1))
                if p == 0:
                    nc.scalar.activation(rs[:, 0:S], side[:, 0, 0:S], ACT.Identity, bias=c("q0"))
                    nc.scalar.activation(rs[:, S:2 * S], side[:, 0, S:2 * S], ACT.Identity, bias=c("k0")).then_inc(qk_raw[s], 1)
                    act.wait_ge(qk_raw[s], it + 1)
                    nc.scalar.activation(es[:], rs[:], ACT.Exp).then_inc(xs_act[s], 1)
                    yield at + 10
                    act.wait_ge(k_turned[s], it + 1)
                    nc.scalar.copy(kTM[:], side[:, 0, 0:P]).then_inc(kTM_ready[s], 1)
                    act.wait_ge(xs_ready[s], it + 1)
                    first_parts(s, 0)
                    return
                cq, ck = (c("zero"), c("zero")) if p == 3 else (c(f"q{p}"), c(f"k{p}"))
                kb = side[:, 1, :] if KEYS[p] == SK else side[:, 0, S:2 * S]
                nc.scalar.activation(xs[s][:, 0:S], side[:, 0, 0:S], ACT.Identity, bias=cq)
                nc.scalar.activation(xs[s][:, S:S + KEYS[p]], kb, ACT.Identity, bias=ck).then_inc(xs_act[s], 1)
                act.wait_ge(xs_act[s], it * 4 + (p + 1))
                first_parts(s, p)

            def core(s, p, groups, blocks, n_max, it, max_base, exp_base, out_base):
                n2 = EXP_UNITS[p]
                at_zero = isinstance(exp_base, int) and exp_base == 0

                def keep_outputs(g):
                    act.wait_ge(av_done, exp_base + (g + 1) * n2)
                    nc.scalar.copy(OT[s][:, g, :], ob[:, g % 2, 0:S]).then_inc(out_kept, 1)

                for b, (kind, g, *rest_) in enumerate(blocks):
                    yield b
                    if kind != "exp":
                        continue
                    i, = rest_
                    u = g * n2 + i
                    if p:
                        act.wait_ge(exp_scores, exp_base + (u + 1))
                        if not at_zero or u >= PROBS:
                            act.wait_ge(av_done, exp_base + (u - (PROBS - 1)))
                        n = 2 * P if p == 2 and i >= 2 else FF
                        nc.scalar.activation(probs[:, u % PROBS, 0:n], eb[:, u % 2, 0:n], ACT.Exp, scale=SCALE[p]).then_inc(probs_ready, 1)
                        if g > groups[0] and i == KEEP_AFTER[p]:
                            keep_outputs(g - 1)
                    elif g > 1 and i == n2 - 1:
                        keep_outputs(g - 2)
                if p:
                    keep_outputs(groups[1] - 1)
                else:
                    keep_outputs(GROUPS[p] - 2)
                    keep_outputs(GROUPS[p] - 1)

            def finish(s, it, p):
                yield 3
                act.wait_ge(an_turned[s], it * 4 + (p + 1))
                nc.scalar.copy(AT[s][:], (end_side[s] if p == 3 else side)[:, 0, 0:S]).then_inc(at_ready[s], 1)

            def chain_of(name, s, it):
                if name == "to0":
                    yield from take(s, it, 0, 0)
                elif name == "to1":
                    yield from finish(s, it, 0)
                    yield from take(s, it, 1, 6)
                elif name == "to2":
                    yield from finish(s, it, 1)
                    yield 10
                    turned(s, it, 2)
                    yield 13
                    act.wait_ge(gexp_in[s], it + 1)
                    for t in range(TQ):
                        ins = nc.scalar.activation(gp[:, t, :], gl[:, t, :], ACT.Exp, bias=gm[:, t:t + 1], accum_out=gsum[:, t:t + 1])
                    ins.then_inc(gexp_out[s], 1)
                    yield 17
                    act.wait_ge(gateT_done[s], it + 1)
                    nc.scalar.copy(gateT[:], side[0:NE, 0, 0:S]).then_inc(gateT_ready[s], 1)
                    yield from take(s, it, 2, 26)
                elif name == "to3":
                    yield from finish(s, it, 2)
                    yield from take(s, it, 3, 6)
                elif name == "end":
                    yield from finish(s, it, 3)
                    yield 9
                    turned(s, it, 5)
                    yield 11
                    for n in range(FC):
                        if n % 2 == 0:
                            act.wait_ge(ffn_h[s], it * 4 + (n // 2 + 1))
                        ins = nc.scalar.activation(f1[:, n, :], end_side[s][:, 1 - n // 2, (n % 2) * S:(n % 2 + 1) * S], ACT.Relu, bias=c("ffn1", n))
                    ins.then_inc(ffn_act[s], 1)
                    yield 23
                    turned(s, it, 7)
                    yield 25
                    for n in range(0, FC, 2):
                        act.wait_ge(ffn_h[s], it * 4 + (n // 2 + 3))
                        ins = nc.scalar.activation(f1[:, n:n + 2, :].rearrange("p a t -> p (a t)"), end_side[s][:, 1 - n // 2, :], ACT.Gelu)
                    ins.then_inc(ffn_act[s], 1)
                    yield 27
                    act.wait_ge(ffn_act[s], it * 2 + 2)
                    nc.scalar.activation(sq[:], f1[:], ACT.Square).then_inc(sq_ready[s], 1)

            program(act, None, core, chain_of)

        @block.vector
        def _(dve):
            chain = Chain("dve", dve, dve_step)
            link, done = chain.link, chain.done
            V_ = nc.vector
            for s in range(2):
                link(V_.memset(V8[s][:], 0.0))
                link(V_.memset(V16[s][:], 0.0))
                V_.memset(V8[s][:, :, :, 8:9], 1.0)
                V_.memset(V16[s][:, :, :, 16:17], 1.0)
            dve.wait_ge(pool_const, 2)
            for s in range(2):
                V_.tensor_copy(KS8[s][:], own_max[:].unsqueeze(2).to_broadcast([P, 8, SK]))
            dve.wait_ge(const_in, 5 * 16)
            V_.tensor_scalar(maskq_add[:], maskq8[:], NEG_MAX, None, ALU.mult)
            V_.tensor_scalar(maskk_add[:], maskk8[:], NEG_EXP, None, ALU.mult)
            V_.tensor_reduce(own[:], head_of[:].rearrange("p a h -> p h a"), AX.X, ALU.add)
            dve.wait_ge(act_const, 1)
            link(V_.tensor_scalar(keep[:], keep[:], 1.0, None, ALU.add))
            link(V_.reciprocal(keep[:], keep[:]))
            dve.wait_ge(act_const, 2)
            dve.wait_ge(pe_const, 1)
            link(V_.tensor_scalar(alpha[:], side[:, 0, 0:2], 0.5 / (D * FF), None, ALU.mult))
            for i, n in enumerate(("up", "down")):
                link(V_.tensor_scalar(wtmp[:, i, :], w(n), alpha[:, i:i + 1], None, ALU.is_gt))
                link(V_.tensor_scalar(sq[:, 0:2, :].rearrange("p a t -> p (a t)"), w(n), -1.0, alpha[:, i:i + 1], ALU.mult, ALU.is_gt))
                link(V_.tensor_tensor(wtmp[:, i, :], wtmp[:, i, :], sq[:, 0:2, :].rearrange("p a t -> p (a t)"), ALU.subtract))
                link(V_.tensor_tensor(wtmp[:, i, :], wtmp[:, i, :], w(n), ALU.subtract))
                link(V_.tensor_tensor(w(n), w(n), wtmp[:, i, :], ALU.add))
            V_.memset(junk[:, 0, 2:3], 0.0).then_inc(dve_const, 1)
            for i in range(2):
                V_.memset(junk[:, 0, i:i + 1], 0.0).then_inc(max_used, 1)
                V_.memset(junk[:, 1, i:i + 1], 0.0).then_inc(out_kept, 1)

            def stats_of(s, src):
                for t in range(TQ):
                    ins = V_.bn_stats(stats[s][:, t, :], src[:, t, :])
                link(ins, plain=True)
                for t in range(TQ):
                    ins = V_.bn_aggr(mv[s][:, t, :], stats[s][:, t, :])
                link(ins)
                V_.tensor_scalar(var_eps[s][:], mv[s][:, :, 1], LN_EPS, None, ALU.add).then_inc(ln_stats[s], 1)

            def norm(s, it, k, src, dst, at):
                stats_of(s, src)
                yield at + 2
                dve.wait_ge(ln_rstd[s], it * NORMS + (k + 1))
                for t in range(TQ):
                    ins = V_.tensor_scalar(dst[:, t, :], src[:, t, :], mv[s][:, t, 0:1], rstd[s][:, t:t + 1], ALU.subtract, ALU.mult)
                norm_last.append(ins)

            norm_last = []

            def take(s, it, p, at):
                keys, heads, hd = KEYS[p], HEADS[p], HD[p]
                tk = keys // P
                yield at
                if p == 0:
                    dve.wait_ge(x_in[s], it * 16 + 16)
                elif p != 2:
                    dve.wait_ge(x_updated[s], it * 5 + (1, None, 3)[p - 1])
                yield from norm(s, it, (0, 1, 3, 4)[p], X_in[s] if p == 0 else X[s], qn[s] if p == 3 else hn[s], at)
                norm_last.pop().then_inc(ln_rows[s], 1)
                if p == 0:
                    yield at + 8
                    dve.wait_ge(xs_act[s], it * 4 + 1)
                    link(V_.tensor_scalar(rs[:], rs[:], 0.0, None, ALU.max))
                    V_.scalar_tensor_tensor(xs[s][:, 0:2 * S], es[:], 1.0, rs[:], ALU.min, ALU.add).then_inc(xs_ready[s], 1)
                yield at + (11 if p == 0 else 8)
                dve.wait_ge(proj_done[s], it * 8 + (2 * p + 2))
                vb = side[:, 0 if keys == SK else 1, 0:tk * D].rearrange("p (t h d) -> p (t h) d", t=tk, h=heads)
                dst = V[p][s][:, 0:tk, :, 0:hd].rearrange("p t h d -> p (t h) d")
                if p == 3:
                    V_.tensor_copy(dst, vb).then_inc(v_ready[s], 1)
                else:
                    bias = row(f"v{p}").rearrange("p (h d) -> p h d", h=heads)
                    for t in range(tk):
                        ins = V_.tensor_tensor(dst[:, t * heads:(t + 1) * heads, :], vb[:, t * heads:(t + 1) * heads, :], bias, ALU.add)
                    ins.then_inc(v_ready[s], 1)
                yield at + (13 if p == 0 else 10)
                n = S + keys
                dve.wait_ge(first_part[s], it * 4 + (p + 1))
                link(V_.tensor_tensor(rest[:, 0:n], xs[s][:, 0:n], parts[s][:, 0, 0:n], ALU.subtract))
                link(V_.tensor_copy(parts[s][:, 1, 0:n], rest[:, 0:n]))
                V_.tensor_tensor(parts[s][:, 2, 0:S], rest[:, 0:S], parts[s][:, 1, 0:S], ALU.subtract)
                V_.tensor_tensor(parts[s][:, 3, S:n], rest[:, S:n], parts[s][:, 1, S:n], ALU.subtract)
                V_.tensor_copy(parts[s][:, 4, 0:S], parts[s][:, 1, 0:S])
                V_.tensor_copy(parts[s][:, 5, S:n], parts[s][:, 1, S:n]).then_inc(split_done[s], 1)
                if p == 0:
                    dve.wait_ge(kv_done[s], it + 1)
                    V_.tensor_tensor(KV[s][:], side[:, 1, :].rearrange("p (h e) -> p h e", h=16),
                                     own[:].unsqueeze(2).to_broadcast([P, 16, VW]), ALU.mult).then_inc(kv_ready[s], 1)

            def core(s, p, groups, blocks, n_max, it, max_base, exp_base, out_base):
                n2 = EXP_UNITS[p]
                at_zero = isinstance(exp_base, int) and exp_base == 0
                for b, blk in enumerate(blocks):
                    yield b
                    if p == 0:
                        _, g, i = blk
                        u = g * n2 + i
                        dve.wait_ge(exp_scores, exp_base + (u + 1))
                        if not at_zero or u >= PROBS:
                            dve.wait_ge(av_done, exp_base + (u - (PROBS - 1)))
                        V_.tensor_tensor(probs[:, u % PROBS, :].rearrange("p (j q) -> p j q", j=4), eb[:, u % 2, :].rearrange("p (j q) -> p j q", j=4),
                                         tri[:].unsqueeze(1).to_broadcast([P, 4, P]), ALU.mult).then_inc(probs_ready, 1)
                    elif blk[0] == "max":
                        _, g, i = blk
                        dve.wait_ge(max_scores, max_base + (n_max + 1))
                        wait_alone(dve)
                        bank = mb[:, n_max % 2, :]
                        if p == 1:
                            h, t = 4 * g + i // 2, i % 2
                            ins = V_.tensor_tensor_reduce(junk[:, n_max % 2, :], bank, maskq_add[:, t, :], 1.0, NEG_EXP, ALU.add, ALU.max, mx[s][:, t, h:h + 1])
                        elif p == 2:
                            h = 4 * g + i
                            V_.tensor_tensor_reduce(junk[:, n_max % 2, 0:P], bank[:, 0:P], winq_add[:, 0, :], 1.0, NEG_EXP, ALU.add, ALU.max, mx[s][:, 0, h:h + 1])
                            ins = V_.tensor_tensor_reduce(junk[:, n_max % 2, P:3 * P], bank[:, P:3 * P], winq_add[:, 1:3, :].rearrange("p a k -> p (a k)"), 1.0, NEG_EXP,
                                                          ALU.add, ALU.max, mx[s][:, 1, h:h + 1])
                        else:
                            h, t = 4 * g + i // 2, i % 2
                            ins = V_.tensor_reduce(mx[s][:, t, h:h + 1], bank, AX.X, ALU.max)
                        ins.then_inc(max_used, 1)
                        n_max += 1
                        if i == MAX_UNITS[p] - 1:
                            dve.wait_ge(max_used, max_base + (n_max + 2))
                            m = mx[s][:, :, 4 * g:4 * g + 4]
                            r = nmr[s][:, :, 4 * g:4 * g + 4]
                            n = [nm[s][:, :, 4 * g:4 * g + 4, a] for a in range(PARTS)]
                            V_.tensor_scalar(n[0], m, -1.0, None, ALU.mult)
                            link(V_.tensor_scalar(r, m, -1.0, None, ALU.mult))
                            link(V_.tensor_tensor(r, r, n[0], ALU.subtract))
                            link(V_.tensor_copy(n[1], r))
                            V_.tensor_tensor(n[2], r, n[1], ALU.subtract).then_inc(nm_ready[s], 1)
                    elif blk[0] == "turn":
                        _, g = blk
                        dve.wait_ge(max_scores, max_base + (n_max + 1))
                        V_.tensor_copy(mrow[s][:, g, :], mb[:, n_max % 2, :].bitcast(BF16)[0:MAX_ROWS, 0:S]).then_inc(max_used, 1)
                        n_max += 1

            def finish(s, it, p):
                heads, hd = HEADS[p], HD[p]
                bank = end_side[s] if p == 3 else side
                yield 1
                dve.wait_ge(o_turned[s], it * 4 + (p + 1))
                n = GROUPS[p] * 4
                o = bank[:, :, 0:n * VW].rearrange("p t (h e) -> p t h e", h=n)
                r = rden[:, 0:TQ * n].rearrange("p (t h) -> p t h", t=TQ)
                if p == 0:
                    link(V_.tensor_scalar(r, o[:, :, :, hd], DEN_EPS, None, ALU.add))
                    link(V_.reciprocal(r, r))
                else:
                    link(V_.reciprocal(r, o[:, :, :, hd]))
                if p == 3:
                    link(V_.tensor_scalar(r, r, keep[:], None, ALU.mult))
                for t in range(TQ):
                    ins = V_.tensor_tensor(An[s][:, t, :].rearrange("p (h d) -> p h d", h=heads), o[:, t, :, 0:hd],
                                           r[:, t, :].unsqueeze(2).to_broadcast([P, n, hd]), ALU.mult)
                ins.then_inc(an_ready[s], 1)
                if p < 3:
                    if p == 0:
                        dve.wait_ge(x_out[s], it * 16 + 16)
                    link(V_.tensor_tensor(X[s][:], (X_in if p == 0 else X)[s][:], row(f"o{p}").unsqueeze(1).to_broadcast([P, TQ, D]), ALU.add))
                yield 5
                dve.wait_ge(o_proj[s], it * 4 + (p + 1))
                y = bank[:, 1, 0:S].rearrange("p (t d) -> p t d", t=TQ)
                if p < 3:
                    V_.tensor_tensor(X[s][:], X[s][:], y, ALU.add).then_inc(x_updated[s], 1)
                else:
                    link(V_.tensor_tensor(acc[:], qn[s][:], y, ALU.add))

            def norm_affine(s, it, k, src, centred, g, dst, b, at):
                stats_of(s, src)
                for t in range(TQ):
                    ins = V_.scalar_tensor_tensor(centred[:, t, :], src[:, t, :], mv[s][:, t, 0:1], row(g), ALU.subtract, ALU.mult)
                link(ins)
                yield at + 2
                dve.wait_ge(ln_rstd[s], it * NORMS + (k + 1))
                for t in range(TQ):
                    ins = V_.scalar_tensor_tensor(dst[:, t, :], centred[:, t, :], rstd[s][:, t:t + 1], b(t), ALU.mult, ALU.add)
                norm_last.append(ins)

            def experts(s, it):
                yield 6
                dve.wait_ge(x_updated[s], it * 5 + 2)
                yield from norm(s, it, 2, X[s], hn[s], 6)
                norm_last.pop().then_inc(ln_rows[s], 1)
                yield 12
                dve.wait_ge(gate_done[s], it + 1)
                link(V_.tensor_tensor(gl[:], side[:, 1, 0:TQ * NE].rearrange("p (t e) -> p t e", t=TQ),
                                      row("gate").unsqueeze(1).to_broadcast([P, TQ, NE]), ALU.add))
                V_.tensor_reduce(gm[:], gl[:], AX.X, ALU.max, negate=True).then_inc(gexp_in[s], 1)
                yield 14
                dve.wait_ge(gexp_out[s], it + 1)
                link(V_.reciprocal(grec[:], gsum[:]))
                link(V_.tensor_tensor(gp[:], gp[:], grec[:].unsqueeze(2).to_broadcast([P, TQ, NE]), ALU.mult))
                flat = gp[:].rearrange("p t e -> p (t e)")
                for t in range(TQ):
                    pj = gp[:, t:t + 1, :].to_broadcast([P, NE, NE])
                    pe_ = gp[:, t, :].unsqueeze(2).to_broadcast([P, NE, NE])
                    sl = slice(t * NE, (t + 1) * NE)
                    V_.tensor_tensor(cmp_gt[:, sl, :], pj, pe_, ALU.is_gt)
                    ins = V_.tensor_tensor(cmp_eq[:, sl, :], pj, pe_, ALU.is_equal)
                link(ins)
                eq = cmp_eq[:].rearrange("p (t e) j -> p t e j", t=TQ)
                link(V_.tensor_tensor(eq, eq, first[:].unsqueeze(1).to_broadcast([P, TQ, NE, NE]), ALU.mult))
                link(V_.tensor_tensor(cmp_gt[:], cmp_gt[:], cmp_eq[:], ALU.add))
                link(V_.tensor_reduce(rank[:].rearrange("p t e -> p (t e)"), cmp_gt[:], AX.X, ALU.add))
                link(V_.scalar_tensor_tensor(gate[:].rearrange("p t e -> p (t e)"), rank[:].rearrange("p t e -> p (t e)"), 2.0, flat, ALU.is_lt, ALU.mult))
                link(V_.tensor_reduce(gsum[:], gate[:], AX.X, ALU.add))
                link(V_.reciprocal(grec[:], gsum[:]))
                V_.tensor_tensor(gate[:], gate[:], grec[:].unsqueeze(2).to_broadcast([P, TQ, NE]), ALU.mult).then_inc(gate_ready[s], 1)
                yield 19
                dve.wait_ge(moe_bias[s], it + 1)
                V_.tensor_tensor(acc[:], X[s][:], side[:, 0, 0:S].rearrange("p (t d) -> p t d", t=TQ), ALU.add).then_inc(experts_used[s], 1)
                dve.wait_ge(experts_used[s], it * 5 + 1)
                for i in range(4):
                    t, half_ = i // 2, i % 2
                    if i:
                        yield 19 + 2 * i
                    dve.wait_ge(experts_done[s], it * 4 + (i + 1))
                    for e in range(4):
                        last = half_ == 1 and e == 3
                        ins = V_.scalar_tensor_tensor((X[s] if last else acc)[:, t, :], side[:, (i + 1) % 2, e * D:(e + 1) * D],
                                                      gate[:, t, half_ * 4 + e:half_ * 4 + e + 1], acc[:, t, :], ALU.mult, ALU.add)
                        if e < 3:
                            link(ins)
                    ins.then_inc(experts_used[s], 1)
                    dve.wait_ge(experts_used[s], it * 5 + (i + 2))

            def chain_of(name, s, it):
                if name == "to0":
                    yield from take(s, it, 0, 0)
                elif name == "to1":
                    yield from finish(s, it, 0)
                    yield from take(s, it, 1, 6)
                elif name == "to2":
                    yield from finish(s, it, 1)
                    yield from experts(s, it)
                    yield from take(s, it, 2, 26)
                elif name == "to3":
                    yield from finish(s, it, 2)
                    yield from take(s, it, 3, 6)
                elif name == "end":
                    yield from finish(s, it, 3)
                    yield from norm_affine(s, it, 5, acc, hn[s], "ln1_g", qn[s], lambda t: row("ln1_b"), 5)
                    norm_last.pop().then_inc(ln_rows[s], 1)
                    dve.wait_ge(ln_rows[s], it * NT + (TURN_OF[5] + 1))
                    link(V_.tensor_tensor(acc[:], qn[s][:], row("ffn2").unsqueeze(1).to_broadcast([P, TQ, D]), ALU.add))
                    link(V_.tensor_tensor(X[s][:], X[s][:], row("ln2_b").unsqueeze(1).to_broadcast([P, TQ, D]), ALU.add))
                    yield 13
                    dve.wait_ge(ffn_y[s], it * 2 + 1)
                    link(V_.tensor_tensor(acc[:], acc[:], end_side[s][:, 0, 0:S].rearrange("p (t d) -> p t d", t=TQ), ALU.add))
                    yield from norm_affine(s, it, 6, acc, hn[s], "ln2_g", X[s], lambda t: X[s][:, t, :], 13)
                    norm_last.pop().then_inc(x_updated[s], 1)
                    dve.wait_ge(x_updated[s], it * 5 + 4)
                    yield 16
                    yield from norm(s, it, 7, X[s], hn[s], 16)
                    norm_last.pop().then_inc(ln_rows[s], 1)
                    yield 31
                    dve.wait_ge(sq_sum[s], it + 1)
                    V_.tensor_scalar(ssum[:], end_side[s][:, 1, 0:TQ], 1.0 / FF, None, ALU.mult).then_inc(rms_sum[s], 1)
                    yield 33
                    dve.wait_ge(rms_root[s], it + 1)
                    for t in range(TQ):
                        ins = V_.scalar_tensor_tensor(X[s][:, t, :], end_side[s][:, 0, t * D:(t + 1) * D], irms[:, t:t + 1], X[s][:, t, :], ALU.mult, ALU.add)
                    ins.then_inc(x_updated[s], 1)

            program(dve, chain, core, chain_of)


GRP_START, MROW_UPTO, STACK_UPTO = [], [], []
GRP_TOTAL = STACK_TOTAL = 0
MROW_TOTAL = [0] * max(GROUPS)
for _p in PHASES:
    _halves = 1 if _p == 3 else 2
    GRP_START.append(GRP_TOTAL)
    for _g in range(GROUPS[_p] if MAX_UNITS[_p] else 0):
        GRP_TOTAL += 1
        MROW_TOTAL[_g] += 16 * _halves
    MROW_UPTO.append(list(MROW_TOTAL))
    STACK_TOTAL += 16 * 2 * _halves
    STACK_UPTO.append(STACK_TOTAL)
chain_counts = {}


def in_order(w, heads):
    w = w.reshape(heads, D // heads, -1)
    if heads == 16:
        w = w.reshape(4, 2, 2, D // heads, -1).transpose(0, 2, 1, 3, 4).reshape(heads, D // heads, -1)
    return w.transpose(1, 0, 2).reshape(D, -1)


def kernel(**a):
    import concourse.bacc as bacc
    from concourse.bass_utils import run_bass_kernel_spmd

    a = {k: np.asarray(v) for k, v in a.items()}

    def turned(w, heads):
        return in_order(w, heads).T

    def chunks(w):
        return w.reshape(FC, P, D).transpose(1, 0, 2).reshape(P, FC * D)

    wi, bi = a["L1_attn_w_in"], a["L1_attn_b_in"]
    parts = {
        "q0": turned(a["L0_attn_Wq"], 16), "k0": turned(a["L0_attn_Wk"], 16), "v0": a["L0_attn_Wv"].T, "o0": a["L0_attn_Wo"].T,
        "q1": turned(a["L0_xattn_q_w"], 16), "k1": turned(a["L0_xattn_k_w"], 16), "v1": a["L0_xattn_v_w"].T, "o1": a["L0_xattn_o_w"].T,
        "gate": a["L0_ffn_Wg"], "experts": a["L0_ffn_We"].transpose(2, 0, 1).reshape(D, NE * D),
        "q2": turned(wi[0:D], 16), "k2": turned(wi[D:2 * D], 16), "v2": wi[2 * D:].T, "o2": a["L1_attn_w_out"].T,
        "q3": turned(a["L1_xattn_Wq"].T, 8), "k3": turned(a["L1_xattn_Wk"].T, 8), "v3": a["L1_xattn_Wv"], "o3": a["L1_xattn_Wo"],
        "ffn1": a["L1_xattn_ffn_w1"], "ffn2": chunks(a["L1_xattn_ffn_w2"]),
        "up": a["L1_ffn_w_up"].T, "down": chunks(a["L1_ffn_w_down"].T),
    }
    columns = {
        "q0": in_order(a["L0_attn_bq"], 16), "k0": in_order(a["L0_attn_bk"], 16),
        "q1": in_order(a["L0_xattn_q_b"], 16), "k1": in_order(a["L0_xattn_k_b"], 16),
        "q2": in_order(bi[0:D], 16), "k2": in_order(bi[D:2 * D], 16), "zero": np.zeros((D, 1), np.float32),
        "ffn1": a["L1_xattn_ffn_b1"].reshape(FC, P).T,
    }
    rows = {
        "v0": a["L0_attn_bv"], "o0": a["L0_attn_bo"], "v1": a["L0_xattn_v_b"], "o1": a["L0_xattn_o_b"],
        "v2": bi[2 * D:], "o2": a["L1_attn_b_out"], "ln1_g": a["L1_xattn_ln1_g"], "ln1_b": a["L1_xattn_ln1_b"],
        "ln2_g": a["L1_xattn_ln2_g"], "ln2_b": a["L1_xattn_ln2_b"], "ffn2": a["L1_xattn_ffn_b2"], "gate": a["L0_ffn_bg"],
        "lambda": a["L1_xattn_lambda_param"].reshape(1),
    }
    mask = a["mask_SxS2_bk1"]
    arrays = {
        "x": a["x"],
        "ctxT": a["ctx_1024"].transpose(0, 2, 1),
        "maskq": mask,
        "maskk": mask.T,
        "weights": np.concatenate([parts[n] for n in W_COLS], axis=1),
        "columns": np.concatenate([columns[n] for n in C_COLS], axis=1),
        "rows": np.concatenate([rows[n] for n in R_COLS]).reshape(1, R_TOTAL),
        "experts_bias": a["L0_ffn_be"],
    }
    arrays = {k: np.ascontiguousarray(v) for k, v in arrays.items()}

    def program():
        nc = bacc.Bacc("TRN2", target_bir_lowering=False, num_devices=1)
        args = [nc.dram_tensor(f"{k}_dram", v.shape, mybir.dt.from_np(v.dtype), kind="ExternalInput").ap() for k, v in arrays.items()]
        args.append(nc.dram_tensor("out_dram", (B, S, D), F32, kind="ExternalOutput").ap())
        decoder(nc, *args)
        return nc

    program()
    nc = program()
    r = run_bass_kernel_spmd(nc, [{f"{k}_dram": v for k, v in arrays.items()}], core_ids=[0])
    return r.results[0]["out_dram"]
```
